# Optimizing a Trainium2 kernel written in Bass

```python
import numpy as np
import jax
import jax.numpy as jnp

def _softmax(x, axis=-1):
    return jax.nn.softmax(x, axis=axis)

def _gelu(x):
    return jax.nn.gelu(x, approximate=True)

def _silu(x):
    return jax.nn.silu(x)

def _sigmoid(x):
    return jax.nn.sigmoid(x)

def _layernorm(x, axis=-1, eps=1e-05):
    m = jnp.mean(x, axis=axis, keepdims=True)
    v = jnp.var(x, axis=axis, keepdims=True)
    return (x - m) / jnp.sqrt(v + eps)

def _scatter_add(tgt, idx, src, axis=0):
    return tgt.at[idx].add(src)

def _segment_sum(src, seg, n):
    return jax.ops.segment_sum(src, seg, n)
kernel_name = 'mk_lm_tower_d2_tok_ids256_r4_dab3f9'

def setup_inputs(seed: int=0):
    np.random.seed(seed)
    _w = jnp.asarray

    def _rec_inputs():
        import jax
        import jax.numpy as jnp
        _rk = jax.random.key(seed)
        x = jax.random.randint(jax.random.fold_in(_rk, 1), (4, 1024), 0, 4360, jnp.int32)
        return x
    x = _rec_inputs()

    def _L0_tok_setup():
        import jax, jax.numpy as jnp
        import numpy as np
        VOCAB = 4360
        PROJ = 64
        PAD_IDX = 0
        key = jax.random.key(seed)
        k1, k2 = jax.random.split(key)
        x = jax.random.randint(k1, (64, 512), 0, VOCAB, dtype=jnp.int64)
        W = jax.random.normal(k2, (PROJ, VOCAB), dtype=jnp.float32) * 0.02
        return {'x': x, 'W': W}
    _L0_tok_all = _L0_tok_setup()
    _L0_tok_in = {k: v for k, v in _L0_tok_all.items() if k in ('W',)}
    del _L0_tok_all

    def _L0_attn_setup():
        import jax, jax.numpy as jnp
        import numpy as np
        key = jax.random.key(seed)
        inputs = jax.random.normal(key, (8, 512, 64), dtype=jnp.float32)
        return {'inputs': inputs}
    _L0_attn_all = _L0_attn_setup()
    _L0_attn_in = {k: v for k, v in _L0_attn_all.items() if k in ()}
    del _L0_attn_all

    def _L0_ffn_setup():
        import jax, jax.numpy as jnp
        import numpy as np
        B, T, C = (64, 96, 64)
        NH, NKV = (4, 2)
        HD = C // NH
        NREP = NH // NKV
        NE, TOPK = (8, 2)
        HID = int(8 / 3 * C)
        EPS_RMS = 1e-06

        def _rope_tables(t_len):
            inv_freq = 1.0 / 10000.0 ** (np.arange(0, HD, 2, dtype=np.float32) / HD)
            t = np.arange(t_len, dtype=np.float32)
            freqs = np.outer(t, inv_freq)
            emb = np.concatenate([freqs, freqs], axis=-1)
            return (jnp.asarray(np.cos(emb)), jnp.asarray(np.sin(emb)))

        def _rotate_half(x):
            h = x.shape[-1] // 2
            return jnp.concatenate([-x[..., h:], x[..., :h]], axis=-1)

        def _rmsnorm(v, w):
            return v * jax.lax.rsqrt(jnp.mean(v * v, axis=-1, keepdims=True) + EPS_RMS) * w
        key = jax.random.key(seed)
        ks = jax.random.split(key, 10)
        s = lambda k, shape: jax.random.normal(k, shape, jnp.float32) * 0.02
        return {'x': jax.random.normal(ks[0], (B, T, C), jnp.float32), 'ln1_w': jnp.ones((C,), jnp.float32), 'ln2_w': jnp.ones((C,), jnp.float32), 'wq': s(ks[1], (NH * HD, C)), 'wk': s(ks[2], (NKV * HD, C)), 'wv': s(ks[3], (NKV * HD, C)), 'wo': s(ks[4], (C, C)), 'router_w': s(ks[5], (NE, C)), 'w1': s(ks[6], (NE, HID, C)), 'w2': s(ks[7], (NE, C, HID)), 'w3': s(ks[8], (NE, HID, C))}
    _L0_ffn_all = _L0_ffn_setup()
    _L0_ffn_in = {k: v for k, v in _L0_ffn_all.items() if k in ('ln1_w', 'ln2_w', 'wq', 'wk', 'wv', 'wo', 'router_w', 'w1', 'w2', 'w3')}
    del _L0_ffn_all

    def _L1_attn_setup():
        import jax, jax.numpy as jnp
        import numpy as np
        key = jax.random.key(seed)
        ks = jax.random.split(key, 4)
        B, S, D = (4, 1024, 64)
        x = jax.random.normal(ks[0], (B, S, D), dtype=jnp.float32)
        Wq = jax.random.normal(ks[1], (D, D), dtype=jnp.float32) * 0.02
        Wk = jax.random.normal(ks[2], (D, D), dtype=jnp.float32) * 0.02
        Wv = jax.random.normal(ks[3], (D, D), dtype=jnp.float32) * 0.02
        bq = jnp.zeros((D,), dtype=jnp.float32)
        bk = jnp.zeros((D,), dtype=jnp.float32)
        bv = jnp.zeros((D,), dtype=jnp.float32)
        return {'x': x, 'Wq': Wq, 'bq': bq, 'Wk': Wk, 'bk': bk, 'Wv': Wv, 'bv': bv}
    _L1_attn_all = _L1_attn_setup()
    _L1_attn_in = {k: v for k, v in _L1_attn_all.items() if k in ('Wq', 'bq', 'Wk', 'bk', 'Wv', 'bv')}
    del _L1_attn_all

    def _L1_ffn_setup():
        import jax, jax.numpy as jnp
        import numpy as np
        B, K, D = (128, 16, 64)
        E = 32
        H = int(D * 0.25)
        key = jax.random.key(seed)
        ks = jax.random.split(key, 7)
        d_rs = D ** (-0.5)
        h_rs = H ** (-0.5)
        x = jax.random.normal(ks[0], (B, K, D), dtype=jnp.float32)
        router_w = jax.random.uniform(ks[1], (E, D), jnp.float32, -d_rs, d_rs)
        router_b = jax.random.uniform(ks[2], (E,), jnp.float32, -d_rs, d_rs)
        W1 = jax.random.uniform(ks[3], (E, D, H), jnp.float32, -h_rs, h_rs)
        b1 = jax.random.uniform(ks[4], (E, H), jnp.float32, -h_rs, h_rs)
        W2 = jax.random.uniform(ks[5], (E, H, D), jnp.float32, -d_rs, d_rs)
        b2 = jax.random.uniform(ks[6], (E, D), jnp.float32, -d_rs, d_rs)
        return {'x': x, 'router_w': router_w, 'router_b': router_b, 'W1': W1, 'b1': b1, 'W2': W2, 'b2': b2}
    _L1_ffn_all = _L1_ffn_setup()
    _L1_ffn_in = {k: v for k, v in _L1_ffn_all.items() if k in ('router_w', 'router_b', 'W1', 'b1', 'W2', 'b2')}
    del _L1_ffn_all
    return {'x': x, 'L0_tok_W': _L0_tok_in['W'], 'L0_ffn_ln1_w': _L0_ffn_in['ln1_w'], 'L0_ffn_ln2_w': _L0_ffn_in['ln2_w'], 'L0_ffn_wq': _L0_ffn_in['wq'], 'L0_ffn_wk': _L0_ffn_in['wk'], 'L0_ffn_wv': _L0_ffn_in['wv'], 'L0_ffn_wo': _L0_ffn_in['wo'], 'L0_ffn_router_w': _L0_ffn_in['router_w'], 'L0_ffn_w1': _L0_ffn_in['w1'], 'L0_ffn_w2': _L0_ffn_in['w2'], 'L0_ffn_w3': _L0_ffn_in['w3'], 'L1_attn_Wq': _L1_attn_in['Wq'], 'L1_attn_bq': _L1_attn_in['bq'], 'L1_attn_Wk': _L1_attn_in['Wk'], 'L1_attn_bk': _L1_attn_in['bk'], 'L1_attn_Wv': _L1_attn_in['Wv'], 'L1_attn_bv': _L1_attn_in['bv'], 'L1_ffn_router_w': _L1_ffn_in['router_w'], 'L1_ffn_router_b': _L1_ffn_in['router_b'], 'L1_ffn_W1': _L1_ffn_in['W1'], 'L1_ffn_b1': _L1_ffn_in['b1'], 'L1_ffn_W2': _L1_ffn_in['W2'], 'L1_ffn_b2': _L1_ffn_in['b2']}

def reference(x, L0_tok_W, L0_ffn_ln1_w, L0_ffn_ln2_w, L0_ffn_wq, L0_ffn_wk, L0_ffn_wv, L0_ffn_wo, L0_ffn_router_w, L0_ffn_w1, L0_ffn_w2, L0_ffn_w3, L1_attn_Wq, L1_attn_bq, L1_attn_Wk, L1_attn_bk, L1_attn_Wv, L1_attn_bv, L1_ffn_router_w, L1_ffn_router_b, L1_ffn_W1, L1_ffn_b1, L1_ffn_W2, L1_ffn_b2):
    import jax
    import jax.numpy as jnp

    def _L0_tok_ref(x, W):
        import jax, jax.numpy as jnp
        import numpy as np
        VOCAB = 4360
        PROJ = 64
        PAD_IDX = 0
        out = jnp.take(W.T, x, axis=0)
        mask = (x != PAD_IDX)[..., None]
        return jnp.where(mask, out, jnp.zeros((), dtype=out.dtype))

    def _L0_attn_ref(inputs):
        import jax, jax.numpy as jnp
        import numpy as np
        d_k = jnp.asarray(inputs.shape[-1], dtype=inputs.dtype)
        scores = jnp.einsum('bnd,bmd->bnm', inputs, inputs) / jnp.sqrt(d_k)
        weights = jax.nn.softmax(scores, axis=-1)
        context = jnp.einsum('bnm,bmd->bnd', weights, inputs)
        return context

    def _L0_ffn_ref(x, ln1_w, ln2_w, wq, wk, wv, wo, router_w, w1, w2, w3):
        import jax, jax.numpy as jnp
        import numpy as np
        B, T, C = (64, 96, 64)
        NH, NKV = (4, 2)
        HD = C // NH
        NREP = NH // NKV
        NE, TOPK = (8, 2)
        HID = int(8 / 3 * C)
        EPS_RMS = 1e-06

        def _rope_tables(t_len):
            inv_freq = 1.0 / 10000.0 ** (np.arange(0, HD, 2, dtype=np.float32) / HD)
            t = np.arange(t_len, dtype=np.float32)
            freqs = np.outer(t, inv_freq)
            emb = np.concatenate([freqs, freqs], axis=-1)
            return (jnp.asarray(np.cos(emb)), jnp.asarray(np.sin(emb)))

        def _rotate_half(x):
            h = x.shape[-1] // 2
            return jnp.concatenate([-x[..., h:], x[..., :h]], axis=-1)

        def _rmsnorm(v, w):
            return v * jax.lax.rsqrt(jnp.mean(v * v, axis=-1, keepdims=True) + EPS_RMS) * w
        Bx, Tx, Cx = x.shape
        h = _rmsnorm(x, ln1_w)
        q = (h @ wq.T).reshape(Bx, Tx, NH, HD).transpose(0, 2, 1, 3)
        k = (h @ wk.T).reshape(Bx, Tx, NKV, HD).transpose(0, 2, 1, 3)
        v = (h @ wv.T).reshape(Bx, Tx, NKV, HD).transpose(0, 2, 1, 3)
        cos, sin = _rope_tables(Tx)
        cos, sin = (cos[None, None], sin[None, None])
        q = q * cos + _rotate_half(q) * sin
        k = k * cos + _rotate_half(k) * sin
        k = jnp.repeat(k, NREP, axis=1)
        v = jnp.repeat(v, NREP, axis=1)
        scores = jnp.einsum('bhtd,bhsd->bhts', q, k) / jnp.sqrt(jnp.float32(HD))
        causal = jnp.tril(jnp.ones((Tx, Tx), dtype=bool))
        scores = jnp.where(causal[None, None], scores, jnp.float32(-1e+30))
        att = jax.nn.softmax(scores, axis=-1)
        y = jnp.einsum('bhts,bhsd->bhtd', att, v).transpose(0, 2, 1, 3).reshape(Bx, Tx, Cx)
        x = x + y @ wo.T
        flat = _rmsnorm(x, ln2_w).reshape(-1, Cx)
        probs = jax.nn.softmax(flat @ router_w.T, axis=-1)
        tp, ti = jax.lax.top_k(probs, TOPK)
        tp = tp / (jnp.sum(tp, axis=-1, keepdims=True) + 1e-09)
        weights = jnp.sum(tp[..., None] * jax.nn.one_hot(ti, NE, dtype=flat.dtype), axis=1)
        out = jnp.zeros_like(flat)
        for e in range(NE):
            hh = jax.nn.silu(flat @ w1[e].T) * (flat @ w3[e].T)
            out = out + weights[:, e:e + 1] * (hh @ w2[e].T)
        return x + out.reshape(Bx, Tx, Cx)

    def _L1_attn_ref(x, Wq, bq, Wk, bk, Wv, bv):
        import jax, jax.numpy as jnp
        import numpy as np
        Q = jnp.einsum('bsd,de->bse', x, Wq) + bq
        K = jnp.einsum('bsd,de,->bse'.replace(',->', '->'), x, Wk) + bk
        V = jnp.einsum('bsd,de->bse', x, Wv) + bv
        scale = 1.0 / jnp.sqrt(jnp.asarray(Q.shape[-1], dtype=jnp.float32))
        scores = jnp.einsum('bqd,bkd->bqk', Q, K) * scale
        weights = jax.nn.softmax(scores, axis=-1)
        return jnp.einsum('bqk,bkd->bqd', weights, V)

    def _L1_ffn_ref(x, router_w, router_b, W1, b1, W2, b2):
        import jax, jax.numpy as jnp
        import numpy as np
        B, K, D = (128, 16, 64)
        E = 32
        H = int(D * 0.25)
        xf = x.reshape(-1, D)
        logits = xf @ router_w.T + router_b
        idx = jnp.argmax(logits, axis=-1)
        w1t = jnp.take(W1, idx, axis=0)
        h = jnp.einsum('nd,ndh->nh', xf, w1t) + jnp.take(b1, idx, axis=0)
        h = jax.nn.relu(h)
        w2t = jnp.take(W2, idx, axis=0)
        out = jnp.einsum('nh,nhd->nd', h, w2t) + jnp.take(b2, idx, axis=0)
        out = jax.nn.relu(out)
        return out.reshape(x.shape)
    h = _L0_tok_ref(x, L0_tok_W)
    h = h + _L0_attn_ref(_layernorm(h, axis=-1))
    h = h + _L0_ffn_ref(_layernorm(h, axis=-1), L0_ffn_ln1_w, L0_ffn_ln2_w, L0_ffn_wq, L0_ffn_wk, L0_ffn_wv, L0_ffn_wo, L0_ffn_router_w, L0_ffn_w1, L0_ffn_w2, L0_ffn_w3)
    h = h + _L1_attn_ref(_layernorm(h, axis=-1), L1_attn_Wq, L1_attn_bq, L1_attn_Wk, L1_attn_bk, L1_attn_Wv, L1_attn_bv)
    h = h + _L1_ffn_ref(_layernorm(h, axis=-1), L1_ffn_router_w, L1_ffn_router_b, L1_ffn_W1, L1_ffn_b1, L1_ffn_W2, L1_ffn_b2)
    return h

_drawn_inputs = setup_inputs


def setup_inputs(seed=0):
    import zlib

    import numpy as np

    out = dict(_drawn_inputs(seed))
    spreads = {'L0_ffn_ln1_w': (1.0, 0.6),
     'L0_ffn_ln2_w': (1.0, 0.6),
     'L1_attn_bq': (0.0, 2.0),
     'L1_attn_bk': (0.0, 2.0),
     'L1_attn_bv': (0.0, 0.435)}
    factors = {'L0_ffn_wq': 8.0,
     'L0_ffn_wk': 8.0,
     'L0_ffn_wv': 8.0,
     'L0_ffn_wo': 8.0,
     'L0_ffn_router_w': 8.0,
     'L0_ffn_w1': 8.0,
     'L0_ffn_w2': 8.0,
     'L0_ffn_w3': 8.0,
     'L1_attn_Wq': 8.0,
     'L1_attn_Wk': 8.0,
     'L1_attn_Wv': 6.136,
     'L1_ffn_b1': 19.237,
     'L1_ffn_router_b': 4.13,
     'L1_ffn_b2': 6.578}
    for name, (base, spread) in spreads.items():
        noise = np.random.default_rng([zlib.crc32(name.encode()), seed]).standard_normal(out[name].shape)
        drawn = base * np.exp(spread * noise) if base else spread * noise
        out[name] = jnp.asarray(drawn.astype(out[name].dtype))
    for name, factor in factors.items():
        out[name] = (out[name] * factor).astype(out[name].dtype)
    return out
```

```python
from contextlib import ExitStack

import concourse.bass as bass
import numpy as np
from concourse import mybir

F32 = mybir.dt.float32
F32R = mybir.dt.float32r
BF16 = mybir.dt.bfloat16
I32 = mybir.dt.int32
U32 = mybir.dt.uint32
ALU = mybir.AluOpType
ACT = mybir.ActivationFunctionType
AX = mybir.AxisListType

P = 128
B, L, D = 4, 1024, 64
VOCAB = 4360
T = L // P
HALF = 512
C = L // HALF
TH = T // C
NH, NKV, HD = 4, 2, 16
NE, TOPK, HID = 8, 2, int(8 / 3 * D)
EH = NE * HID
MT = -(-EH // P)
E1, H1 = 32, 16
M1 = E1 * H1 // P
LN_EPS, RMS_EPS = 1e-5, 1e-6
NEG = -1e30

COLS = {}
_at = 0
for _name, _n in (("qk", 96), ("qk_swapped", 96), ("v", 32), ("router", NE), ("w1", EH), ("w3", EH),
                  ("q2", P), ("k2", P), ("v2", D), ("router2", E1), ("w1_2", E1 * H1)):
    COLS[_name] = (_at, _at + _n)
    _at += _n
WCOLS = _at
GROUP1 = (0, COLS["v"][1])
GROUP2 = (COLS["router"][0], COLS["w3"][1])
GROUP3 = (COLS["q2"][0], WCOLS)



def causal_tiles(width_of):
    out = []
    for blk in range(T):
        for c in range(C):
            w = width_of(blk, c)
            if w > 0:
                n = min(NH, HALF // w)
                n = {1: 1, 2: 2, 3: 2, 4: 4}[n]
                out += [(blk, c, w, tuple(range(h, h + n))) for h in range(0, NH, n)]
    return out


MAX_TILES = causal_tiles(lambda blk, c: min(HALF, P * (blk + 1) - HALF * c))
PROB_TILES = causal_tiles(lambda blk, c: min(HALF, HALF * (c + 1) - P * blk))
NMAX, NPROB = len(MAX_TILES), len(PROB_TILES)
NSELF = T * C

NRING = 8
NHID = 4
DVE_FRONT, DVE_BACK = 11, 21


def at(eng, i, per, n):
    if isinstance(i, int):
        return i * per + n
    eng.reg_alu(WAIT_REGISTER[eng.engine], i * per, n, ALU.add)
    return WAIT_REGISTER[eng.engine]


WAIT_REGISTER = {}


def tower(nc, a, out):
    ctx = ExitStack()
    with ctx:
        def sb(name, shape, dt=F32):
            return ctx.enter_context(nc.sbuf_tensor(name, shape, dt))

        def ps(name, shape, dt=F32):
            return ctx.enter_context(nc.psum_tensor(name, shape, dt))

        ident = sb("ident", [P, P])
        ident16 = sb("ident16", [P, P], BF16)
        mask_qk = sb("mask_qk", [P, P], BF16)
        mask_kq = sb("mask_kq", [P, P], BF16)
        cos = sb("cos", [96, L])
        sin = sb("sin", [96, L])
        iota = sb("iota", [P, E1])
        spread = sb("spread", [40, MT * P], F32R)
        block16 = sb("block16", [E1, E1 * H1], BF16)
        lnw = sb("lnw", [P, 2])
        w_s = sb("w_s", [P, WCOLS], F32R)
        wo = sb("wo", [D, D])
        w2 = sb("w2", [P, MT, D])
        w2_2 = sb("w2_2", [P, M1, D])
        b1_2 = sb("b1_2", [P, M1])
        b2_2 = sb("b2_2", [E1, D])
        bq = sb("bq", [P, 1])
        bk = sb("bk", [P, 1])
        bv = sb("bv", [P, D])
        rb = sb("rb", [P, E1])
        minus_half = sb("minus_half", [P, T])

        negm_dram = nc.dram_tensor("negm_rows", (NH * T, P), F32, kind="Internal").ap()
        negm3_dram = nc.dram_tensor("negm3_rows", (T, P), F32, kind="Internal").ap()

        def wait_apart(eng, sem, count):
            eng.wait_ge(signal["filled"], 9)
            eng.wait_ge(sem, count)

        def weight(name, lo=0, n=None):
            c0, c1 = COLS[name]
            return w_s[:, c0 + lo:(c1 if n is None else c0 + lo + n)]

        idx = sb("idx", [P, T], I32)
        emb = sb("emb", [P, T, D])
        keep = sb("keep", [P, T])
        h0 = sb("h0", [P, T, D])
        stats = sb("stats", [P, T, 6])
        mv = sb("mv", [P, T, 2])
        veps = sb("veps", [P, T])
        rstd = sb("rstd", [P, T])
        xd = sb("xd", [P, T, 2, D])
        x1v = sb("x1v", [P, T, D + 1])
        hh = sb("hh", [P, L], F32R)
        ll = sb("ll", [P, L], F32R)
        aa = sb("aa", [P, L], F32R)
        prob = sb("prob", [P, NRING, HALF])
        rsum = sb("rsum", [P, T])
        h1 = sb("h1", [P, T, D])
        x2 = sb("x2", [P, T, D])
        sq = sb("sq", [P, T, D])
        att = sq
        ssum = sb("ssum", [P, T])
        rope_a = sb("rope_a", [96, 2, HALF])
        rope_b = sb("rope_b", [96, 2, HALF])
        qk = rope_a[:].rearrange("p c n -> p (c n)")
        qkh = sb("qkh", [96, L], F32R)
        qkl = sb("qkl", [96, L], F32R)
        qs = sb("qs", [P, NH, L], F32R)
        ks = sb("ks", [P, L], F32R)
        v1 = sb("v1", [P, T, NKV, 32])
        mx = sb("mx", [P, NH, T, C])
        mxt = sb("mxt", [P, NH, T])
        negm = sb("negm", [NH * T, P], F32R)
        ot = sb("ot", [P, L])
        rs4 = sb("rs4", [P, T, NH])
        y = sb("y", [P, T, D])
        yt = rope_b[0:D].rearrange("p c n -> p (c n)")
        x3 = sb("x3", [P, T, D])
        w_f = prob[:].rearrange("p r n -> p (r n)")[:, 0:WCOLS]
        res = sb("res", [P, T, D])
        x3d = sb("x3d", [P, T, 2, D])
        bhh = sb("bhh", [P, L], F32R)
        bll = sb("bll", [P, L], F32R)
        lg = sb("lg", [P, T, NE])
        lmax = sb("lmax", [P, T])
        ex = sb("ex", [P, T, NE])
        esum = sb("esum", [P, T])
        top8 = sb("top8", [P, T, 8])
        topi = sb("topi", [P, T, 8], U32)
        topf = sb("topf", [P, T, 2])
        oh_a = sb("oh_a", [P, T, NE])
        oh_b = sb("oh_b", [P, T, NE])
        wt = sb("wt", [40, L], F32R)
        sa = sb("sa", [P, 2, HALF])
        ub = sb("ub", [P, 2, HALF])
        hid = sb("hid", [P, NHID, HALF])
        spread_f = hid[0:40].rearrange("p r n -> p (r n)")[:, 0:MT * P]
        mt = sb("mt", [P, HALF])
        h2 = sb("h2", [P, T, D])
        bstats = sb("bstats", [P, T, 6])
        bmv = sb("bmv", [P, T, 2])
        bveps = sb("bveps", [P, T])
        brstd = sb("brstd", [P, T])
        bxd = sb("bxd", [P, T, 2, D])
        qh = sb("qh", [P, L], F32R)
        ql = sb("ql", [D + 1, L], F32R)
        ka = sb("ka", [P, L], F32R)
        k2 = sb("k2", [D + 1, L], F32R)
        v2 = sb("v2", [P, T, D + 1])
        bprob = hid
        mx3 = sb("mx3", [P, C, T])
        m3 = sb("m3", [P, T])
        negm3 = sb("negm3", [T, P], F32R)
        brsum = sb("brsum", [P, T])
        batt = sb("batt", [P, T, D])
        h3 = sb("h3", [P, T, D])
        lg5 = sb("lg5", [P, T, E1])
        top8b = sb("top8b", [P, T, 8])
        topib = sb("topib", [P, T, 8], U32)
        topfb = sb("topfb", [P, T])
        others = sb("others", [P, T, E1])
        otherst = sb("otherst", [E1, L], BF16)
        chosent = sa[0:E1].rearrange("p c n -> p (c n)")
        mt2 = mt
        h4 = sb("h4", [P, T, D])

        fw = ps("fw", [P, 2, HALF])
        fo = ps("fo", [P, 2, HALF])
        bw = ps("bw", [P, 2, HALF])
        bo = ps("bo", [P, 2, HALF])

        names = """const_loaded w1_loaded w2_loaded w_scaled w_high w_split w_ready filled v1_zeroed const_cast
            idx_loaded emb_gathered emb_used step_f step_b pool_step
            var1 rstd1 x1_ready x1T hh1 aa1 ll1 aal1 s1 e1 pv1 h1_ready
            var2 rstd2 ssq2 rrms2 x2_ready x2T hh2 ll2 qk_ps rope_used qk_ready qkh_ready qkl_ready
            v_ps v_ready spread_done sm max_used max_ready maxT negm_ready negm_stored negm_placed negm3_stored
            s2 e2 pv2 ot_ready otT y_ready yT yt_ready wo_ps x3_ready ssq3 rrms3 x3_done
            x3T hh3 ll3 lg_ps lmax_ready ex_ready rw_ready rwT wth_ready wt_ready
            moe_a moe_b moe_w silu ub_ready hid_ready w2_step moe_out mt_ready mtT h2_ready
            var4 rstd4 x4_ready x4T hh4 ll4 q_ps qh_ready ql_ready k_ps ka_ready k2_ready kal_ready
            v2_ps v2_ready sm3 max3_used m3_ready m3T negm3_ready negm3_placed
            s3 e3 pv3 h3_ready var5 rstd5 x5_ready x5T hh5 ll5 lg5_ps others_ready othersT
            otherst_ready chosent_ready s5 hid5_ready w5_step out5 mt5_ready mt5T h4_ready h4_free
            """.split()
        signal = {n: ctx.enter_context(nc.semaphore(n)) for n in names}

        def dup(ap):
            return ap.unsqueeze(2).to_broadcast([P, ap.shape[1], D])

        block = ctx.enter_context(nc.Block())

        @block.sync
        def _(sp):
            WAIT_REGISTER[sp.engine] = sp.alloc_register("wait_value")
            early = [(ident, a["ident"]), (lnw, a["lnw"]), (ident16, a["ident16"]), (mask_qk, a["mask_qk"]),
                     (mask_kq, a["mask_kq"]), (cos, a["cos"]), (sin, a["sin"]), (wo, a["wo"]), (iota, a["iota"]),
                     (spread_f, a["spread"]), (block16, a["block16"]), (w2_2, a["w2_2"]), (b1_2, a["b1_2"]),
                     (b2_2, a["b2_2"]), (bq, a["bq"]), (bk, a["bk"])]
            for dst, src in early:
                sp.dma_start(dst[:], src).then_inc(signal["const_loaded"], 16)
            sp.dma_start(bv[:], a["bv"].partition_broadcast(P)).then_inc(signal["const_loaded"], 16)
            sp.dma_start(rb[:], a["rb"].partition_broadcast(P)).then_inc(signal["const_loaded"], 16)
            for half in range(2):
                sp.dma_start(w_f[D * half:D * half + D, :], a["wcat"]).then_inc(signal["w1_loaded"], 16)
            sp.dma_start(w2[:, 0:MT - 1, :], a["w2"][0:(MT - 1) * P].rearrange("(m p) d -> p m d", p=P)) \
                .then_inc(signal["w2_loaded"], 16)
            sp.dma_start(w2[0:EH - (MT - 1) * P, MT - 1, :], a["w2"][(MT - 1) * P:EH]).then_inc(signal["w2_loaded"], 16)

            with sp.Fori(0, B, 1) as i:
                def spread_rows(dst, src):
                    sp.dma_start(dst.bitcast(F32), src.bitcast(F32)).then_inc(signal["spread_done"], 16)

                sp.wait_ge(signal["qkh_ready"], at(sp, i, C, C))
                for r in (0, 2):
                    for h in range(NH):
                        row = 32 * r + HD * (h // 2)
                        spread_rows(qs[row:row + HD, h, :], qkh[HD * h:HD * h + HD, :])
                for r in (0, 1):
                    spread_rows(ks[32 * r:32 * r + 32, :], qkh[64:96, :])
                sp.wait_ge(signal["qkl_ready"], at(sp, i, C, C))
                spread_rows(ks[64:96, :], qkl[64:96, :])
                for h in range(NH):
                    row = 32 + HD * (h // 2)
                    spread_rows(qs[row:row + HD, h, :], qkl[HD * h:HD * h + HD, :])
                sp.wait_ge(signal["negm_ready"], at(sp, i, 1, 1))
                sp.dma_start(negm_dram, negm[:].bitcast(F32)).then_inc(signal["negm_stored"], 16)
                sp.wait_ge(signal["negm_stored"], at(sp, i, 16, 16))
                sp.dma_start(qs[96:97, :, :].bitcast(F32), negm_dram.rearrange("(o h t) n -> o h (t n)", o=1, h=NH)) \
                    .then_inc(signal["negm_placed"], 16)
                sp.wait_ge(signal["negm3_ready"], at(sp, i, 1, 1))
                sp.dma_start(negm3_dram, negm3[:].bitcast(F32)).then_inc(signal["negm3_stored"], 16)
                sp.wait_ge(signal["negm3_stored"], at(sp, i, 16, 16))
                sp.dma_start(ql[D:D + 1, :].bitcast(F32), negm3_dram.rearrange("(o t) n -> o (t n)", o=1)) \
                    .then_inc(signal["negm3_placed"], 16)
                sp.wait_ge(signal["h4_ready"], at(sp, i, 1, 1))
                sp.dma_start(out[bass.ds(i, 1)].rearrange("b (t p) d -> p (b t) d", p=P), h4[:]) \
                    .then_inc(signal["h4_free"], 16)
            sp.wait_ge(signal["h4_free"], at(sp, B, 16, 16))

        @block.gpsimd
        def _(pool):
            WAIT_REGISTER[pool.engine] = pool.alloc_register("wait_value")
            pool.memset(minus_half[:], -0.5).then_inc(signal["filled"], 1)
            pool.memset(x1v[:, :, D:D + 1], 1.0).then_inc(signal["filled"], 1)
            pool.memset(v2[:, :, D:D + 1], 1.0).then_inc(signal["filled"], 1)
            pool.memset(v1[:], 0.0).then_inc(signal["v1_zeroed"], 1)
            pool.wait_ge(signal["v1_zeroed"], 1)
            pool.memset(v1[:, :, :, HD:HD + 1], 1.0).then_inc(signal["filled"], 1)
            pool.memset(mx[:], -3e38).then_inc(signal["filled"], 1)
            pool.memset(wt[:].bitcast(F32), 0.0).then_inc(signal["filled"], 1)
            pool.memset(qs[:].bitcast(F32), 0.0).then_inc(signal["filled"], 1)

            def gather(b):
                pool.dma_start(idx[:], a["x"][bass.ds(b, 1)].rearrange("b p t -> p (b t)")) \
                    .then_inc(signal["idx_loaded"], 16)
                wait_apart(pool, signal["idx_loaded"], at(pool, b, 16, 16))
                for t in range(T):
                    pool.indirect_dma_start(emb[:, t, :], None, a["table"],
                                            bass.IndirectOffsetOnAxis(idx[:, t:t + 1], 0)) \
                        .then_inc(signal["emb_gathered"], 16)

            gather(0)
            with pool.Fori(0, B, 1) as i:
                def power(n, ready, src, scale, eps, tmp, dst, done):
                    wait_apart(pool, ready, at(pool, i, 1, 1))
                    pool.tensor_scalar(tmp[:], src, scale, eps, ALU.mult, ALU.add).then_inc(signal["pool_step"], 1)
                    pool.wait_ge(signal["pool_step"], at(pool, i, 6, n))
                    pool.tensor_tensor(dst[:], tmp[:], minus_half[:], ALU.pow).then_inc(done, 1)

                power(1, signal["var1"], mv[:, :, 1], 1.0, LN_EPS, veps, rstd, signal["rstd1"])
                power(2, signal["var2"], mv[:, :, 1], 1.0, LN_EPS, veps, rstd, signal["rstd2"])
                power(3, signal["ssq2"], ssum[:], 1.0 / D, RMS_EPS, veps, rstd, signal["rrms2"])
                power(4, signal["ssq3"], ssum[:], 1.0 / D, RMS_EPS, veps, rstd, signal["rrms3"])
                gather(i + 1)
                power(5, signal["var4"], bmv[:, :, 1], 1.0, LN_EPS, bveps, brstd, signal["rstd4"])
                power(6, signal["var5"], bmv[:, :, 1], 1.0, LN_EPS, bveps, brstd, signal["rstd5"])
            pool.wait_ge(signal["emb_gathered"], at(pool, B + 1, 16 * T, 0))

        @block.scalar
        def _(act):
            WAIT_REGISTER[act.engine] = act.alloc_register("wait_value")
            def copy(dst, src):
                return act.activation(dst, src, ACT.Copy)

            def high(i, ready, psum, dst, done):
                for c in range(C):
                    act.wait_ge(ready, at(act, i, C, c + 1))
                    copy(dst[:, HALF * c:HALF * c + HALF], psum[:, c, :]).then_inc(done, 1)

            act.wait_ge(signal["const_loaded"], 16 * 18)
            copy(spread[:], spread_f).then_inc(signal["const_cast"], 1)
            with act.Fori(0, B, 1) as i:
                for c in range(C):
                    half = slice(HALF * c, HALF * c + HALF)
                    act.wait_ge(signal["x1T"], at(act, i, C, c + 1))
                    copy(hh[:, half], fo[:, c, :]).then_inc(signal["hh1"], 1)
                    copy(aa[:, half], fo[:, c, :]).then_inc(signal["aa1"], 1)
                for u in range(NSELF):
                    act.wait_ge(signal["s1"], at(act, i, NSELF, u + 1))
                    if u >= 4:
                        act.wait_ge(signal["pv1"], at(act, i, NSELF, u - 3))
                    act.activation(prob[:, u % 4, :], fw[:, u % 2, :], ACT.Exp, scale=1.0 / 8).then_inc(signal["e1"], 1)
                high(i, signal["x2T"], fo, hh, signal["hh2"])
                for c in range(C):
                    act.wait_ge(signal["qk_ready"], at(act, i, C, c + 1))
                    copy(qkh[:, HALF * c:HALF * c + HALF], qk[:, HALF * c:HALF * c + HALF]).then_inc(signal["qkh_ready"], 1)
                act.wait_ge(signal["v_ps"], at(act, i, 1, 1))
                copy(v1[:, :, :, 0:HD], fo[:, 0, 0:T * 32].rearrange("p (t g d) -> p t g d", t=T, g=NKV)) \
                    .then_inc(signal["v_ready"], 1)
                act.wait_ge(signal["maxT"], at(act, i, 1, 1))
                act.activation(negm[:], fo[0:NH * T, 1, 0:P], ACT.Copy, scale=-1.0).then_inc(signal["negm_ready"], 1)
                for u, (j, c, w, heads) in enumerate(PROB_TILES):
                    act.wait_ge(signal["s2"], at(act, i, NPROB, u + 1))
                    if u >= NRING:
                        act.wait_ge(signal["pv2"], at(act, i, NPROB, u - NRING + 1))
                    n = w * len(heads)
                    act.activation(prob[:, u % NRING, 0:n], fw[:, u % 2, 0:n], ACT.Exp, scale=0.25) \
                        .then_inc(signal["e2"], 1)
                act.wait_ge(signal["pv2"], at(act, i, NPROB, NPROB))
                for c in range(C):
                    copy(ot[:, HALF * c:HALF * c + HALF], fo[:, c, :]).then_inc(signal["ot_ready"], 1)
                for c in range(C):
                    act.wait_ge(signal["yT"], at(act, i, C, c + 1))
                    copy(yt[:, HALF * c:HALF * c + HALF], fo[0:D, c, :]).then_inc(signal["yt_ready"], 1)
                high(i, signal["x3T"], bo, bhh, signal["hh3"])
                act.wait_ge(signal["lmax_ready"], at(act, i, 1, 1))
                act.activation(ex[:], lg[:], ACT.Exp).then_inc(signal["ex_ready"], 1)
                for c in range(C):
                    act.wait_ge(signal["rwT"], at(act, i, C, c + 1))
                    copy(wt[0:NE, HALF * c:HALF * c + HALF], bo[0:NE, c, :]).then_inc(signal["wth_ready"], 1)
                for u in range(MT * C):
                    m = u // C
                    n = min(P, EH - m * P)
                    act.wait_ge(signal["moe_a"], at(act, i, MT * C, u + 1))
                    if u >= 2:
                        act.wait_ge(signal["ub_ready"], at(act, i, MT * C, u - 1))
                    act.activation(sa[0:n, u % 2, :], bw[0:n, 0, :], ACT.Silu).then_inc(signal["silu"], 1)
                act.wait_ge(signal["w2_step"], at(act, i, MT, MT))
                copy(mt[:], bo[:, 1, :]).then_inc(signal["mt_ready"], 1)
                high(i, signal["x4T"], bo, bhh, signal["hh4"])
                for c in range(C):
                    half = slice(HALF * c, HALF * c + HALF)
                    act.wait_ge(signal["q_ps"], at(act, i, C, c + 1))
                    act.activation(qh[:, half], bw[:, c, :], ACT.Identity, bias=bq[:, 0:1]).then_inc(signal["qh_ready"], 1)
                for c in range(C):
                    half = slice(HALF * c, HALF * c + HALF)
                    act.wait_ge(signal["k_ps"], at(act, i, C, c + 1))
                    act.activation(ka[:, half], bw[:, c, :], ACT.Identity, bias=bk[:, 0:1]).then_inc(signal["ka_ready"], 1)
                    act.activation(k2[0:D, half], bw[0:D, c, :], ACT.Identity, bias=bk[0:D, 0:1]) \
                        .then_inc(signal["k2_ready"], 1)
                act.wait_ge(signal["m3T"], at(act, i, 1, 1))
                act.activation(negm3[:], bo[0:T, 1, 0:P], ACT.Copy, scale=-1.0).then_inc(signal["negm3_ready"], 1)
                for u in range(NSELF):
                    act.wait_ge(signal["s3"], at(act, i, NSELF, u + 1))
                    if u >= 4:
                        act.wait_ge(signal["pv3"], at(act, i, NSELF, u - 3))
                    act.activation(bprob[:, u % 4, :], bw[:, u % 2, :], ACT.Exp, scale=1.0 / 8).then_inc(signal["e3"], 1)
                high(i, signal["x5T"], bo, bhh, signal["hh5"])
                for c in range(C):
                    act.wait_ge(signal["othersT"], at(act, i, C, c + 1))
                    copy(otherst[:, HALF * c:HALF * c + HALF], bo[0:E1, c, :]).then_inc(signal["otherst_ready"], 1)
                for u in range(M1 * C):
                    act.wait_ge(signal["s5"], at(act, i, M1 * C, u + 1))
                    if u >= NHID:
                        act.wait_ge(signal["w5_step"], at(act, i, M1, (u - NHID) // C + 1))
                    act.activation(hid[:, u % NHID, :], bw[:, u % 2, :], ACT.Relu, bias=b1_2[:, u // C:u // C + 1]) \
                        .then_inc(signal["hid5_ready"], 1)
                act.wait_ge(signal["w5_step"], at(act, i, M1, M1))
                act.activation(mt2[:], bo[:, 1, :], ACT.Relu).then_inc(signal["mt5_ready"], 1)

        @block.vector
        def _(dve):
            WAIT_REGISTER[dve.engine] = dve.alloc_register("wait_value")
            dve.memset(ks[96:128, :].bitcast(F32), 1.0).then_inc(signal["filled"], 1)
            dve.memset(k2[D:D + 1, :].bitcast(F32), 1.0).then_inc(signal["filled"], 1)
            dve.memset(h4[:], 0.0).then_inc(signal["h4_free"], 16)
            dve.wait_ge(signal["const_loaded"], 16 * 18)
            dve.wait_ge(signal["w1_loaded"], 32)
            for k, (c0, c1) in enumerate((GROUP1, GROUP2)):
                dve.tensor_scalar(w_f[:, c0:c1], w_f[:, c0:c1], lnw[:, k:k + 1], None, ALU.mult).then_inc(signal["w_scaled"], 1)
            dve.wait_ge(signal["w_scaled"], 2)
            dve.tensor_copy(w_s[:], w_f[:]).then_inc(signal["w_high"], 1)
            dve.wait_ge(signal["w_high"], 1)
            dve.tensor_tensor(w_s[D:P, :], w_f[D:P, :], w_s[D:P, :].bitcast(F32), ALU.subtract).then_inc(signal["w_ready"], 1)
            dve.wait_ge(signal["filled"], 9)

            def low(i, ready, psum, high_of, dst, done, rows=slice(0, P)):
                for c in range(C):
                    half = slice(HALF * c, HALF * c + HALF)
                    dve.wait_ge(ready, at(dve, i, C, c + 1))
                    dve.tensor_tensor(dst[rows, half], psum[rows, c, :], high_of[rows, half].bitcast(F32),
                                      ALU.subtract).then_inc(done, 1)

            with dve.Fori(0, B, 1) as i:
                count = {"f": 0, "b": 0}

                def link(ins, which="f", apart=False):
                    count[which] += 1
                    sem, per = (signal["step_f"], DVE_FRONT) if which == "f" else (signal["step_b"], DVE_BACK)
                    ins.then_inc(sem, 1)
                    if apart:
                        wait_apart(dve, sem, at(dve, i, per, count[which]))
                    else:
                        dve.wait_ge(sem, at(dve, i, per, count[which]))

                def moments(src, st, m, which):
                    for t in range(T):
                        ins = dve.bn_stats(st[:, t, :], src[:, t, :])
                    link(ins, which, apart=True)
                    for t in range(T):
                        ins = dve.bn_aggr(m[:, t, :], st[:, t, :])
                    return ins

                dve.wait_ge(signal["emb_gathered"], at(dve, i, 16 * T, 16 * T))
                link(dve.tensor_scalar(keep[:], idx[:], 0, None, ALU.not_equal))
                dve.tensor_tensor(h0[:], emb[:], dup(keep[:]), ALU.mult).then_inc(signal["emb_used"], 1)
                dve.wait_ge(signal["emb_used"], at(dve, i, 1, 1))
                moments(h0, stats, mv, "f").then_inc(signal["var1"], 1)
                dve.wait_ge(signal["rstd1"], at(dve, i, 1, 1))
                for t in range(T):
                    dve.tensor_scalar(xd[:, t, :, :], h0[:, t, :].unsqueeze(1).to_broadcast([P, 2, D]), mv[:, t, 0:1],
                                      rstd[:, t:t + 1], ALU.subtract, ALU.mult).then_inc(signal["x1_ready"], 1)
                dve.wait_ge(signal["x1_ready"], at(dve, i, T + 1, T))
                dve.tensor_copy(x1v[:, :, 0:D], xd[:, :, 0, :]).then_inc(signal["x1_ready"], 1)
                for c in range(C):
                    half = slice(HALF * c, HALF * c + HALF)
                    dve.wait_ge(signal["hh1"], at(dve, i, C, c + 1))
                    dve.wait_ge(signal["aa1"], at(dve, i, C, c + 1))
                    dve.tensor_tensor(ll[:, half], fo[:, c, :], hh[:, half].bitcast(F32), ALU.subtract) \
                        .then_inc(signal["ll1"], 1)
                    dve.tensor_tensor(aa[D:P, half], fo[D:P, c, :], aa[D:P, half].bitcast(F32), ALU.subtract) \
                        .then_inc(signal["aal1"], 1)
                dve.wait_ge(signal["pv1"], at(dve, i, NSELF, NSELF))
                acc = fo[:, :, 0:TH * (D + 1)].rearrange("p c (t d) -> p c t d", t=TH)
                link(dve.reciprocal(rsum[:].rearrange("p (c t) -> p c t", c=C), acc[:, :, :, D]))
                for c in range(C):
                    ins = dve.tensor_tensor(att[:, TH * c:TH * c + TH, :], acc[:, c, :, 0:D],
                                            dup(rsum[:, TH * c:TH * c + TH]), ALU.mult)
                link(ins)
                dve.tensor_tensor(h1[:], att[:], h0[:], ALU.add).then_inc(signal["h1_ready"], 1)
                dve.wait_ge(signal["h1_ready"], at(dve, i, 1, 1))
                moments(h1, stats, mv, "f").then_inc(signal["var2"], 1)
                dve.wait_ge(signal["rstd2"], at(dve, i, 1, 1))
                for t in range(T):
                    ins = dve.tensor_scalar(x2[:, t, :], h1[:, t, :], mv[:, t, 0:1], rstd[:, t:t + 1],
                                            ALU.subtract, ALU.mult)
                link(ins)

                def rms(src, ssq, rrms, dst, done):
                    link(dve.tensor_tensor(sq[:], src[:], src[:], ALU.mult))
                    dve.tensor_reduce(ssum[:], sq[:], AX.X, ALU.add).then_inc(ssq, 1)
                    dve.wait_ge(rrms, at(dve, i, 1, 1))
                    for r in range(2):
                        ins = dve.tensor_tensor(dst[:, :, r, :], src[:], dup(rstd[:]), ALU.mult)
                    ins.then_inc(done, 1)

                rms(x2, signal["ssq2"], signal["rrms2"], xd, signal["x2_ready"])
                low(i, signal["hh2"], fo, hh, ll, signal["ll2"])
                for c in range(C):
                    half = slice(HALF * c, HALF * c + HALF)
                    dve.wait_ge(signal["qk_ps"], at(dve, i, C, c + 1))
                    dve.tensor_tensor(rope_a[:, c, :], fw[0:96, 0, :], cos[:, half], ALU.mult).then_inc(signal["rope_used"], 1)
                    dve.tensor_tensor(rope_b[:, c, :], fw[0:96, 1, :], sin[:, half], ALU.mult).then_inc(signal["rope_used"], 1)
                    dve.wait_ge(signal["rope_used"], at(dve, i, 2 * C, 2 * c + 2))
                    dve.tensor_tensor(qk[:, half], rope_a[:, c, :], rope_b[:, c, :], ALU.add).then_inc(signal["qk_ready"], 1)
                for c in range(C):
                    half = slice(HALF * c, HALF * c + HALF)
                    dve.wait_ge(signal["qkh_ready"], at(dve, i, C, c + 1))
                    dve.tensor_tensor(qkl[:, half], qk[:, half], qkh[:, half].bitcast(F32), ALU.subtract) \
                        .then_inc(signal["qkl_ready"], 1)
                for u, (j, c, w, heads) in enumerate(MAX_TILES):
                    dve.wait_ge(signal["sm"], at(dve, i, NMAX, u + 1))
                    n = len(heads)
                    dve.tensor_reduce(mx[:, heads[0]:heads[0] + n, j, c],
                                      fw[:, u % 2, 0:n * w].rearrange("p (h w) -> p h w", h=n),
                                      AX.X, ALU.max).then_inc(signal["max_used"], 1)
                dve.wait_ge(signal["max_used"], at(dve, i, NMAX, NMAX))
                dve.tensor_reduce(mxt[:], mx[:], AX.X, ALU.max).then_inc(signal["max_ready"], 1)
                dve.wait_ge(signal["otT"], at(dve, i, C, C))
                for c in range(C):
                    o4 = fo[:, c, :].rearrange("p (t h d) -> p t h d", t=TH, h=NH)
                    link(dve.reciprocal(rs4[:, TH * c:TH * c + TH, :], o4[:, :, :, HD]))
                    dve.tensor_tensor(y[:, TH * c:TH * c + TH, :].rearrange("p t (h d) -> p t h d", h=NH),
                                      o4[:, :, :, 0:HD],
                                      rs4[:, TH * c:TH * c + TH, :].unsqueeze(3).to_broadcast([P, TH, NH, HD]),
                                      ALU.mult).then_inc(signal["y_ready"], 1)
                dve.wait_ge(signal["wo_ps"], at(dve, i, 1, 1))
                link(dve.tensor_tensor(x3[:], fw[:, 0, :].rearrange("p (t d) -> p t d", t=T), x2[:], ALU.add))
                dve.tensor_tensor(res[:], x3[:], h1[:], ALU.add).then_inc(signal["x3_ready"], 1)
                rms(x3, signal["ssq3"], signal["rrms3"], x3d, signal["x3_done"])
                assert count["f"] == DVE_FRONT, count

                low(i, signal["hh3"], bo, bhh, bll, signal["ll3"])
                dve.wait_ge(signal["lg_ps"], at(dve, i, 1, 1))
                lg_ps = bw[:, 0, 0:T * NE].rearrange("p (t e) -> p t e", t=T)
                link(dve.tensor_reduce(lmax[:], lg_ps, AX.X, ALU.max), "b")
                dve.tensor_tensor(lg[:], lg_ps, lmax[:].unsqueeze(2).to_broadcast([P, T, NE]), ALU.subtract) \
                    .then_inc(signal["lmax_ready"], 1)
                wait_apart(dve, signal["lmax_ready"], at(dve, i, 1, 1))
                for t in range(T):
                    ins = dve.max(top8[:, t, :], lg[:, t, :])
                link(ins, "b", apart=True)
                for t in range(T):
                    ins = dve.max_index(topi[:, t, :], top8[:, t, :], lg[:, t, :])
                link(ins, "b")
                link(dve.tensor_copy(topf[:], topi[:, :, 0:2]), "b")
                experts = iota[:, 0:NE].unsqueeze(1).to_broadcast([P, T, NE])
                dve.tensor_tensor(oh_a[:], experts, topf[:, :, 0:1].to_broadcast([P, T, NE]), ALU.is_equal)
                link(dve.tensor_tensor(oh_b[:], experts, topf[:, :, 1:2].to_broadcast([P, T, NE]), ALU.is_equal), "b")
                link(dve.tensor_tensor(oh_a[:], oh_a[:], oh_b[:], ALU.add), "b")
                dve.wait_ge(signal["ex_ready"], at(dve, i, 1, 1))
                link(dve.tensor_reduce(esum[:], ex[:], AX.X, ALU.add), "b")
                link(dve.reciprocal(esum[:], esum[:]), "b")
                link(dve.tensor_tensor(ex[:], ex[:], esum[:].unsqueeze(2).to_broadcast([P, T, NE]), ALU.mult), "b")
                link(dve.tensor_tensor(ex[:], ex[:], oh_a[:], ALU.mult), "b")
                link(dve.tensor_reduce(esum[:], ex[:], AX.X, ALU.add), "b")
                link(dve.tensor_scalar(esum[:], esum[:], 1e-9, None, ALU.add), "b")
                link(dve.reciprocal(esum[:], esum[:]), "b")
                dve.tensor_tensor(ex[:], ex[:], esum[:].unsqueeze(2).to_broadcast([P, T, NE]), ALU.mult) \
                    .then_inc(signal["rw_ready"], 1)
                for c in range(C):
                    half = slice(HALF * c, HALF * c + HALF)
                    dve.wait_ge(signal["wth_ready"], at(dve, i, C, c + 1))
                    dve.tensor_tensor(wt[32:32 + NE, half], bo[0:NE, c, :], wt[0:NE, half].bitcast(F32), ALU.subtract) \
                        .then_inc(signal["wt_ready"], 1)
                for u in range(MT * C):
                    n = min(P, EH - u // C * P)
                    dve.wait_ge(signal["silu"], at(dve, i, MT * C, u + 1))
                    dve.wait_ge(signal["moe_b"], at(dve, i, MT * C, u + 1))
                    dve.tensor_tensor(ub[0:n, u % 2, :], sa[0:n, u % 2, :], bw[0:n, 1, :], ALU.mult) \
                        .then_inc(signal["ub_ready"], 1)
                    dve.wait_ge(signal["ub_ready"], at(dve, i, MT * C, u + 1))
                    dve.wait_ge(signal["moe_w"], at(dve, i, MT * C, u + 1))
                    if u >= NHID:
                        dve.wait_ge(signal["w2_step"], at(dve, i, MT, (u - NHID) // C + 1))
                    dve.tensor_tensor(hid[0:n, u % NHID, :], ub[0:n, u % 2, :], bo[0:n, 0, :], ALU.mult) \
                        .then_inc(signal["hid_ready"], 1)
                dve.wait_ge(signal["mtT"], at(dve, i, 1, 1))

                def by_half(x):
                    return x.rearrange("p (c t) d -> p t c d", c=C)

                dve.tensor_tensor(by_half(h2[:]), bw[:, 0, :].rearrange("p (t c d) -> p t c d", t=TH, c=C),
                                  by_half(res[:]), ALU.add).then_inc(signal["h2_ready"], 1)
                dve.wait_ge(signal["h2_ready"], at(dve, i, 1, 1))

                def norm_back(src, var, rstd_done, done):
                    moments(src, bstats, bmv, "b").then_inc(var, 1)
                    dve.wait_ge(rstd_done, at(dve, i, 1, 1))
                    for t in range(T):
                        ins = dve.tensor_scalar(bxd[:, t, :, :], src[:, t, :].unsqueeze(1).to_broadcast([P, 2, D]),
                                                bmv[:, t, 0:1], brstd[:, t:t + 1], ALU.subtract, ALU.mult)
                    ins.then_inc(done, 1)

                norm_back(h2, signal["var4"], signal["rstd4"], signal["x4_ready"])
                low(i, signal["hh4"], bo, bhh, bll, signal["ll4"])
                for c in range(C):
                    half = slice(HALF * c, HALF * c + HALF)
                    dve.wait_ge(signal["qh_ready"], at(dve, i, C, c + 1))
                    dve.scalar_tensor_tensor(out=ql[0:D, half], in0=bw[0:D, c, :], scalar=bq[0:D, 0:1],
                                             in1=qh[0:D, half].bitcast(F32), op0=ALU.add, op1=ALU.subtract) \
                        .then_inc(signal["ql_ready"], 1)
                for c in range(C):
                    half = slice(HALF * c, HALF * c + HALF)
                    dve.wait_ge(signal["ka_ready"], at(dve, i, C, c + 1))
                    dve.wait_ge(signal["k2_ready"], at(dve, i, C, c + 1))
                    dve.scalar_tensor_tensor(out=ka[D:P, half], in0=bw[D:P, c, :], scalar=bk[D:P, 0:1],
                                             in1=ka[D:P, half].bitcast(F32), op0=ALU.add, op1=ALU.subtract) \
                        .then_inc(signal["kal_ready"], 1)
                dve.wait_ge(signal["v2_ps"], at(dve, i, 1, 1))
                dve.tensor_tensor(v2[:, :, 0:D], bo[:, 0, :].rearrange("p (t d) -> p t d", t=T),
                                  bv[:].unsqueeze(1).to_broadcast([P, T, D]), ALU.add).then_inc(signal["v2_ready"], 1)
                for u in range(NSELF):
                    dve.wait_ge(signal["sm3"], at(dve, i, NSELF, u + 1))
                    dve.tensor_reduce(mx3[:, u % C, u // C:u // C + 1], bw[:, u % 2, :], AX.X, ALU.max) \
                        .then_inc(signal["max3_used"], 1)
                dve.wait_ge(signal["max3_used"], at(dve, i, NSELF, NSELF))
                dve.tensor_tensor(m3[:], mx3[:, 0, :], mx3[:, 1, :], ALU.max).then_inc(signal["m3_ready"], 1)
                dve.wait_ge(signal["pv3"], at(dve, i, NSELF, NSELF))
                bacc = bo[:, :, 0:TH * (D + 1)].rearrange("p c (t d) -> p c t d", t=TH)
                link(dve.reciprocal(brsum[:].rearrange("p (c t) -> p c t", c=C), bacc[:, :, :, D]), "b")
                for c in range(C):
                    ins = dve.tensor_tensor(batt[:, TH * c:TH * c + TH, :], bacc[:, c, :, 0:D],
                                            dup(brsum[:, TH * c:TH * c + TH]), ALU.mult)
                link(ins, "b")
                dve.tensor_tensor(h3[:], batt[:], h2[:], ALU.add).then_inc(signal["h3_ready"], 1)
                dve.wait_ge(signal["h3_ready"], at(dve, i, 1, 1))
                norm_back(h3, signal["var5"], signal["rstd5"], signal["x5_ready"])
                low(i, signal["hh5"], bo, bhh, bll, signal["ll5"])
                dve.wait_ge(signal["lg5_ps"], at(dve, i, 1, 1))
                link(dve.tensor_tensor(lg5[:], bw[:, 0, 0:T * E1].rearrange("p (t e) -> p t e", t=T),
                                       rb[:].unsqueeze(1).to_broadcast([P, T, E1]), ALU.add), "b", apart=True)
                for t in range(T):
                    ins = dve.max(top8b[:, t, :], lg5[:, t, :])
                link(ins, "b", apart=True)
                for t in range(T):
                    ins = dve.max_index(topib[:, t, :], top8b[:, t, :], lg5[:, t, :])
                link(ins, "b")
                link(dve.tensor_copy(topfb[:], topib[:, :, 0]), "b")
                dve.tensor_tensor(others[:], iota[:].unsqueeze(1).to_broadcast([P, T, E1]),
                                  topfb[:].unsqueeze(2).to_broadcast([P, T, E1]), ALU.not_equal) \
                    .then_inc(signal["others_ready"], 1)
                for c in range(C):
                    dve.wait_ge(signal["otherst_ready"], at(dve, i, C, c + 1))
                    dve.tensor_scalar(chosent[:, HALF * c:HALF * c + HALF], bo[0:E1, c, :], -1.0, 1.0,
                                      ALU.mult, ALU.add).then_inc(signal["chosent_ready"], 1)
                dve.wait_ge(signal["h4_free"], at(dve, i, 16, 16))
                dve.wait_ge(signal["mt5T"], at(dve, i, 1, 1))
                dve.tensor_tensor(by_half(h4[:]), bw[:, 0, :].rearrange("p (t c d) -> p t c d", t=TH, c=C),
                                  by_half(h3[:]), ALU.add).then_inc(signal["h4_ready"], 1)
                assert count["b"] == DVE_BACK, count

        @block.tensor
        def _(pe):
            WAIT_REGISTER[pe.engine] = pe.alloc_register("wait_value")
            pe.wait_ge(signal["w_ready"], 1)
            pe.wait_ge(signal["const_cast"], 1)
            pe.wait_ge(signal["w2_loaded"], 32)
            pe.wait_ge(signal["filled"], 9)

            def transposes(src, psum, done):
                for t in range(T):
                    ins = pe.transpose(psum[:, t // TH, P * (t % TH):P * (t % TH) + P],
                                       src[:, t, :, :].rearrange("p r d -> p (r d)"), ident[:])
                    if t % TH == TH - 1:
                        ins.then_inc(done, 1)

            def project(dst, w, h, l, c):
                half = slice(HALF * c, HALF * c + HALF)
                pe.matmul(dst, w, h[:, half], start=True, stop=False)
                return pe.matmul(dst, w, l[:, half], start=False, stop=True)

            def project_rows(dst, w, h, l, t):
                pe.matmul(dst, h[:, P * t:P * t + P], w, start=True, stop=False)
                return pe.matmul(dst, l[:, P * t:P * t + P], w, start=False, stop=True)

            def weigh(psum, pr, values, u):
                j, c = u // C, u % C
                for t in range(TH):
                    ins = pe.matmul(psum[:, c, (D + 1) * t:(D + 1) * (t + 1)], pr[:, u % 4, P * t:P * t + P],
                                    values[:, j, :], start=(j == 0 and t == 0), stop=(j == T - 1),
                                    skip_group_check=True)
                return ins

            def back_rows(src, psum):
                for t in range(TH):
                    ins = pe.transpose(psum[:, P * t:P * t + P], src[:, P * t:P * t + P], ident[:])
                return ins

            with pe.Fori(0, B, 1) as i:
                pe.wait_ge(signal["x1_ready"], at(pe, i, T + 1, T + 1))
                transposes(xd, fo, signal["x1T"])

                def scores1(u):
                    j, c = u // C, u % C
                    if u < C:
                        pe.wait_ge(signal["ll1"], at(pe, i, C, c + 1))
                        pe.wait_ge(signal["aal1"], at(pe, i, C, c + 1))
                    if u >= 2:
                        pe.wait_ge(signal["e1"], at(pe, i, NSELF, u - 1))
                    project(fw[:, u % 2, :], aa[:, P * j:P * j + P], hh, ll, c).then_inc(signal["s1"], 1)

                for u in range(NSELF + 2):
                    if u < NSELF:
                        scores1(u)
                    if u >= 2:
                        pe.wait_ge(signal["e1"], at(pe, i, NSELF, u - 1))
                        weigh(fo, prob, x1v, u - 2).then_inc(signal["pv1"], 1)
                pe.wait_ge(signal["x2_ready"], at(pe, i, 1, 1))
                transposes(xd, fo, signal["x2T"])
                for c in range(C):
                    pe.wait_ge(signal["ll2"], at(pe, i, C, c + 1))
                    if c:
                        pe.wait_ge(signal["rope_used"], at(pe, i, 2 * C, 2 * c))
                    project(fw[0:96, 0, :], weight("qk"), hh, ll, c)
                    project(fw[0:96, 1, :], weight("qk_swapped"), hh, ll, c).then_inc(signal["qk_ps"], 1)
                for t in range(T):
                    ins = project_rows(fo[:, 0, 32 * t:32 * t + 32], weight("v"), hh, ll, t)
                ins.then_inc(signal["v_ps"], 1)
                pe.wait_ge(signal["spread_done"], at(pe, i, 16 * 15, 16 * 15))
                for u, (j, c, w, heads) in enumerate(MAX_TILES):
                    if u < 2:
                        pe.wait_ge(signal["rope_used"], at(pe, i, 2 * C, 2 * C))
                    else:
                        pe.wait_ge(signal["max_used"], at(pe, i, NMAX, u - 1))
                    diagonal = HALF * c + w == P * (j + 1)
                    for n, h in enumerate(heads):
                        dst = fw[:, u % 2, n * w:n * w + w]
                        if diagonal:
                            pe.matmul(dst[:, w - P:w], ident16[:], mask_qk[:], start=True, stop=False,
                                      skip_group_check=True)
                        ins = pe.matmul(dst, qs[0:96, h, P * j:P * j + P], ks[0:96, HALF * c:HALF * c + w],
                                        start=not diagonal, stop=True, skip_group_check=True)
                    ins.then_inc(signal["sm"], 1)
                pe.wait_ge(signal["max_ready"], at(pe, i, 1, 1))
                pe.wait_ge(signal["hh2"], at(pe, i, C, C))
                pe.transpose(fo[0:NH * T, 1, 0:P], mxt[:].rearrange("p h t -> p (h t)"), ident[:]).then_inc(signal["maxT"], 1)
                pe.wait_ge(signal["negm_placed"], at(pe, i, 16, 16))
                pe.wait_ge(signal["v_ready"], at(pe, i, 1, 1))

                def scores2(u):
                    j, c, w, heads = PROB_TILES[u]
                    if u >= 2:
                        pe.wait_ge(signal["e2"], at(pe, i, NPROB, u - 1))
                    q0 = HALF * (c + 1) - w
                    diagonal = q0 == P * j
                    for n, h in enumerate(heads):
                        dst = fw[:, u % 2, n * w:n * w + w]
                        if diagonal:
                            pe.matmul(dst[:, 0:P], ident16[:], mask_kq[:], start=True, stop=False,
                                      skip_group_check=True)
                        ins = pe.matmul(dst, ks[0:97, P * j:P * j + P], qs[0:97, h, q0:q0 + w],
                                        start=not diagonal, stop=True, skip_group_check=True)
                    ins.then_inc(signal["s2"], 1)

                def weigh2(u):
                    j, c, w, heads = PROB_TILES[u]
                    pe.wait_ge(signal["e2"], at(pe, i, NPROB, u + 1))
                    for n, h in enumerate(heads):
                        ins = pe.matmul(fo[32 * h:32 * h + 32, c, HALF - w:HALF], v1[:, j, h // 2, :],
                                        prob[:, u % NRING, n * w:n * w + w], start=(j == 0),
                                        stop=(j == TH * (c + 1) - 1), skip_group_check=True,
                                        tile_position=(0, 32 * h))
                    ins.then_inc(signal["pv2"], 1)

                groups = {}
                for u, (j, c, w, heads) in enumerate(PROB_TILES):
                    groups.setdefault((j, c), []).append(u)
                groups = list(groups.values())
                for g in range(len(groups) + 1):
                    if g < len(groups):
                        for u in groups[g]:
                            scores2(u)
                    if g >= 1:
                        for u in groups[g - 1]:
                            weigh2(u)
                pe.wait_ge(signal["ot_ready"], at(pe, i, C, C))
                for t in range(T):
                    ins = pe.transpose(fo[:, t // TH, P * (t % TH):P * (t % TH) + P], ot[:, P * t:P * t + P], ident[:])
                    if t % TH == TH - 1:
                        ins.then_inc(signal["otT"], 1)
                for t in range(T):
                    if t % TH == 0:
                        wait_apart(pe, signal["y_ready"], at(pe, i, C, t // TH + 1))
                    ins = pe.transpose(fo[0:D, t // TH, P * (t % TH):P * (t % TH) + P], y[:, t, :], ident[:])
                    if t % TH == TH - 1:
                        ins.then_inc(signal["yT"], 1)
                for t in range(T):
                    if t % TH == 0:
                        pe.wait_ge(signal["yt_ready"], at(pe, i, C, t // TH + 1))
                    ins = pe.matmul(fw[:, 0, D * t:D * t + D], yt[:, P * t:P * t + P], wo[:], start=True, stop=True)
                ins.then_inc(signal["wo_ps"], 1)

                pe.wait_ge(signal["x3_done"], at(pe, i, 1, 1))
                transposes(x3d, bo, signal["x3T"])
                pe.wait_ge(signal["ll3"], at(pe, i, C, C))
                for t in range(T):
                    ins = project_rows(bw[:, 0, NE * t:NE * t + NE], weight("router"), bhh, bll, t)
                ins.then_inc(signal["lg_ps"], 1)
                pe.wait_ge(signal["rw_ready"], at(pe, i, 1, 1))
                for t in range(T):
                    ins = pe.transpose(bo[0:NE, t // TH, P * (t % TH):P * (t % TH) + P], ex[:, t, :], ident[:])
                    if t % TH == TH - 1:
                        ins.then_inc(signal["rwT"], 1)
                pe.wait_ge(signal["wt_ready"], at(pe, i, C, C))

                def experts_out(m):
                    pe.wait_ge(signal["hid_ready"], at(pe, i, MT * C, C * m + C))
                    n = min(P, EH - m * P)
                    for c in range(C):
                        ins = pe.matmul(bo[D * c:D * c + D, 1, :], w2[0:n, m, :], hid[0:n, (C * m + c) % NHID, :],
                                        start=(m == 0), stop=(m == MT - 1), skip_group_check=True,
                                        tile_position=(0, D * c))
                    ins.then_inc(signal["w2_step"], 1)
                    return ins

                for u in range(MT * C):
                    m, c = u // C, u % C
                    n = min(P, EH - m * P)
                    if u >= 1:
                        pe.wait_ge(signal["silu"], at(pe, i, MT * C, u))
                    project(bw[0:n, 0, :], weight("w1", P * m, n), bhh, bll, c).then_inc(signal["moe_a"], 1)
                    if u >= 1:
                        pe.wait_ge(signal["ub_ready"], at(pe, i, MT * C, u))
                    project(bw[0:n, 1, :], weight("w3", P * m, n), bhh, bll, c).then_inc(signal["moe_b"], 1)
                    if u >= 1:
                        pe.wait_ge(signal["hid_ready"], at(pe, i, MT * C, u))
                    pe.matmul(bo[0:n, 0, :], spread[:, P * m:P * m + n], wt[:, HALF * c:HALF * c + HALF],
                              start=True, stop=True).then_inc(signal["moe_w"], 1)
                    if c == 0 and m >= 1:
                        experts_out(m - 1)
                pe.wait_ge(signal["hid_ready"], at(pe, i, MT * C, MT * C))
                experts_out(MT - 1)
                pe.wait_ge(signal["mt_ready"], at(pe, i, 1, 1))
                back_rows(mt, bw[:, 0, :]).then_inc(signal["mtT"], 1)
                pe.wait_ge(signal["x4_ready"], at(pe, i, 1, 1))
                transposes(bxd, bo, signal["x4T"])
                pe.wait_ge(signal["h2_ready"], at(pe, i, 1, 1))
                for c in range(C):
                    pe.wait_ge(signal["ll4"], at(pe, i, C, c + 1))
                    project(bw[:, c, :], weight("q2"), bhh, bll, c).then_inc(signal["q_ps"], 1)
                for t in range(T):
                    ins = project_rows(bo[:, 0, D * t:D * t + D], weight("v2"), bhh, bll, t)
                ins.then_inc(signal["v2_ps"], 1)
                for c in range(C):
                    pe.wait_ge(signal["ql_ready"], at(pe, i, C, c + 1))
                    project(bw[:, c, :], weight("k2"), bhh, bll, c).then_inc(signal["k_ps"], 1)
                for u in range(NSELF):
                    j, c = u // C, u % C
                    if u < 2:
                        pe.wait_ge(signal["kal_ready"], at(pe, i, C, c + 1))
                        pe.wait_ge(signal["k2_ready"], at(pe, i, C, c + 1))
                    else:
                        pe.wait_ge(signal["max3_used"], at(pe, i, NSELF, u - 1))
                    pe.matmul(bw[:, u % 2, :], qh[:, P * j:P * j + P], ka[:, HALF * c:HALF * c + HALF],
                              start=True, stop=True).then_inc(signal["sm3"], 1)
                pe.wait_ge(signal["m3_ready"], at(pe, i, 1, 1))
                pe.transpose(bo[0:T, 1, 0:P], m3[:], ident[:]).then_inc(signal["m3T"], 1)
                pe.wait_ge(signal["negm3_placed"], at(pe, i, 16, 16))
                pe.wait_ge(signal["v2_ready"], at(pe, i, 1, 1))

                def scores3(u):
                    j, c = u // C, u % C
                    half = slice(HALF * c, HALF * c + HALF)
                    if u >= 2:
                        pe.wait_ge(signal["e3"], at(pe, i, NSELF, u - 1))
                    pe.matmul(bw[:, u % 2, :], ka[:, P * j:P * j + P], qh[:, half], start=True, stop=False)
                    pe.matmul(bw[:, u % 2, :], k2[:, P * j:P * j + P], ql[:, half], start=False, stop=True) \
                        .then_inc(signal["s3"], 1)

                for u in range(NSELF + 2):
                    if u < NSELF:
                        scores3(u)
                    if u >= 2:
                        pe.wait_ge(signal["e3"], at(pe, i, NSELF, u - 1))
                        weigh(bo, bprob, v2, u - 2).then_inc(signal["pv3"], 1)
                pe.wait_ge(signal["x5_ready"], at(pe, i, 1, 1))
                transposes(bxd, bo, signal["x5T"])
                pe.wait_ge(signal["ll5"], at(pe, i, C, C))
                for t in range(T):
                    ins = project_rows(bw[:, 0, E1 * t:E1 * t + E1], weight("router2"), bhh, bll, t)
                ins.then_inc(signal["lg5_ps"], 1)
                pe.wait_ge(signal["others_ready"], at(pe, i, 1, 1))
                for t in range(T):
                    ins = pe.transpose(bo[0:E1, t // TH, P * (t % TH):P * (t % TH) + P], others[:, t, :], ident[:])
                    if t % TH == TH - 1:
                        ins.then_inc(signal["othersT"], 1)

                def experts2_out(m):
                    pe.wait_ge(signal["hid5_ready"], at(pe, i, M1 * C, C * m + C))
                    for c in range(C):
                        ins = pe.matmul(bo[D * c:D * c + D, 1, :], w2_2[:, m, :], hid[:, (C * m + c) % NHID, :],
                                        start=False, stop=(m == M1 - 1), skip_group_check=True,
                                        tile_position=(0, D * c))
                    ins.then_inc(signal["w5_step"], 1)

                pe.wait_ge(signal["chosent_ready"], at(pe, i, C, C))
                pe.wait_ge(signal["otherst_ready"], at(pe, i, C, C))
                for c in range(C):
                    pe.matmul(bo[D * c:D * c + D, 1, :], b2_2[:], chosent[:, HALF * c:HALF * c + HALF],
                              start=True, stop=False, skip_group_check=True, tile_position=(0, D * c))
                for u in range(M1 * C):
                    m, c = u // C, u % C
                    if u >= 2:
                        pe.wait_ge(signal["hid5_ready"], at(pe, i, M1 * C, u - 1))
                    half = slice(HALF * c, HALF * c + HALF)
                    w = weight("w1_2", P * m, P)
                    pe.matmul(bw[:, u % 2, :], w, bhh[:, half], start=True, stop=False)
                    pe.matmul(bw[:, u % 2, :], w, bll[:, half], start=False, stop=False)
                    pe.matmul(bw[:, u % 2, :], block16[:, P * m:P * m + P], otherst[:, half],
                              start=False, stop=True).then_inc(signal["s5"], 1)
                    if c == 1 and m >= 1:
                        experts2_out(m - 1)
                experts2_out(M1 - 1)
                pe.wait_ge(signal["mt5_ready"], at(pe, i, 1, 1))
                back_rows(mt2, bw[:, 0, :]).then_inc(signal["mt5T"], 1)


def constants():
    p = np.arange(P)
    inv = 1.0 / 10000.0 ** (np.arange(0, HD, 2, dtype=np.float32) / HD)
    angles = np.outer(np.arange(L, dtype=np.float32), inv)
    emb = np.concatenate([angles, angles], axis=-1)
    sign = np.where(np.arange(HD) < HD // 2, -1.0, 1.0).astype(np.float32)
    spread = np.zeros((40, MT * P), np.float32)
    for e in range(NE):
        spread[[e, 32 + e], e * HID:(e + 1) * HID] = 1.0
    block16 = np.zeros((E1, E1 * H1), np.float32)
    for e in range(E1):
        block16[e, e * H1:(e + 1) * H1] = NEG
    bf16 = mybir.dt.np(BF16)
    return {
        "ident": np.eye(P, dtype=np.float32),
        "ident16": np.eye(P, dtype=np.float32).astype(bf16),
        "mask_qk": np.where(p[None, :] > p[:, None], NEG, 0.0).astype(bf16),
        "mask_kq": np.where(p[None, :] < p[:, None], NEG, 0.0).astype(bf16),
        "cos": np.ascontiguousarray(np.tile(np.cos(emb).T, (6, 1))),
        "sin": np.ascontiguousarray(np.tile((np.sin(emb) * sign).T, (6, 1))),
        "iota": np.tile(np.arange(E1, dtype=np.float32), (P, 1)),
        "spread": spread,
        "block16": block16.astype(bf16),
    }


def layout(v):
    wq, wk = v["L0_ffn_wq"], v["L0_ffn_wk"]

    def swapped(w):
        n = w.shape[0] // HD
        return w.reshape(n, 2, HD // 2, D)[:, ::-1].reshape(n * HD, D)

    wide = [wq, wk, swapped(wq), swapped(wk), v["L0_ffn_wv"], v["L0_ffn_router_w"],
            v["L0_ffn_w1"].reshape(EH, D), v["L0_ffn_w3"].reshape(EH, D),
            v["L1_attn_Wq"].T, v["L1_attn_Wq"].T, v["L1_attn_Wk"].T, v["L1_attn_Wk"].T, v["L1_attn_Wv"].T,
            v["L1_ffn_router_w"], v["L1_ffn_W1"].transpose(0, 2, 1).reshape(E1 * H1, D)]
    lnw = np.stack([v["L0_ffn_ln1_w"], v["L0_ffn_ln2_w"]], axis=1)
    return {
        "x": np.concatenate([v["x"], v["x"][:1]]).reshape(B + 1, T, P).transpose(0, 2, 1),
        "table": v["L0_tok_W"].T,
        "wcat": np.concatenate(wide, axis=0).T,
        "lnw": np.concatenate([lnw, lnw], axis=0),
        "wo": v["L0_ffn_wo"].T,
        "w2": v["L0_ffn_w2"].transpose(0, 2, 1).reshape(EH, D),
        "w2_2": v["L1_ffn_W2"].reshape(M1, P, D).transpose(1, 0, 2),
        "b1_2": v["L1_ffn_b1"].reshape(M1, P).T,
        "b2_2": v["L1_ffn_b2"],
        "bq": np.concatenate([v["L1_attn_bq"]] * 2).reshape(P, 1),
        "bk": np.concatenate([v["L1_attn_bk"]] * 2).reshape(P, 1),
        "bv": v["L1_attn_bv"],
        "rb": v["L1_ffn_router_b"],
    }


def kernel(**inputs):
    import concourse.bacc as bacc
    from concourse.bass_utils import run_bass_kernel_spmd

    nc = bacc.Bacc("TRN2", target_bir_lowering=False, num_devices=1)
    given = {k: np.asarray(x) for k, x in inputs.items()}
    arrays = {k: np.ascontiguousarray(x) for k, x in {**layout(given), **constants()}.items()}
    aps = {k: nc.dram_tensor(f"in_{k}", x.shape, mybir.dt.from_np(x.dtype), kind="ExternalInput").ap()
           for k, x in arrays.items()}
    out = nc.dram_tensor("out", (B, L, D), F32, kind="ExternalOutput").ap()
    tower(nc, aps, out)
    r = run_bass_kernel_spmd(nc, [{f"in_{k}": x for k, x in arrays.items()}], core_ids=[0])
    return r.results[0]["out"]
```

```python
from contextlib import ExitStack

import concourse.bass as bass
import numpy as np
from concourse import mybir

F32 = mybir.dt.float32
F32R = mybir.dt.float32r
BF16 = mybir.dt.bfloat16
I32 = mybir.dt.int32
U32 = mybir.dt.uint32
ALU = mybir.AluOpType
ACT = mybir.ActivationFunctionType
AX = mybir.AxisListType

P = 128
B, L, D = 4, 1024, 64
VOCAB = 4360
T = L // P
HALF = 512
C = L // HALF
TH = T // C
NH, NKV, HD = 4, 2, 16
NE, TOPK, HID = 8, 2, int(8 / 3 * D)
EH = NE * HID
MT = -(-EH // P)
E1, H1 = 32, 16
M1 = E1 * H1 // P
LN_EPS, RMS_EPS = 1e-5, 1e-6
NEG = -1e30

COLS = {}
_at = 0
for _name, _n in (("qk", 96), ("qk_swapped", 96), ("v", 32), ("router", NE), ("w1", EH), ("w3", EH),
                  ("q2", P), ("k2", P), ("v2", D), ("router2", E1), ("w1_2", E1 * H1)):
    COLS[_name] = (_at, _at + _n)
    _at += _n
WCOLS = _at
GROUP1 = (0, COLS["v"][1])
GROUP2 = (COLS["router"][0], COLS["w3"][1])
GROUP3 = (COLS["q2"][0], WCOLS)



def causal_tiles(width_of):
    out = []
    for blk in range(T):
        for c in range(C):
            w = width_of(blk, c)
            if w > 0:
                n = min(NH, HALF // w)
                n = {1: 1, 2: 2, 3: 2, 4: 4}[n]
                out += [(blk, c, w, tuple(range(h, h + n))) for h in range(0, NH, n)]
    return out


MAX_TILES = causal_tiles(lambda blk, c: min(HALF, P * (blk + 1) - HALF * c))
PROB_TILES = causal_tiles(lambda blk, c: min(HALF, HALF * (c + 1) - P * blk))
NMAX, NPROB = len(MAX_TILES), len(PROB_TILES)
NSELF = T * C

NRING = 8
NHID = 4
DVE_FRONT, DVE_BACK = 11, 21


def groups_of(tiles):
    keys = []
    for blk, c, _, _ in tiles:
        if (blk, c) not in keys:
            keys.append((blk, c))
    return [keys.index(tile[:2]) for tile in tiles]


MAX_GROUP, PROB_GROUP = groups_of(MAX_TILES), groups_of(PROB_TILES)


def parts(name, n):
    return ["%s.%d" % (name, k) for k in range(n)]


FRONT = ["emb", "x1", "x1T"] + parts("attn1", T + 1) + ["h1", "x2", "x2d", "x2T", "qk", "qkh", "qkl", "v"] \
    + parts("max", 12) + ["negm"] + parts("prob", 13) + ["y", "yT", "wo", "x3"]
BACK = ["x3T", "router", "top2", "weights", "rwT"] + parts("moe", MT + 1) + ["h2", "x4", "x4T", "q2", "v2", "k2"] \
    + parts("max3", T) + ["negm3"] + parts("attn3", T + 1) + ["h3", "x5", "x5T", "lg5", "othersT"] \
    + parts("ffn5", M1 + 1) + ["out", "store"]
TOGETHER = (
    ("emb", "attn1.8", "x3T", "rwT"),
    ("h1", "max.11", "moe.0", "x4T"),
    ("negm", "prob.12", "q2", "attn3.0"),
    ("y", "x3", "attn3.1", "store"),
)


def order_of_steps():
    order = []
    for f0, f1, b0, b1 in TOGETHER:
        front = [(k, "front") for k in FRONT[FRONT.index(f0):FRONT.index(f1) + 1]]
        back = [(k, "back") for k in BACK[BACK.index(b0):BACK.index(b1) + 1]]
        at_front = [((k + 0.5) / len(front), k, 0, step) for k, step in enumerate(front)]
        at_back = [((k + 0.5) / len(back), k, 1, step) for k, step in enumerate(back)]
        order += [step for _, _, _, step in sorted(at_front + at_back)]
    assert len(order) == len(FRONT) + len(BACK)
    return order


STEPS = order_of_steps()


def take_steps(front, back):
    halves = {"front": front, "back": back}
    coming = {k: next(h) for k, h in halves.items() if h is not None}
    for name, half in STEPS:
        while coming.get(half) == name:
            coming[half] = next(halves[half], None)
    assert not any(coming.values()), coming


def pipeline(eng, front, back):
    take_steps(front(0), None)
    with eng.Fori(1, B, 1) as i:
        take_steps(front(i), back((i, 1)))
    take_steps(None, back(B - 1))


def first(i):
    return isinstance(i, int) and i == 0


def at(eng, i, per, n):
    if isinstance(i, int):
        return i * per + n
    if isinstance(i, tuple):
        i, behind = i
        n -= behind * per
    if n == 0:
        eng.reg_alu(WAIT_REGISTER[eng.engine], i * per, 1, ALU.max)
    else:
        eng.reg_alu(WAIT_REGISTER[eng.engine], i * per, n, ALU.add)
    return WAIT_REGISTER[eng.engine]


WAIT_REGISTER = {}


def tower(nc, a, out):
    ctx = ExitStack()
    with ctx:
        def sb(name, shape, dt=F32):
            return ctx.enter_context(nc.sbuf_tensor(name, shape, dt))

        def ps(name, shape, dt=F32):
            return ctx.enter_context(nc.psum_tensor(name, shape, dt))

        ident = sb("ident", [P, P])
        ident16 = sb("ident16", [P, P], BF16)
        mask_qk = sb("mask_qk", [P, P], BF16)
        mask_kq = sb("mask_kq", [P, P], BF16)
        cos = sb("cos", [96, L])
        sin = sb("sin", [96, L])
        iota = sb("iota", [P, E1])
        spread = sb("spread", [40, MT * P], F32R)
        block16 = sb("block16", [E1, E1 * H1], BF16)
        lnw = sb("lnw", [P, 2])
        w_s = sb("w_s", [P, WCOLS], F32R)
        wo = sb("wo", [D, D])
        w2 = sb("w2", [P, MT, D])
        w2_2 = sb("w2_2", [P, M1, D])
        b1_2 = sb("b1_2", [P, M1])
        b2_2 = sb("b2_2", [E1, D])
        bq = sb("bq", [P, 1])
        bk = sb("bk", [P, 1])
        bv = sb("bv", [P, D])
        rb = sb("rb", [P, E1])
        minus_half = sb("minus_half", [P, T])

        negm_dram = nc.dram_tensor("negm_rows", (NH * T, P), F32, kind="Internal").ap()
        negm3_dram = nc.dram_tensor("negm3_rows", (T, P), F32, kind="Internal").ap()

        def wait_apart(eng, sem, count):
            eng.wait_ge(signal["filled"], 9)
            eng.wait_ge(sem, count)

        def weight(name, lo=0, n=None):
            c0, c1 = COLS[name]
            return w_s[:, c0 + lo:(c1 if n is None else c0 + lo + n)]

        idx = sb("idx", [P, T], I32)
        emb = sb("emb", [P, T, D])
        keep = sb("keep", [P, T])
        h0 = sb("h0", [P, T, D])
        stats = sb("stats", [P, T, 6])
        mv = sb("mv", [P, T, 2])
        veps = sb("veps", [P, T])
        rstd = sb("rstd", [P, T])
        xd = sb("xd", [P, T, 2, D])
        x1v = sb("x1v", [P, T, D + 1])
        hh = sb("hh", [P, L], F32R)
        ll = sb("ll", [P, L], F32R)
        aa = sb("aa", [P, L], F32R)
        prob = sb("prob", [P, NRING, HALF])
        rsum = sb("rsum", [P, T])
        h1 = sb("h1", [P, T, D])
        x2 = sb("x2", [P, T, D])
        sq = sb("sq", [P, T, D])
        att = sq
        ssum = sb("ssum", [P, T])
        rope_a = sb("rope_a", [96, 2, HALF])
        rope_b = sb("rope_b", [96, 2, HALF])
        qk = rope_a[:].rearrange("p c n -> p (c n)")
        qkh = sb("qkh", [96, L], F32R)
        qkl = sb("qkl", [96, L], F32R)
        qs = sb("qs", [P, NH, L], F32R)
        ks = sb("ks", [P, L], F32R)
        v1 = sb("v1", [P, T, NKV, 32])
        mx = sb("mx", [P, NH, T, C])
        mxt = sb("mxt", [P, NH, T])
        negm = sb("negm", [NH * T, P], F32R)
        ot = sb("ot", [P, L])
        rs4 = sb("rs4", [P, T, NH])
        y = sb("y", [P, T, D])
        yt = rope_b[0:D].rearrange("p c n -> p (c n)")
        x3 = sb("x3", [P, T, D])
        w_f = prob[:].rearrange("p r n -> p (r n)")[:, 0:WCOLS]
        res = sb("res", [P, T, D])
        x3d = sb("x3d", [P, T, 2, D])
        bhh = sb("bhh", [P, L], F32R)
        bll = sb("bll", [P, L], F32R)
        lg = sb("lg", [P, T, NE])
        lmax = sb("lmax", [P, T])
        ex = sb("ex", [P, T, NE])
        esum = sb("esum", [P, T])
        top8 = sb("top8", [P, T, 8])
        topi = sb("topi", [P, T, 8], U32)
        topf = sb("topf", [P, T, 2])
        oh_a = sb("oh_a", [P, T, NE])
        oh_b = sb("oh_b", [P, T, NE])
        wt = sb("wt", [40, L], F32R)
        sa = sb("sa", [P, 2, HALF])
        ub = sb("ub", [P, 2, HALF])
        hid = sb("hid", [P, NHID, HALF])
        spread_f = hid[0:40].rearrange("p r n -> p (r n)")[:, 0:MT * P]
        mt = sb("mt", [P, HALF])
        h2 = sb("h2", [P, T, D])
        bstats = sb("bstats", [P, T, 6])
        bmv = sb("bmv", [P, T, 2])
        bveps = sb("bveps", [P, T])
        brstd = sb("brstd", [P, T])
        bxd = sb("bxd", [P, T, 2, D])
        qh = sb("qh", [P, L], F32R)
        ql = sb("ql", [D + 1, L], F32R)
        ka = sb("ka", [P, L], F32R)
        k2 = sb("k2", [D + 1, L], F32R)
        v2 = sb("v2", [P, T, D + 1])
        bprob = hid
        mx3 = sb("mx3", [P, C, T])
        m3 = sb("m3", [P, T])
        negm3 = sb("negm3", [T, P], F32R)
        brsum = sb("brsum", [P, T])
        batt = sb("batt", [P, T, D])
        h3 = sb("h3", [P, T, D])
        lg5 = sb("lg5", [P, T, E1])
        top8b = sb("top8b", [P, T, 8])
        topib = sb("topib", [P, T, 8], U32)
        topfb = sb("topfb", [P, T])
        others = sb("others", [P, T, E1])
        otherst = sb("otherst", [E1, L], BF16)
        chosent = sa[0:E1].rearrange("p c n -> p (c n)")
        mt2 = mt
        h4 = sb("h4", [P, T, D])

        fw = ps("fw", [P, 2, HALF])
        fo = ps("fo", [P, 2, HALF])
        bw = ps("bw", [P, 2, HALF])
        bo = ps("bo", [P, 2, HALF])

        names = """const_loaded w1_loaded w2_loaded w_scaled w_high w_split w_ready filled v1_zeroed const_cast
            idx_loaded emb_gathered emb_used step_f step_b pool_step_f pool_step_b
            var1 rstd1 x1_ready x1T hh1 aa1 ll1 aal1 s1 e1 pv1 h1_ready
            var2 rstd2 ssq2 rrms2 x2_ready x2T hh2 ll2 qk_ps rope_used qk_ready qkh_ready qkl_ready
            v_ps v_ready spread_done sm max_used max_ready maxT negm_ready negm_stored negm_placed negm3_stored
            s2 e2 pv2 ot_ready otT y_ready yT yt_ready wo_ps x3_ready ssq3 rrms3 x3_done
            x3T hh3 ll3 lg_ps lmax_ready ex_ready rw_ready rwT wth_ready wt_ready
            moe_a moe_b moe_w silu ub_ready hid_ready w2_step moe_out mt_ready mtT h2_ready
            var4 rstd4 x4_ready x4T hh4 ll4 q_ps qh_ready ql_ready k_ps ka_ready k2_ready kal_ready
            v2_ps v2_ready sm3 max3_used m3_ready m3T negm3_ready negm3_placed
            s3 e3 pv3 h3_ready var5 rstd5 x5_ready x5T hh5 ll5 lg5_ps others_ready othersT
            otherst_ready chosent_ready s5 hid5_ready w5_step out5 mt5_ready mt5T h4_ready h4_free
            """.split()
        signal = {n: ctx.enter_context(nc.semaphore(n)) for n in names}

        def dup(ap):
            return ap.unsqueeze(2).to_broadcast([P, ap.shape[1], D])

        block = ctx.enter_context(nc.Block())

        @block.sync
        def _(sp):
            WAIT_REGISTER[sp.engine] = sp.alloc_register("wait_value")
            early = [(ident, a["ident"]), (lnw, a["lnw"]), (ident16, a["ident16"]), (mask_qk, a["mask_qk"]),
                     (mask_kq, a["mask_kq"]), (cos, a["cos"]), (sin, a["sin"]), (wo, a["wo"]), (iota, a["iota"]),
                     (spread_f, a["spread"]), (block16, a["block16"]), (w2_2, a["w2_2"]), (b1_2, a["b1_2"]),
                     (b2_2, a["b2_2"]), (bq, a["bq"]), (bk, a["bk"])]
            for dst, src in early:
                sp.dma_start(dst[:], src).then_inc(signal["const_loaded"], 16)
            sp.dma_start(bv[:], a["bv"].partition_broadcast(P)).then_inc(signal["const_loaded"], 16)
            sp.dma_start(rb[:], a["rb"].partition_broadcast(P)).then_inc(signal["const_loaded"], 16)
            for half in range(2):
                sp.dma_start(w_f[D * half:D * half + D, :], a["wcat"]).then_inc(signal["w1_loaded"], 16)
            sp.dma_start(w2[:, 0:MT - 1, :], a["w2"][0:(MT - 1) * P].rearrange("(m p) d -> p m d", p=P)) \
                .then_inc(signal["w2_loaded"], 16)
            sp.dma_start(w2[0:EH - (MT - 1) * P, MT - 1, :], a["w2"][(MT - 1) * P:EH]).then_inc(signal["w2_loaded"], 16)

            def front(i):
                yield "qkh"
                def spread_rows(dst, src):
                    sp.dma_start(dst.bitcast(F32), src.bitcast(F32)).then_inc(signal["spread_done"], 16)

                sp.wait_ge(signal["qkh_ready"], at(sp, i, C, C))
                for r in (0, 2):
                    for h in range(NH):
                        row = 32 * r + HD * (h // 2)
                        spread_rows(qs[row:row + HD, h, :], qkh[HD * h:HD * h + HD, :])
                for r in (0, 1):
                    spread_rows(ks[32 * r:32 * r + 32, :], qkh[64:96, :])
                yield "qkl"
                sp.wait_ge(signal["qkl_ready"], at(sp, i, C, C))
                spread_rows(ks[64:96, :], qkl[64:96, :])
                for h in range(NH):
                    row = 32 + HD * (h // 2)
                    spread_rows(qs[row:row + HD, h, :], qkl[HD * h:HD * h + HD, :])
                yield "negm"
                sp.wait_ge(signal["negm_ready"], at(sp, i, 1, 1))
                sp.dma_start(negm_dram, negm[:].bitcast(F32)).then_inc(signal["negm_stored"], 16)
                sp.wait_ge(signal["negm_stored"], at(sp, i, 16, 16))
                sp.dma_start(qs[96:97, :, :].bitcast(F32), negm_dram.rearrange("(o h t) n -> o h (t n)", o=1, h=NH)) \
                    .then_inc(signal["negm_placed"], 16)

            def back(i):
                yield "negm3"
                sp.wait_ge(signal["negm3_ready"], at(sp, i, 1, 1))
                sp.dma_start(negm3_dram, negm3[:].bitcast(F32)).then_inc(signal["negm3_stored"], 16)
                sp.wait_ge(signal["negm3_stored"], at(sp, i, 16, 16))
                sp.dma_start(ql[D:D + 1, :].bitcast(F32), negm3_dram.rearrange("(o t) n -> o (t n)", o=1)) \
                    .then_inc(signal["negm3_placed"], 16)
                yield "store"
                sp.wait_ge(signal["h4_ready"], at(sp, i, 1, 1))
                b = i[0] - i[1] if isinstance(i, tuple) else i
                sp.dma_start(out[bass.ds(b, 1)].rearrange("b (t p) d -> p (b t) d", p=P), h4[:]) \
                    .then_inc(signal["h4_free"], 16)

            pipeline(sp, front, back)
            sp.wait_ge(signal["h4_free"], at(sp, B, 16, 16))

        @block.gpsimd
        def _(pool):
            WAIT_REGISTER[pool.engine] = pool.alloc_register("wait_value")
            pool.memset(minus_half[:], -0.5).then_inc(signal["filled"], 1)
            pool.memset(x1v[:, :, D:D + 1], 1.0).then_inc(signal["filled"], 1)
            pool.memset(v2[:, :, D:D + 1], 1.0).then_inc(signal["filled"], 1)
            pool.memset(v1[:], 0.0).then_inc(signal["v1_zeroed"], 1)
            pool.wait_ge(signal["v1_zeroed"], 1)
            pool.memset(v1[:, :, :, HD:HD + 1], 1.0).then_inc(signal["filled"], 1)
            pool.memset(mx[:], -3e38).then_inc(signal["filled"], 1)
            pool.memset(wt[:].bitcast(F32), 0.0).then_inc(signal["filled"], 1)
            pool.memset(qs[:].bitcast(F32), 0.0).then_inc(signal["filled"], 1)

            def gather(b):
                pool.dma_start(idx[:], a["x"][bass.ds(b, 1)].rearrange("b p t -> p (b t)")) \
                    .then_inc(signal["idx_loaded"], 16)
                wait_apart(pool, signal["idx_loaded"], at(pool, b, 16, 16))
                for t in range(T):
                    pool.indirect_dma_start(emb[:, t, :], None, a["table"],
                                            bass.IndirectOffsetOnAxis(idx[:, t:t + 1], 0)) \
                        .then_inc(signal["emb_gathered"], 16)

            def power(i, step, n, ready, src, scale, eps, tmp, dst, done):
                wait_apart(pool, ready, at(pool, i, 1, 1))
                pool.tensor_scalar(tmp[:], src, scale, eps, ALU.mult, ALU.add).then_inc(step, 1)
                pool.wait_ge(step, at(pool, i, 4 if step is signal["pool_step_f"] else 2, n))
                pool.tensor_tensor(dst[:], tmp[:], minus_half[:], ALU.pow).then_inc(done, 1)

            def front(i):
                step = signal["pool_step_f"]
                yield "x1"
                power(i, step, 1, signal["var1"], mv[:, :, 1], 1.0, LN_EPS, veps, rstd, signal["rstd1"])
                yield "x2"
                power(i, step, 2, signal["var2"], mv[:, :, 1], 1.0, LN_EPS, veps, rstd, signal["rstd2"])
                yield "x2d"
                power(i, step, 3, signal["ssq2"], ssum[:], 1.0 / D, RMS_EPS, veps, rstd, signal["rrms2"])
                yield "x3"
                power(i, step, 4, signal["ssq3"], ssum[:], 1.0 / D, RMS_EPS, veps, rstd, signal["rrms3"])
                gather(i + 1)

            def back(i):
                step = signal["pool_step_b"]
                yield "x4"
                power(i, step, 1, signal["var4"], bmv[:, :, 1], 1.0, LN_EPS, bveps, brstd, signal["rstd4"])
                yield "x5"
                power(i, step, 2, signal["var5"], bmv[:, :, 1], 1.0, LN_EPS, bveps, brstd, signal["rstd5"])

            gather(0)
            pipeline(pool, front, back)
            pool.wait_ge(signal["emb_gathered"], at(pool, B + 1, 16 * T, 0))

        @block.scalar
        def _(act):
            WAIT_REGISTER[act.engine] = act.alloc_register("wait_value")
            def copy(dst, src):
                return act.activation(dst, src, ACT.Copy)

            def high(i, ready, psum, dst, done):
                for c in range(C):
                    act.wait_ge(ready, at(act, i, C, c + 1))
                    copy(dst[:, HALF * c:HALF * c + HALF], psum[:, c, :]).then_inc(done, 1)

            act.wait_ge(signal["const_loaded"], 16 * 18)
            copy(spread[:], spread_f).then_inc(signal["const_cast"], 1)
            def front(i):
                yield "x1T"
                for c in range(C):
                    half = slice(HALF * c, HALF * c + HALF)
                    act.wait_ge(signal["x1T"], at(act, i, C, c + 1))
                    copy(hh[:, half], fo[:, c, :]).then_inc(signal["hh1"], 1)
                    copy(aa[:, half], fo[:, c, :]).then_inc(signal["aa1"], 1)
                for u in range(NSELF):
                    yield "attn1.%d" % (u // 2)
                    act.wait_ge(signal["s1"], at(act, i, NSELF, u + 1))
                    if u >= 4:
                        act.wait_ge(signal["pv1"], at(act, i, NSELF, u - 3))
                    act.activation(prob[:, u % 4, :], fw[:, u % 2, :], ACT.Exp, scale=1.0 / 8).then_inc(signal["e1"], 1)
                yield "x2T"
                high(i, signal["x2T"], fo, hh, signal["hh2"])
                yield "qkh"
                for c in range(C):
                    act.wait_ge(signal["qk_ready"], at(act, i, C, c + 1))
                    copy(qkh[:, HALF * c:HALF * c + HALF], qk[:, HALF * c:HALF * c + HALF]).then_inc(signal["qkh_ready"], 1)
                yield "v"
                act.wait_ge(signal["v_ps"], at(act, i, 1, 1))
                copy(v1[:, :, :, 0:HD], fo[:, 0, 0:T * 32].rearrange("p (t g d) -> p t g d", t=T, g=NKV)) \
                    .then_inc(signal["v_ready"], 1)
                yield "negm"
                act.wait_ge(signal["maxT"], at(act, i, 1, 1))
                act.activation(negm[:], fo[0:NH * T, 1, 0:P], ACT.Copy, scale=-1.0).then_inc(signal["negm_ready"], 1)
                for u, (j, c, w, heads) in enumerate(PROB_TILES):
                    yield "prob.%d" % PROB_GROUP[u]
                    act.wait_ge(signal["s2"], at(act, i, NPROB, u + 1))
                    if u >= NRING:
                        act.wait_ge(signal["pv2"], at(act, i, NPROB, u - NRING + 1))
                    n = w * len(heads)
                    act.activation(prob[:, u % NRING, 0:n], fw[:, u % 2, 0:n], ACT.Exp, scale=0.25) \
                        .then_inc(signal["e2"], 1)
                yield "y"
                act.wait_ge(signal["pv2"], at(act, i, NPROB, NPROB))
                for c in range(C):
                    copy(ot[:, HALF * c:HALF * c + HALF], fo[:, c, :]).then_inc(signal["ot_ready"], 1)
                yield "yT"
                for c in range(C):
                    act.wait_ge(signal["yT"], at(act, i, C, c + 1))
                    copy(yt[:, HALF * c:HALF * c + HALF], fo[0:D, c, :]).then_inc(signal["yt_ready"], 1)

            def back(i):
                yield "x3T"
                high(i, signal["x3T"], bo, bhh, signal["hh3"])
                yield "router"
                act.wait_ge(signal["lmax_ready"], at(act, i, 1, 1))
                act.activation(ex[:], lg[:], ACT.Exp).then_inc(signal["ex_ready"], 1)
                yield "rwT"
                for c in range(C):
                    act.wait_ge(signal["rwT"], at(act, i, C, c + 1))
                    copy(wt[0:NE, HALF * c:HALF * c + HALF], bo[0:NE, c, :]).then_inc(signal["wth_ready"], 1)
                for u in range(MT * C):
                    m = u // C
                    yield "moe.%d" % m
                    n = min(P, EH - m * P)
                    act.wait_ge(signal["moe_a"], at(act, i, MT * C, u + 1))
                    if u >= 2:
                        act.wait_ge(signal["ub_ready"], at(act, i, MT * C, u - 1))
                    act.activation(sa[0:n, u % 2, :], bw[0:n, 0, :], ACT.Silu).then_inc(signal["silu"], 1)
                yield "h2"
                act.wait_ge(signal["w2_step"], at(act, i, MT, MT))
                copy(mt[:], bo[:, 1, :]).then_inc(signal["mt_ready"], 1)
                yield "x4T"
                high(i, signal["x4T"], bo, bhh, signal["hh4"])
                yield "q2"
                for c in range(C):
                    half = slice(HALF * c, HALF * c + HALF)
                    act.wait_ge(signal["q_ps"], at(act, i, C, c + 1))
                    act.activation(qh[:, half], bw[:, c, :], ACT.Identity, bias=bq[:, 0:1]).then_inc(signal["qh_ready"], 1)
                yield "k2"
                for c in range(C):
                    half = slice(HALF * c, HALF * c + HALF)
                    act.wait_ge(signal["k_ps"], at(act, i, C, c + 1))
                    act.activation(ka[:, half], bw[:, c, :], ACT.Identity, bias=bk[:, 0:1]).then_inc(signal["ka_ready"], 1)
                    act.activation(k2[0:D, half], bw[0:D, c, :], ACT.Identity, bias=bk[0:D, 0:1]) \
                        .then_inc(signal["k2_ready"], 1)
                yield "negm3"
                act.wait_ge(signal["m3T"], at(act, i, 1, 1))
                act.activation(negm3[:], bo[0:T, 1, 0:P], ACT.Copy, scale=-1.0).then_inc(signal["negm3_ready"], 1)
                for u in range(NSELF):
                    yield "attn3.%d" % (u // 2)
                    act.wait_ge(signal["s3"], at(act, i, NSELF, u + 1))
                    if u >= 4:
                        act.wait_ge(signal["pv3"], at(act, i, NSELF, u - 3))
                    act.activation(bprob[:, u % 4, :], bw[:, u % 2, :], ACT.Exp, scale=1.0 / 8).then_inc(signal["e3"], 1)
                yield "x5T"
                high(i, signal["x5T"], bo, bhh, signal["hh5"])
                yield "othersT"
                for c in range(C):
                    act.wait_ge(signal["othersT"], at(act, i, C, c + 1))
                    copy(otherst[:, HALF * c:HALF * c + HALF], bo[0:E1, c, :]).then_inc(signal["otherst_ready"], 1)
                for u in range(M1 * C):
                    yield "ffn5.%d" % (u // C)
                    act.wait_ge(signal["s5"], at(act, i, M1 * C, u + 1))
                    if u >= NHID:
                        act.wait_ge(signal["w5_step"], at(act, i, M1, (u - NHID) // C + 1))
                    act.activation(hid[:, u % NHID, :], bw[:, u % 2, :], ACT.Relu, bias=b1_2[:, u // C:u // C + 1]) \
                        .then_inc(signal["hid5_ready"], 1)
                yield "out"
                act.wait_ge(signal["w5_step"], at(act, i, M1, M1))
                act.activation(mt2[:], bo[:, 1, :], ACT.Relu).then_inc(signal["mt5_ready"], 1)

            pipeline(act, front, back)

        @block.vector
        def _(dve):
            WAIT_REGISTER[dve.engine] = dve.alloc_register("wait_value")
            dve.memset(ks[96:128, :].bitcast(F32), 1.0).then_inc(signal["filled"], 1)
            dve.memset(k2[D:D + 1, :].bitcast(F32), 1.0).then_inc(signal["filled"], 1)
            dve.memset(h4[:], 0.0).then_inc(signal["h4_free"], 16)
            dve.wait_ge(signal["const_loaded"], 16 * 18)
            dve.wait_ge(signal["w1_loaded"], 32)
            for k, (c0, c1) in enumerate((GROUP1, GROUP2)):
                dve.tensor_scalar(w_f[:, c0:c1], w_f[:, c0:c1], lnw[:, k:k + 1], None, ALU.mult).then_inc(signal["w_scaled"], 1)
            dve.wait_ge(signal["w_scaled"], 2)
            dve.tensor_copy(w_s[:], w_f[:]).then_inc(signal["w_high"], 1)
            dve.wait_ge(signal["w_high"], 1)
            dve.tensor_tensor(w_s[D:P, :], w_f[D:P, :], w_s[D:P, :].bitcast(F32), ALU.subtract).then_inc(signal["w_ready"], 1)
            dve.wait_ge(signal["filled"], 9)

            def low(i, ready, psum, high_of, dst, done, rows=slice(0, P)):
                for c in range(C):
                    half = slice(HALF * c, HALF * c + HALF)
                    dve.wait_ge(ready, at(dve, i, C, c + 1))
                    dve.tensor_tensor(dst[rows, half], psum[rows, c, :], high_of[rows, half].bitcast(F32),
                                      ALU.subtract).then_inc(done, 1)

            count = {}

            def link(ins, i, which="f", apart=False):
                count[which] += 1
                sem, per = (signal["step_f"], DVE_FRONT) if which == "f" else (signal["step_b"], DVE_BACK)
                ins.then_inc(sem, 1)
                if apart:
                    wait_apart(dve, sem, at(dve, i, per, count[which]))
                else:
                    dve.wait_ge(sem, at(dve, i, per, count[which]))

            def moments(i, src, st, m, which):
                for t in range(T):
                    ins = dve.bn_stats(st[:, t, :], src[:, t, :])
                link(ins, i, which, apart=True)
                for t in range(T):
                    ins = dve.bn_aggr(m[:, t, :], st[:, t, :])
                return ins

            def front(i):
                count["f"] = 0
                yield "emb"
                dve.wait_ge(signal["emb_gathered"], at(dve, i, 16 * T, 16 * T))
                link(dve.tensor_scalar(keep[:], idx[:], 0, None, ALU.not_equal), i)
                dve.tensor_tensor(h0[:], emb[:], dup(keep[:]), ALU.mult).then_inc(signal["emb_used"], 1)
                dve.wait_ge(signal["emb_used"], at(dve, i, 1, 1))
                moments(i, h0, stats, mv, "f").then_inc(signal["var1"], 1)
                yield "x1"
                dve.wait_ge(signal["rstd1"], at(dve, i, 1, 1))
                for t in range(T):
                    dve.tensor_scalar(xd[:, t, :, :], h0[:, t, :].unsqueeze(1).to_broadcast([P, 2, D]), mv[:, t, 0:1],
                                      rstd[:, t:t + 1], ALU.subtract, ALU.mult).then_inc(signal["x1_ready"], 1)
                dve.wait_ge(signal["x1_ready"], at(dve, i, T + 1, T))
                dve.tensor_copy(x1v[:, :, 0:D], xd[:, :, 0, :]).then_inc(signal["x1_ready"], 1)
                yield "x1T"
                for c in range(C):
                    half = slice(HALF * c, HALF * c + HALF)
                    dve.wait_ge(signal["hh1"], at(dve, i, C, c + 1))
                    dve.wait_ge(signal["aa1"], at(dve, i, C, c + 1))
                    dve.tensor_tensor(ll[:, half], fo[:, c, :], hh[:, half].bitcast(F32), ALU.subtract) \
                        .then_inc(signal["ll1"], 1)
                    dve.tensor_tensor(aa[D:P, half], fo[D:P, c, :], aa[D:P, half].bitcast(F32), ALU.subtract) \
                        .then_inc(signal["aal1"], 1)
                yield "h1"
                dve.wait_ge(signal["pv1"], at(dve, i, NSELF, NSELF))
                acc = fo[:, :, 0:TH * (D + 1)].rearrange("p c (t d) -> p c t d", t=TH)
                link(dve.reciprocal(rsum[:].rearrange("p (c t) -> p c t", c=C), acc[:, :, :, D]), i)
                for c in range(C):
                    ins = dve.tensor_tensor(att[:, TH * c:TH * c + TH, :], acc[:, c, :, 0:D],
                                            dup(rsum[:, TH * c:TH * c + TH]), ALU.mult)
                link(ins, i)
                dve.tensor_tensor(h1[:], att[:], h0[:], ALU.add).then_inc(signal["h1_ready"], 1)
                dve.wait_ge(signal["h1_ready"], at(dve, i, 1, 1))
                moments(i, h1, stats, mv, "f").then_inc(signal["var2"], 1)
                yield "x2"
                dve.wait_ge(signal["rstd2"], at(dve, i, 1, 1))
                for t in range(T):
                    ins = dve.tensor_scalar(x2[:, t, :], h1[:, t, :], mv[:, t, 0:1], rstd[:, t:t + 1],
                                            ALU.subtract, ALU.mult)
                link(ins, i)

                def squares(src, ssq):
                    link(dve.tensor_tensor(sq[:], src[:], src[:], ALU.mult), i)
                    dve.tensor_reduce(ssum[:], sq[:], AX.X, ALU.add).then_inc(ssq, 1)

                def rms(src, rrms, dst, done):
                    dve.wait_ge(rrms, at(dve, i, 1, 1))
                    for r in range(2):
                        ins = dve.tensor_tensor(dst[:, :, r, :], src[:], dup(rstd[:]), ALU.mult)
                    ins.then_inc(done, 1)

                squares(x2, signal["ssq2"])
                yield "x2d"
                rms(x2, signal["rrms2"], xd, signal["x2_ready"])
                yield "x2T"
                low(i, signal["hh2"], fo, hh, ll, signal["ll2"])
                yield "qk"
                for c in range(C):
                    half = slice(HALF * c, HALF * c + HALF)
                    dve.wait_ge(signal["qk_ps"], at(dve, i, C, c + 1))
                    dve.tensor_tensor(rope_a[:, c, :], fw[0:96, 0, :], cos[:, half], ALU.mult).then_inc(signal["rope_used"], 1)
                    dve.tensor_tensor(rope_b[:, c, :], fw[0:96, 1, :], sin[:, half], ALU.mult).then_inc(signal["rope_used"], 1)
                    dve.wait_ge(signal["rope_used"], at(dve, i, 2 * C, 2 * c + 2))
                    dve.tensor_tensor(qk[:, half], rope_a[:, c, :], rope_b[:, c, :], ALU.add).then_inc(signal["qk_ready"], 1)
                yield "qkl"
                for c in range(C):
                    half = slice(HALF * c, HALF * c + HALF)
                    dve.wait_ge(signal["qkh_ready"], at(dve, i, C, c + 1))
                    dve.tensor_tensor(qkl[:, half], qk[:, half], qkh[:, half].bitcast(F32), ALU.subtract) \
                        .then_inc(signal["qkl_ready"], 1)
                for u, (j, c, w, heads) in enumerate(MAX_TILES):
                    yield "max.%d" % MAX_GROUP[u]
                    dve.wait_ge(signal["sm"], at(dve, i, NMAX, u + 1))
                    n = len(heads)
                    dve.tensor_reduce(mx[:, heads[0]:heads[0] + n, j, c],
                                      fw[:, u % 2, 0:n * w].rearrange("p (h w) -> p h w", h=n),
                                      AX.X, ALU.max).then_inc(signal["max_used"], 1)
                yield "negm"
                dve.wait_ge(signal["max_used"], at(dve, i, NMAX, NMAX))
                dve.tensor_reduce(mxt[:], mx[:], AX.X, ALU.max).then_inc(signal["max_ready"], 1)
                yield "y"
                dve.wait_ge(signal["otT"], at(dve, i, C, C))
                for c in range(C):
                    o4 = fo[:, c, :].rearrange("p (t h d) -> p t h d", t=TH, h=NH)
                    link(dve.reciprocal(rs4[:, TH * c:TH * c + TH, :], o4[:, :, :, HD]), i)
                    dve.tensor_tensor(y[:, TH * c:TH * c + TH, :].rearrange("p t (h d) -> p t h d", h=NH),
                                      o4[:, :, :, 0:HD],
                                      rs4[:, TH * c:TH * c + TH, :].unsqueeze(3).to_broadcast([P, TH, NH, HD]),
                                      ALU.mult).then_inc(signal["y_ready"], 1)
                yield "wo"
                dve.wait_ge(signal["wo_ps"], at(dve, i, 1, 1))
                link(dve.tensor_tensor(x3[:], fw[:, 0, :].rearrange("p (t d) -> p t d", t=T), x2[:], ALU.add), i)
                if not first(i):
                    dve.wait_ge(signal["h2_ready"], at(dve, i, 1, 0))
                dve.tensor_tensor(res[:], x3[:], h1[:], ALU.add).then_inc(signal["x3_ready"], 1)
                squares(x3, signal["ssq3"])
                yield "x3"
                if not first(i):
                    dve.wait_ge(signal["x3T"], at(dve, i, C, 0))
                rms(x3, signal["rrms3"], x3d, signal["x3_done"])
                assert count["f"] == DVE_FRONT, count

            def back(i):
                count["b"] = 0
                yield "x3T"
                low(i, signal["hh3"], bo, bhh, bll, signal["ll3"])
                yield "router"
                dve.wait_ge(signal["lg_ps"], at(dve, i, 1, 1))
                lg_ps = bw[:, 0, 0:T * NE].rearrange("p (t e) -> p t e", t=T)
                link(dve.tensor_reduce(lmax[:], lg_ps, AX.X, ALU.max), i, "b")
                dve.tensor_tensor(lg[:], lg_ps, lmax[:].unsqueeze(2).to_broadcast([P, T, NE]), ALU.subtract) \
                    .then_inc(signal["lmax_ready"], 1)
                wait_apart(dve, signal["lmax_ready"], at(dve, i, 1, 1))
                yield "top2"
                for t in range(T):
                    ins = dve.max(top8[:, t, :], lg[:, t, :])
                link(ins, i, "b", apart=True)
                for t in range(T):
                    ins = dve.max_index(topi[:, t, :], top8[:, t, :], lg[:, t, :])
                link(ins, i, "b")
                link(dve.tensor_copy(topf[:], topi[:, :, 0:2]), i, "b")
                experts = iota[:, 0:NE].unsqueeze(1).to_broadcast([P, T, NE])
                dve.tensor_tensor(oh_a[:], experts, topf[:, :, 0:1].to_broadcast([P, T, NE]), ALU.is_equal)
                link(dve.tensor_tensor(oh_b[:], experts, topf[:, :, 1:2].to_broadcast([P, T, NE]), ALU.is_equal), i, "b")
                link(dve.tensor_tensor(oh_a[:], oh_a[:], oh_b[:], ALU.add), i, "b")
                yield "weights"
                dve.wait_ge(signal["ex_ready"], at(dve, i, 1, 1))
                link(dve.tensor_reduce(esum[:], ex[:], AX.X, ALU.add), i, "b")
                link(dve.reciprocal(esum[:], esum[:]), i, "b")
                link(dve.tensor_tensor(ex[:], ex[:], esum[:].unsqueeze(2).to_broadcast([P, T, NE]), ALU.mult), i, "b")
                link(dve.tensor_tensor(ex[:], ex[:], oh_a[:], ALU.mult), i, "b")
                link(dve.tensor_reduce(esum[:], ex[:], AX.X, ALU.add), i, "b")
                link(dve.tensor_scalar(esum[:], esum[:], 1e-9, None, ALU.add), i, "b")
                link(dve.reciprocal(esum[:], esum[:]), i, "b")
                dve.tensor_tensor(ex[:], ex[:], esum[:].unsqueeze(2).to_broadcast([P, T, NE]), ALU.mult) \
                    .then_inc(signal["rw_ready"], 1)
                yield "rwT"
                for c in range(C):
                    half = slice(HALF * c, HALF * c + HALF)
                    dve.wait_ge(signal["wth_ready"], at(dve, i, C, c + 1))
                    dve.tensor_tensor(wt[32:32 + NE, half], bo[0:NE, c, :], wt[0:NE, half].bitcast(F32), ALU.subtract) \
                        .then_inc(signal["wt_ready"], 1)
                for u in range(MT * C):
                    n = min(P, EH - u // C * P)
                    yield "moe.%d" % (u // C)
                    dve.wait_ge(signal["silu"], at(dve, i, MT * C, u + 1))
                    dve.wait_ge(signal["moe_b"], at(dve, i, MT * C, u + 1))
                    dve.tensor_tensor(ub[0:n, u % 2, :], sa[0:n, u % 2, :], bw[0:n, 1, :], ALU.mult) \
                        .then_inc(signal["ub_ready"], 1)
                    dve.wait_ge(signal["ub_ready"], at(dve, i, MT * C, u + 1))
                    dve.wait_ge(signal["moe_w"], at(dve, i, MT * C, u + 1))
                    if u >= NHID:
                        dve.wait_ge(signal["w2_step"], at(dve, i, MT, (u - NHID) // C + 1))
                    dve.tensor_tensor(hid[0:n, u % NHID, :], ub[0:n, u % 2, :], bo[0:n, 0, :], ALU.mult) \
                        .then_inc(signal["hid_ready"], 1)
                yield "h2"
                dve.wait_ge(signal["mtT"], at(dve, i, 1, 1))

                def by_half(x):
                    return x.rearrange("p (c t) d -> p t c d", c=C)

                dve.tensor_tensor(by_half(h2[:]), bw[:, 0, :].rearrange("p (t c d) -> p t c d", t=TH, c=C),
                                  by_half(res[:]), ALU.add).then_inc(signal["h2_ready"], 1)
                dve.wait_ge(signal["h2_ready"], at(dve, i, 1, 1))

                def norm_back(src, rstd_done, done):
                    dve.wait_ge(rstd_done, at(dve, i, 1, 1))
                    for t in range(T):
                        ins = dve.tensor_scalar(bxd[:, t, :, :], src[:, t, :].unsqueeze(1).to_broadcast([P, 2, D]),
                                                bmv[:, t, 0:1], brstd[:, t:t + 1], ALU.subtract, ALU.mult)
                    ins.then_inc(done, 1)

                moments(i, h2, bstats, bmv, "b").then_inc(signal["var4"], 1)
                yield "x4"
                norm_back(h2, signal["rstd4"], signal["x4_ready"])
                yield "x4T"
                low(i, signal["hh4"], bo, bhh, bll, signal["ll4"])
                yield "q2"
                for c in range(C):
                    half = slice(HALF * c, HALF * c + HALF)
                    dve.wait_ge(signal["qh_ready"], at(dve, i, C, c + 1))
                    dve.scalar_tensor_tensor(out=ql[0:D, half], in0=bw[0:D, c, :], scalar=bq[0:D, 0:1],
                                             in1=qh[0:D, half].bitcast(F32), op0=ALU.add, op1=ALU.subtract) \
                        .then_inc(signal["ql_ready"], 1)
                yield "k2"
                for c in range(C):
                    half = slice(HALF * c, HALF * c + HALF)
                    dve.wait_ge(signal["ka_ready"], at(dve, i, C, c + 1))
                    dve.wait_ge(signal["k2_ready"], at(dve, i, C, c + 1))
                    dve.scalar_tensor_tensor(out=ka[D:P, half], in0=bw[D:P, c, :], scalar=bk[D:P, 0:1],
                                             in1=ka[D:P, half].bitcast(F32), op0=ALU.add, op1=ALU.subtract) \
                        .then_inc(signal["kal_ready"], 1)
                dve.wait_ge(signal["v2_ps"], at(dve, i, 1, 1))
                dve.tensor_tensor(v2[:, :, 0:D], bo[:, 0, :].rearrange("p (t d) -> p t d", t=T),
                                  bv[:].unsqueeze(1).to_broadcast([P, T, D]), ALU.add).then_inc(signal["v2_ready"], 1)
                for u in range(NSELF):
                    yield "max3.%d" % (u // 2)
                    dve.wait_ge(signal["sm3"], at(dve, i, NSELF, u + 1))
                    dve.tensor_reduce(mx3[:, u % C, u // C:u // C + 1], bw[:, u % 2, :], AX.X, ALU.max) \
                        .then_inc(signal["max3_used"], 1)
                yield "negm3"
                dve.wait_ge(signal["max3_used"], at(dve, i, NSELF, NSELF))
                dve.tensor_tensor(m3[:], mx3[:, 0, :], mx3[:, 1, :], ALU.max).then_inc(signal["m3_ready"], 1)
                yield "h3"
                dve.wait_ge(signal["pv3"], at(dve, i, NSELF, NSELF))
                bacc = bo[:, :, 0:TH * (D + 1)].rearrange("p c (t d) -> p c t d", t=TH)
                link(dve.reciprocal(brsum[:].rearrange("p (c t) -> p c t", c=C), bacc[:, :, :, D]), i, "b")
                for c in range(C):
                    ins = dve.tensor_tensor(batt[:, TH * c:TH * c + TH, :], bacc[:, c, :, 0:D],
                                            dup(brsum[:, TH * c:TH * c + TH]), ALU.mult)
                link(ins, i, "b")
                dve.tensor_tensor(h3[:], batt[:], h2[:], ALU.add).then_inc(signal["h3_ready"], 1)
                dve.wait_ge(signal["h3_ready"], at(dve, i, 1, 1))
                moments(i, h3, bstats, bmv, "b").then_inc(signal["var5"], 1)
                yield "x5"
                norm_back(h3, signal["rstd5"], signal["x5_ready"])
                yield "x5T"
                low(i, signal["hh5"], bo, bhh, bll, signal["ll5"])
                yield "lg5"
                dve.wait_ge(signal["lg5_ps"], at(dve, i, 1, 1))
                link(dve.tensor_tensor(lg5[:], bw[:, 0, 0:T * E1].rearrange("p (t e) -> p t e", t=T),
                                       rb[:].unsqueeze(1).to_broadcast([P, T, E1]), ALU.add), i, "b", apart=True)
                for t in range(T):
                    ins = dve.max(top8b[:, t, :], lg5[:, t, :])
                link(ins, i, "b", apart=True)
                for t in range(T):
                    ins = dve.max_index(topib[:, t, :], top8b[:, t, :], lg5[:, t, :])
                link(ins, i, "b")
                link(dve.tensor_copy(topfb[:], topib[:, :, 0]), i, "b")
                dve.tensor_tensor(others[:], iota[:].unsqueeze(1).to_broadcast([P, T, E1]),
                                  topfb[:].unsqueeze(2).to_broadcast([P, T, E1]), ALU.not_equal) \
                    .then_inc(signal["others_ready"], 1)
                yield "othersT"
                for c in range(C):
                    dve.wait_ge(signal["otherst_ready"], at(dve, i, C, c + 1))
                    dve.tensor_scalar(chosent[:, HALF * c:HALF * c + HALF], bo[0:E1, c, :], -1.0, 1.0,
                                      ALU.mult, ALU.add).then_inc(signal["chosent_ready"], 1)
                yield "out"
                dve.wait_ge(signal["h4_free"], at(dve, i, 16, 16))
                dve.wait_ge(signal["mt5T"], at(dve, i, 1, 1))
                dve.tensor_tensor(by_half(h4[:]), bw[:, 0, :].rearrange("p (t c d) -> p t c d", t=TH, c=C),
                                  by_half(h3[:]), ALU.add).then_inc(signal["h4_ready"], 1)
                assert count["b"] == DVE_BACK, count

            pipeline(dve, front, back)

        @block.tensor
        def _(pe):
            WAIT_REGISTER[pe.engine] = pe.alloc_register("wait_value")
            pe.wait_ge(signal["w_ready"], 1)
            pe.wait_ge(signal["const_cast"], 1)
            pe.wait_ge(signal["w2_loaded"], 32)
            pe.wait_ge(signal["filled"], 9)

            def transposes(src, psum, done):
                for t in range(T):
                    ins = pe.transpose(psum[:, t // TH, P * (t % TH):P * (t % TH) + P],
                                       src[:, t, :, :].rearrange("p r d -> p (r d)"), ident[:])
                    if t % TH == TH - 1:
                        ins.then_inc(done, 1)

            def project(dst, w, h, l, c):
                half = slice(HALF * c, HALF * c + HALF)
                pe.matmul(dst, w, h[:, half], start=True, stop=False)
                return pe.matmul(dst, w, l[:, half], start=False, stop=True)

            def project_rows(dst, w, h, l, t):
                pe.matmul(dst, h[:, P * t:P * t + P], w, start=True, stop=False)
                return pe.matmul(dst, l[:, P * t:P * t + P], w, start=False, stop=True)

            def weigh(psum, pr, values, u):
                j, c = u // C, u % C
                for t in range(TH):
                    ins = pe.matmul(psum[:, c, (D + 1) * t:(D + 1) * (t + 1)], pr[:, u % 4, P * t:P * t + P],
                                    values[:, j, :], start=(j == 0 and t == 0), stop=(j == T - 1),
                                    skip_group_check=True)
                return ins

            def back_rows(src, psum):
                for t in range(TH):
                    ins = pe.transpose(psum[:, P * t:P * t + P], src[:, P * t:P * t + P], ident[:])
                return ins

            def front(i):
                yield "x1T"
                pe.wait_ge(signal["x1_ready"], at(pe, i, T + 1, T + 1))
                transposes(xd, fo, signal["x1T"])

                def scores1(u):
                    j, c = u // C, u % C
                    if u < C:
                        pe.wait_ge(signal["ll1"], at(pe, i, C, c + 1))
                        pe.wait_ge(signal["aal1"], at(pe, i, C, c + 1))
                    if u >= 2:
                        pe.wait_ge(signal["e1"], at(pe, i, NSELF, u - 1))
                    project(fw[:, u % 2, :], aa[:, P * j:P * j + P], hh, ll, c).then_inc(signal["s1"], 1)

                for u in range(NSELF + 2):
                    yield "attn1.%d" % (u // 2)
                    if u < NSELF:
                        scores1(u)
                    if u >= 2:
                        pe.wait_ge(signal["e1"], at(pe, i, NSELF, u - 1))
                        weigh(fo, prob, x1v, u - 2).then_inc(signal["pv1"], 1)
                yield "x2T"
                pe.wait_ge(signal["x2_ready"], at(pe, i, 1, 1))
                transposes(xd, fo, signal["x2T"])
                yield "qk"
                for c in range(C):
                    pe.wait_ge(signal["ll2"], at(pe, i, C, c + 1))
                    if c:
                        pe.wait_ge(signal["rope_used"], at(pe, i, 2 * C, 2 * c))
                    project(fw[0:96, 0, :], weight("qk"), hh, ll, c)
                    project(fw[0:96, 1, :], weight("qk_swapped"), hh, ll, c).then_inc(signal["qk_ps"], 1)
                yield "v"
                for t in range(T):
                    ins = project_rows(fo[:, 0, 32 * t:32 * t + 32], weight("v"), hh, ll, t)
                ins.then_inc(signal["v_ps"], 1)
                yield "max.0"
                pe.wait_ge(signal["spread_done"], at(pe, i, 16 * 15, 16 * 15))
                for u, (j, c, w, heads) in enumerate(MAX_TILES):
                    yield "max.%d" % MAX_GROUP[u]
                    if u < 2:
                        pe.wait_ge(signal["rope_used"], at(pe, i, 2 * C, 2 * C))
                    else:
                        pe.wait_ge(signal["max_used"], at(pe, i, NMAX, u - 1))
                    diagonal = HALF * c + w == P * (j + 1)
                    for n, h in enumerate(heads):
                        dst = fw[:, u % 2, n * w:n * w + w]
                        if diagonal:
                            pe.matmul(dst[:, w - P:w], ident16[:], mask_qk[:], start=True, stop=False,
                                      skip_group_check=True)
                        ins = pe.matmul(dst, qs[0:96, h, P * j:P * j + P], ks[0:96, HALF * c:HALF * c + w],
                                        start=not diagonal, stop=True, skip_group_check=True)
                    ins.then_inc(signal["sm"], 1)
                yield "negm"
                pe.wait_ge(signal["max_ready"], at(pe, i, 1, 1))
                pe.wait_ge(signal["hh2"], at(pe, i, C, C))
                pe.transpose(fo[0:NH * T, 1, 0:P], mxt[:].rearrange("p h t -> p (h t)"), ident[:]).then_inc(signal["maxT"], 1)
                yield "prob.0"
                pe.wait_ge(signal["negm_placed"], at(pe, i, 16, 16))
                pe.wait_ge(signal["v_ready"], at(pe, i, 1, 1))

                def scores2(u):
                    j, c, w, heads = PROB_TILES[u]
                    if u >= 2:
                        pe.wait_ge(signal["e2"], at(pe, i, NPROB, u - 1))
                    q0 = HALF * (c + 1) - w
                    diagonal = q0 == P * j
                    for n, h in enumerate(heads):
                        dst = fw[:, u % 2, n * w:n * w + w]
                        if diagonal:
                            pe.matmul(dst[:, 0:P], ident16[:], mask_kq[:], start=True, stop=False,
                                      skip_group_check=True)
                        ins = pe.matmul(dst, ks[0:97, P * j:P * j + P], qs[0:97, h, q0:q0 + w],
                                        start=not diagonal, stop=True, skip_group_check=True)
                    ins.then_inc(signal["s2"], 1)

                def weigh2(u):
                    j, c, w, heads = PROB_TILES[u]
                    pe.wait_ge(signal["e2"], at(pe, i, NPROB, u + 1))
                    for n, h in enumerate(heads):
                        ins = pe.matmul(fo[32 * h:32 * h + 32, c, HALF - w:HALF], v1[:, j, h // 2, :],
                                        prob[:, u % NRING, n * w:n * w + w], start=(j == 0),
                                        stop=(j == TH * (c + 1) - 1), skip_group_check=True,
                                        tile_position=(0, 32 * h))
                    ins.then_inc(signal["pv2"], 1)

                groups = {}
                for u, (j, c, w, heads) in enumerate(PROB_TILES):
                    groups.setdefault((j, c), []).append(u)
                groups = list(groups.values())
                for g in range(len(groups) + 1):
                    yield "prob.%d" % g
                    if g < len(groups):
                        for u in groups[g]:
                            scores2(u)
                    if g >= 1:
                        for u in groups[g - 1]:
                            weigh2(u)
                yield "y"
                pe.wait_ge(signal["ot_ready"], at(pe, i, C, C))
                for t in range(T):
                    ins = pe.transpose(fo[:, t // TH, P * (t % TH):P * (t % TH) + P], ot[:, P * t:P * t + P], ident[:])
                    if t % TH == TH - 1:
                        ins.then_inc(signal["otT"], 1)
                yield "yT"
                for t in range(T):
                    if t % TH == 0:
                        wait_apart(pe, signal["y_ready"], at(pe, i, C, t // TH + 1))
                    ins = pe.transpose(fo[0:D, t // TH, P * (t % TH):P * (t % TH) + P], y[:, t, :], ident[:])
                    if t % TH == TH - 1:
                        ins.then_inc(signal["yT"], 1)
                yield "wo"
                for t in range(T):
                    if t % TH == 0:
                        pe.wait_ge(signal["yt_ready"], at(pe, i, C, t // TH + 1))
                    ins = pe.matmul(fw[:, 0, D * t:D * t + D], yt[:, P * t:P * t + P], wo[:], start=True, stop=True)
                ins.then_inc(signal["wo_ps"], 1)

            def back(i):
                yield "x3T"
                pe.wait_ge(signal["x3_done"], at(pe, i, 1, 1))
                transposes(x3d, bo, signal["x3T"])
                yield "router"
                pe.wait_ge(signal["ll3"], at(pe, i, C, C))
                for t in range(T):
                    ins = project_rows(bw[:, 0, NE * t:NE * t + NE], weight("router"), bhh, bll, t)
                ins.then_inc(signal["lg_ps"], 1)
                yield "rwT"
                pe.wait_ge(signal["rw_ready"], at(pe, i, 1, 1))
                for t in range(T):
                    ins = pe.transpose(bo[0:NE, t // TH, P * (t % TH):P * (t % TH) + P], ex[:, t, :], ident[:])
                    if t % TH == TH - 1:
                        ins.then_inc(signal["rwT"], 1)
                yield "moe.0"
                pe.wait_ge(signal["wt_ready"], at(pe, i, C, C))

                def experts_out(m):
                    pe.wait_ge(signal["hid_ready"], at(pe, i, MT * C, C * m + C))
                    n = min(P, EH - m * P)
                    for c in range(C):
                        ins = pe.matmul(bo[D * c:D * c + D, 1, :], w2[0:n, m, :], hid[0:n, (C * m + c) % NHID, :],
                                        start=(m == 0), stop=(m == MT - 1), skip_group_check=True,
                                        tile_position=(0, D * c))
                    ins.then_inc(signal["w2_step"], 1)
                    return ins

                for u in range(MT * C):
                    m, c = u // C, u % C
                    yield "moe.%d" % m
                    n = min(P, EH - m * P)
                    if u >= 1:
                        pe.wait_ge(signal["silu"], at(pe, i, MT * C, u))
                    project(bw[0:n, 0, :], weight("w1", P * m, n), bhh, bll, c).then_inc(signal["moe_a"], 1)
                    if u >= 1:
                        pe.wait_ge(signal["ub_ready"], at(pe, i, MT * C, u))
                    project(bw[0:n, 1, :], weight("w3", P * m, n), bhh, bll, c).then_inc(signal["moe_b"], 1)
                    if u >= 1:
                        pe.wait_ge(signal["hid_ready"], at(pe, i, MT * C, u))
                    pe.matmul(bo[0:n, 0, :], spread[:, P * m:P * m + n], wt[:, HALF * c:HALF * c + HALF],
                              start=True, stop=True).then_inc(signal["moe_w"], 1)
                    if c == 0 and m >= 1:
                        experts_out(m - 1)
                yield "moe.%d" % MT
                pe.wait_ge(signal["hid_ready"], at(pe, i, MT * C, MT * C))
                experts_out(MT - 1)
                yield "h2"
                pe.wait_ge(signal["mt_ready"], at(pe, i, 1, 1))
                back_rows(mt, bw[:, 0, :]).then_inc(signal["mtT"], 1)
                yield "x4T"
                pe.wait_ge(signal["x4_ready"], at(pe, i, 1, 1))
                transposes(bxd, bo, signal["x4T"])
                yield "q2"
                pe.wait_ge(signal["h2_ready"], at(pe, i, 1, 1))
                for c in range(C):
                    pe.wait_ge(signal["ll4"], at(pe, i, C, c + 1))
                    project(bw[:, c, :], weight("q2"), bhh, bll, c).then_inc(signal["q_ps"], 1)
                yield "v2"
                for t in range(T):
                    ins = project_rows(bo[:, 0, D * t:D * t + D], weight("v2"), bhh, bll, t)
                ins.then_inc(signal["v2_ps"], 1)
                yield "k2"
                for c in range(C):
                    pe.wait_ge(signal["ql_ready"], at(pe, i, C, c + 1))
                    project(bw[:, c, :], weight("k2"), bhh, bll, c).then_inc(signal["k_ps"], 1)
                for u in range(NSELF):
                    j, c = u // C, u % C
                    yield "max3.%d" % (u // 2)
                    if u < 2:
                        pe.wait_ge(signal["kal_ready"], at(pe, i, C, c + 1))
                        pe.wait_ge(signal["k2_ready"], at(pe, i, C, c + 1))
                    else:
                        pe.wait_ge(signal["max3_used"], at(pe, i, NSELF, u - 1))
                    pe.matmul(bw[:, u % 2, :], qh[:, P * j:P * j + P], ka[:, HALF * c:HALF * c + HALF],
                              start=True, stop=True).then_inc(signal["sm3"], 1)
                yield "negm3"
                pe.wait_ge(signal["m3_ready"], at(pe, i, 1, 1))
                pe.transpose(bo[0:T, 1, 0:P], m3[:], ident[:]).then_inc(signal["m3T"], 1)
                yield "attn3.0"
                pe.wait_ge(signal["negm3_placed"], at(pe, i, 16, 16))
                pe.wait_ge(signal["v2_ready"], at(pe, i, 1, 1))

                def scores3(u):
                    j, c = u // C, u % C
                    half = slice(HALF * c, HALF * c + HALF)
                    if u >= 2:
                        pe.wait_ge(signal["e3"], at(pe, i, NSELF, u - 1))
                    pe.matmul(bw[:, u % 2, :], ka[:, P * j:P * j + P], qh[:, half], start=True, stop=False)
                    pe.matmul(bw[:, u % 2, :], k2[:, P * j:P * j + P], ql[:, half], start=False, stop=True) \
                        .then_inc(signal["s3"], 1)

                for u in range(NSELF + 2):
                    yield "attn3.%d" % (u // 2)
                    if u < NSELF:
                        scores3(u)
                    if u >= 2:
                        pe.wait_ge(signal["e3"], at(pe, i, NSELF, u - 1))
                        weigh(bo, bprob, v2, u - 2).then_inc(signal["pv3"], 1)
                yield "x5T"
                pe.wait_ge(signal["x5_ready"], at(pe, i, 1, 1))
                transposes(bxd, bo, signal["x5T"])
                yield "lg5"
                pe.wait_ge(signal["ll5"], at(pe, i, C, C))
                for t in range(T):
                    ins = project_rows(bw[:, 0, E1 * t:E1 * t + E1], weight("router2"), bhh, bll, t)
                ins.then_inc(signal["lg5_ps"], 1)
                yield "othersT"
                pe.wait_ge(signal["others_ready"], at(pe, i, 1, 1))
                for t in range(T):
                    ins = pe.transpose(bo[0:E1, t // TH, P * (t % TH):P * (t % TH) + P], others[:, t, :], ident[:])
                    if t % TH == TH - 1:
                        ins.then_inc(signal["othersT"], 1)

                def experts2_out(m):
                    pe.wait_ge(signal["hid5_ready"], at(pe, i, M1 * C, C * m + C))
                    for c in range(C):
                        ins = pe.matmul(bo[D * c:D * c + D, 1, :], w2_2[:, m, :], hid[:, (C * m + c) % NHID, :],
                                        start=False, stop=(m == M1 - 1), skip_group_check=True,
                                        tile_position=(0, D * c))
                    ins.then_inc(signal["w5_step"], 1)

                yield "ffn5.0"
                pe.wait_ge(signal["chosent_ready"], at(pe, i, C, C))
                pe.wait_ge(signal["otherst_ready"], at(pe, i, C, C))
                for c in range(C):
                    pe.matmul(bo[D * c:D * c + D, 1, :], b2_2[:], chosent[:, HALF * c:HALF * c + HALF],
                              start=True, stop=False, skip_group_check=True, tile_position=(0, D * c))
                for u in range(M1 * C):
                    m, c = u // C, u % C
                    yield "ffn5.%d" % m
                    if u >= 2:
                        pe.wait_ge(signal["hid5_ready"], at(pe, i, M1 * C, u - 1))
                    half = slice(HALF * c, HALF * c + HALF)
                    w = weight("w1_2", P * m, P)
                    pe.matmul(bw[:, u % 2, :], w, bhh[:, half], start=True, stop=False)
                    pe.matmul(bw[:, u % 2, :], w, bll[:, half], start=False, stop=False)
                    pe.matmul(bw[:, u % 2, :], block16[:, P * m:P * m + P], otherst[:, half],
                              start=False, stop=True).then_inc(signal["s5"], 1)
                    if c == 1 and m >= 1:
                        experts2_out(m - 1)
                yield "ffn5.%d" % M1
                experts2_out(M1 - 1)
                yield "out"
                pe.wait_ge(signal["mt5_ready"], at(pe, i, 1, 1))
                back_rows(mt2, bw[:, 0, :]).then_inc(signal["mt5T"], 1)

            pipeline(pe, front, back)


def constants():
    p = np.arange(P)
    inv = 1.0 / 10000.0 ** (np.arange(0, HD, 2, dtype=np.float32) / HD)
    angles = np.outer(np.arange(L, dtype=np.float32), inv)
    emb = np.concatenate([angles, angles], axis=-1)
    sign = np.where(np.arange(HD) < HD // 2, -1.0, 1.0).astype(np.float32)
    spread = np.zeros((40, MT * P), np.float32)
    for e in range(NE):
        spread[[e, 32 + e], e * HID:(e + 1) * HID] = 1.0
    block16 = np.zeros((E1, E1 * H1), np.float32)
    for e in range(E1):
        block16[e, e * H1:(e + 1) * H1] = NEG
    bf16 = mybir.dt.np(BF16)
    return {
        "ident": np.eye(P, dtype=np.float32),
        "ident16": np.eye(P, dtype=np.float32).astype(bf16),
        "mask_qk": np.where(p[None, :] > p[:, None], NEG, 0.0).astype(bf16),
        "mask_kq": np.where(p[None, :] < p[:, None], NEG, 0.0).astype(bf16),
        "cos": np.ascontiguousarray(np.tile(np.cos(emb).T, (6, 1))),
        "sin": np.ascontiguousarray(np.tile((np.sin(emb) * sign).T, (6, 1))),
        "iota": np.tile(np.arange(E1, dtype=np.float32), (P, 1)),
        "spread": spread,
        "block16": block16.astype(bf16),
    }


def layout(v):
    wq, wk = v["L0_ffn_wq"], v["L0_ffn_wk"]

    def swapped(w):
        n = w.shape[0] // HD
        return w.reshape(n, 2, HD // 2, D)[:, ::-1].reshape(n * HD, D)

    wide = [wq, wk, swapped(wq), swapped(wk), v["L0_ffn_wv"], v["L0_ffn_router_w"],
            v["L0_ffn_w1"].reshape(EH, D), v["L0_ffn_w3"].reshape(EH, D),
            v["L1_attn_Wq"].T, v["L1_attn_Wq"].T, v["L1_attn_Wk"].T, v["L1_attn_Wk"].T, v["L1_attn_Wv"].T,
            v["L1_ffn_router_w"], v["L1_ffn_W1"].transpose(0, 2, 1).reshape(E1 * H1, D)]
    lnw = np.stack([v["L0_ffn_ln1_w"], v["L0_ffn_ln2_w"]], axis=1)
    return {
        "x": np.concatenate([v["x"], v["x"][:1]]).reshape(B + 1, T, P).transpose(0, 2, 1),
        "table": v["L0_tok_W"].T,
        "wcat": np.concatenate(wide, axis=0).T,
        "lnw": np.concatenate([lnw, lnw], axis=0),
        "wo": v["L0_ffn_wo"].T,
        "w2": v["L0_ffn_w2"].transpose(0, 2, 1).reshape(EH, D),
        "w2_2": v["L1_ffn_W2"].reshape(M1, P, D).transpose(1, 0, 2),
        "b1_2": v["L1_ffn_b1"].reshape(M1, P).T,
        "b2_2": v["L1_ffn_b2"],
        "bq": np.concatenate([v["L1_attn_bq"]] * 2).reshape(P, 1),
        "bk": np.concatenate([v["L1_attn_bk"]] * 2).reshape(P, 1),
        "bv": v["L1_attn_bv"],
        "rb": v["L1_ffn_router_b"],
    }


def kernel(**inputs):
    import concourse.bacc as bacc
    from concourse.bass_utils import run_bass_kernel_spmd

    nc = bacc.Bacc("TRN2", target_bir_lowering=False, num_devices=1)
    given = {k: np.asarray(x) for k, x in inputs.items()}
    arrays = {k: np.ascontiguousarray(x) for k, x in {**layout(given), **constants()}.items()}
    aps = {k: nc.dram_tensor(f"in_{k}", x.shape, mybir.dt.from_np(x.dtype), kind="ExternalInput").ap()
           for k, x in arrays.items()}
    out = nc.dram_tensor("out", (B, L, D), F32, kind="ExternalOutput").ap()
    tower(nc, aps, out)
    r = run_bass_kernel_spmd(nc, [{f"in_{k}": x for k, x in arrays.items()}], core_ids=[0])
    return r.results[0]["out"]
```

```python
from contextlib import ExitStack

import concourse.bass as bass
import numpy as np
from concourse import mybir

F32 = mybir.dt.float32
F32R = mybir.dt.float32r
BF16 = mybir.dt.bfloat16
I32 = mybir.dt.int32
U32 = mybir.dt.uint32
ALU = mybir.AluOpType
ACT = mybir.ActivationFunctionType
AX = mybir.AxisListType

P = 128
B, L, D = 4, 1024, 64
VOCAB = 4360
T = L // P
HALF = 512
C = L // HALF
TH = T // C
NH, NKV, HD = 4, 2, 16
NE, TOPK, HID = 8, 2, int(8 / 3 * D)
EH = NE * HID
MT = -(-EH // P)
E1, H1 = 32, 16
M1 = E1 * H1 // P
LN_EPS, RMS_EPS = 1e-5, 1e-6
NEG = -1e30

COLS = {}
_at = 0
for _name, _n in (("qk", 96), ("qk_swapped", 96), ("v", 32), ("router", NE), ("w1", EH), ("w3", EH),
                  ("q2", P), ("k2", P), ("v2", D), ("router2", E1), ("w1_2", E1 * H1)):
    COLS[_name] = (_at, _at + _n)
    _at += _n
WCOLS = _at
GROUP1 = (0, COLS["v"][1])
GROUP2 = (COLS["router"][0], COLS["w3"][1])
GROUP3 = (COLS["q2"][0], WCOLS)



def causal_tiles(width_of):
    out = []
    for blk in range(T):
        for c in range(C):
            w = width_of(blk, c)
            if w > 0:
                n = min(NH, HALF // w)
                n = 2 if n == 3 else n
                out += [(blk, c, w, tuple(range(h, h + n))) for h in range(0, NH, n)]
    return out


MAX_TILES = causal_tiles(lambda blk, c: min(HALF, P * (blk + 1) - HALF * c))
PROB_TILES = sorted(causal_tiles(lambda blk, c: min(HALF, HALF * (c + 1) - P * blk)), key=lambda tile: tile[1])
SECOND = [tile[1] for tile in PROB_TILES].index(1)
NMAX, NPROB = len(MAX_TILES), len(PROB_TILES)
NSELF = T * C

NRING = 8
NHID = 8
FILLS = 7
DVE_EMBED, DVE_FRONT = 3, 16
DVE_ROUTE, DVE_BACK = 13, 23


def parts(name, n):
    return ["%s.%d" % (name, k) for k in range(n)]


def by_tile(make, use, n, behind):
    order = []
    for k in range(n + behind):
        order += parts(use, n)[k - behind:k - behind + 1] if k >= behind else []
        order += parts(make, n)[k:k + 1]
    return order


EMBED = ["emb", "rstd1", "x1", "x1T", "x1H", "x1L"] + parts("attn1", T + 1)
ATTEND = ["c1", "h1", "rstd2", "x2", "rrms2", "x2d", "x2T", "x2H", "x2L", "qk.0", "qk.1", "qk.2", "qkh", "qkl", "v"] \
    + by_tile("max", "reduce", NMAX, 2) + ["negm"] + by_tile("prob", "exp", NPROB, 1) + ["last_heads"] \
    + ["heads", "y", "yT", "wo", "x3", "rrms3", "x3d"]
ROUTE = ["x3T", "x3H", "x3L", "router", "lmax", "top2", "weights", "rwT", "rwL"]
EXPERTS = parts("moe", MT * C + 1) + ["moe_out", "h2", "rstd4", "x4", "x4T", "x4H", "x4L", "q2", "q2L", "v2", "k2", "k2L"] \
    + by_tile("max3", "reduce3", NSELF, 2) + ["negm3"] + parts("attn3", T + 1) \
    + ["c3", "h3", "rstd5", "x5", "x5T", "x5H", "x5L", "lg5", "top1", "othersT", "chosen"]
FINISH = parts("ffn5", M1 + 1) + ["out", "h4", "store"]


def alternate(a, b):
    both = [((k + 0.5) / len(x), n, step) for n, x in enumerate((a, b)) for k, step in enumerate(x)]
    return [step for _, _, step in sorted(both)]


def beside(a, b, *ends):
    out, i, j = [], 0, 0
    for end_a, end_b in (*ends, (a[-1], b[-1])):
        i1, j1 = a.index(end_a) + 1 if end_a else 0, b.index(end_b) + 1 if end_b else 0
        out += alternate(a[i:i1], b[j:j1])
        i, j = i1, j1
    return out


ATTEND_BESIDE_EXPERTS = beside(
    ATTEND, EXPERTS,
    ("rrms2", "moe.6"), ("x2L", "moe.11"), ("v", "moe.17"), ("v", "moe.21"), ("max.11", "moe.22"),
    ("reduce.10", "h2"), ("reduce.21", "h2"), ("max.37", "reduce3.1"), ("exp.1", "max3.13"),
    ("exp.3", "max3.13"), ("exp.5", "max3.13"), ("exp.5", "reduce3.15"), ("exp.7", "reduce3.15"),
    ("exp.7", "negm3"), ("exp.10", "negm3"), ("exp.18", "c3"), ("exp.28", "rstd5"),
    ("exp.34", "othersT"))
EMBED_BESIDE_FINISH = beside(
    EMBED, FINISH + ROUTE,
    ("emb", "ffn5.2"), ("x1L", "x3H"), ("attn1.2", "x3H"), ("attn1.3", "router"), ("attn1.7", "rwL"))
EMBED_BESIDE_ROUTE = beside(EMBED, ROUTE)


def take_steps(order, *stages):
    coming = [next(stage, None) for stage in stages]
    for name in order:
        for n, stage in enumerate(stages):
            while coming[n] == name:
                coming[n] = next(stage, None)
    assert coming == [None] * len(stages), coming


def pipeline(eng, embed, attend, route, experts, finish):
    take_steps(EMBED, embed(0))
    take_steps(ATTEND, attend(0))
    take_steps(EMBED_BESIDE_ROUTE, embed(1), route(0))
    with eng.Fori(1, B - 1, 1) as i:
        take_steps(ATTEND_BESIDE_EXPERTS, attend(i), experts((i, -1)))
        take_steps(EMBED_BESIDE_FINISH, embed((i, 1)), finish((i, -1)), route(i))
    take_steps(ATTEND_BESIDE_EXPERTS, attend(B - 1), experts(B - 2))
    take_steps(FINISH + ROUTE, finish(B - 2), route(B - 1))
    take_steps(EXPERTS, experts(B - 1))
    take_steps(FINISH, finish(B - 1))


def first(i):
    return isinstance(i, int) and i == 0


def at(eng, i, per, n):
    if isinstance(i, int):
        return i * per + n
    if isinstance(i, tuple):
        i, ahead = i
        n += ahead * per
    if n == 0:
        eng.reg_alu(WAIT_REGISTER[eng.engine], i * per, 1, ALU.max)
    else:
        eng.reg_alu(WAIT_REGISTER[eng.engine], i * per, n, ALU.add)
    return WAIT_REGISTER[eng.engine]


WAIT_REGISTER = {}


def tower(nc, a, out):
    ctx = ExitStack()
    with ctx:
        def sb(name, shape, dt=F32):
            return ctx.enter_context(nc.sbuf_tensor(name, shape, dt))

        def ps(name, shape, dt=F32):
            return ctx.enter_context(nc.psum_tensor(name, shape, dt))

        ident = sb("ident", [P, P])
        ident16 = sb("ident16", [P, P], BF16)
        mask_qk = sb("mask_qk", [P, P], BF16)
        mask_kq = sb("mask_kq", [P, P], BF16)
        cos = sb("cos", [96, L])
        sin = sb("sin", [96, L])
        iota = sb("iota", [P, E1])
        spread = sb("spread", [40, MT * P], F32R)
        block16 = sb("block16", [E1, E1 * H1], BF16)
        lnw = sb("lnw", [P, 2])
        w_s = sb("w_s", [P, WCOLS], F32R)
        wo = sb("wo", [D, D])
        w2 = sb("w2", [P, MT, D])
        w2_2 = sb("w2_2", [P, M1, D])
        b1_2 = sb("b1_2", [P, M1])
        b2_2 = sb("b2_2", [E1, D])
        bq = sb("bq", [P, 1])
        bk = sb("bk", [P, 1])
        bv = sb("bv", [P, D])
        rb = sb("rb", [P, E1])
        minus_half = sb("minus_half", [P, T])
        ones = sb("ones", [P, 1])

        negm_dram = nc.dram_tensor("negm_rows", (NH * T, P), F32, kind="Internal").ap()
        negm3_dram = nc.dram_tensor("negm3_rows", (T, P), F32, kind="Internal").ap()

        def wait_apart(eng, sem, count):
            eng.wait_ge(signal["started"], 1)
            eng.wait_ge(sem, count)

        def weight(name, lo=0, n=None):
            c0, c1 = COLS[name]
            return w_s[:, c0 + lo:(c1 if n is None else c0 + lo + n)]

        idx = sb("idx", [P, T], I32)
        emb = sb("emb", [P, T, D])
        keep = sb("keep", [P, T])
        h0 = sb("h0", [P, T, D])
        stats = sb("stats", [P, T, 6])
        mv = sb("mv", [P, T, 2])
        veps = sb("veps", [P, T])
        rstd = sb("rstd", [P, T])
        xd = sb("xd", [P, T, 2, D])
        hh = sb("hh", [P, L], F32R)
        ll = sb("ll", [P, L], F32R)
        aa = sb("aa", [P, L], F32R)
        prob = sb("prob", [P, NRING, HALF])
        esum1 = sb("esum1", [P, T, C])
        den1 = sb("den1", [P, T])
        rsum = sb("rsum", [P, T])
        h1 = sb("h1", [P, T, D])
        x2 = sb("x2", [P, T, D])
        sq = sb("sq", [P, T, D])
        att = sq
        ssum = sb("ssum", [P, T])
        rope_a = sb("rope_a", [96, 2, HALF])
        rope_b = sb("rope_b", [96, 2, HALF])
        qk = rope_a[:].rearrange("p c n -> p (c n)")
        qkh = sb("qkh", [96, L], F32R)
        qkl = sb("qkl", [96, L], F32R)
        qs = sb("qs", [P, NH, L], F32R)
        ks = sb("ks", [P, L], F32R)
        spread_f = ((0, L, rope_a[0:40].rearrange("p c n -> p (c n)")),
                    (L, MT * P, rope_b[0:40].rearrange("p c n -> p (c n)")[:, 0:MT * P - L]))
        v1 = sb("v1", [P, T, NKV, 32])
        mx = sb("mx", [P, NH, T, C])
        mxt = sb("mxt", [P, NH, T])
        negm = sb("negm", [NH * T, P], F32R)
        ot = sb("ot", [P, L])
        rs4 = sb("rs4", [P, T, NH])
        y = sb("y", [P, T, D])
        yt = rope_b[0:D].rearrange("p c n -> p (c n)")
        x3 = sb("x3", [P, T, D])
        res = sb("res", [P, T, D])
        x3d = sb("x3d", [P, T, 2, D])
        bhh = sb("bhh", [P, L], F32R)
        bll = sb("bll", [P, L], F32R)
        lg = sb("lg", [P, T, NE])
        lmax = sb("lmax", [P, T])
        ex = sb("ex", [P, T, NE])
        esum = sb("esum", [P, T])
        top8 = sb("top8", [P, T, 8])
        topi = sb("topi", [P, T, 8], U32)
        topf = sb("topf", [P, T, 2])
        oh_a = sb("oh_a", [P, T, NE])
        oh_b = sb("oh_b", [P, T, NE])
        wt = sb("wt", [40, L], F32R)
        sa = sb("sa", [P, 2, HALF])
        ub = sb("ub", [P, 2, HALF])
        hid = sb("hid", [P, NHID, HALF])
        w_f = hid[:].rearrange("p r n -> p (r n)")[:, 0:WCOLS]
        mt = sb("mt", [P, HALF])
        h2 = sb("h2", [P, T, D])
        bstats = sb("bstats", [P, T, 6])
        bmv = sb("bmv", [P, T, 2])
        bveps = sb("bveps", [P, T])
        brstd = sb("brstd", [P, T])
        bxd = sb("bxd", [P, T, 2, D])
        weights = bxd[:].rearrange("p (u t) r d -> p u (t r d)", u=2)
        qh = sb("qh", [P, L], F32R)
        ql = sb("ql", [D + 1, L], F32R)
        ka = sb("ka", [P, L], F32R)
        k2 = sb("k2", [D + 1, L], F32R)
        v2 = sb("v2", [P, T, D])
        sums = sa
        bprob = hid
        mx3 = sb("mx3", [P, C, T])
        m3 = sb("m3", [P, T])
        negm3 = sb("negm3", [T, P], F32R)
        brsum = sb("brsum", [P, TH, C])
        batt = sb("batt", [P, T, D])
        h3 = sb("h3", [P, T, D])
        lg5 = sb("lg5", [P, T, E1])
        top8b = sb("top8b", [P, T, 8])
        topib = sb("topib", [P, T, 8], U32)
        topfb = sb("topfb", [P, T])
        others = sb("others", [P, T, E1])
        otherst = sb("otherst", [E1, L], BF16)
        chosent = sa[0:E1].rearrange("p c n -> p (c n)")
        mt2 = mt
        h4 = sb("h4", [P, T, D])

        fw = ps("fw", [P, 2, HALF])
        fo = ps("fo", [P, 2, HALF])
        bw = ps("bw", [P, 2, HALF])
        bo = ps("bo", [P, 2, HALF])

        attn1_ring = (fw[:, 0, :], fw[:, 1, :], fo[:, 0, :])
        max_ring = (fw[:, 0, :], fw[:, 1, :], fo[:, 1, :])
        prob_ring = ((fw[:, 0, :], fw[:, 1, :], fo[:, 1, :]), (fw[:, 0, :], fw[:, 1, :], fo[:, 0, :]))
        attn3_ring = max3_ring = (bw[:, 0, :], bw[:, 1, :], bo[:, 1, :])
        ffn5_ring = (bw[:, 0, :], bw[:, 1, :], bo[:, 0, :])

        def prob_bank(u):
            return prob_ring[0][u % 3] if u < SECOND else prob_ring[1][(u - SECOND) % 3]

        names = """started ident_loaded const_loaded w1_loaded w2_loaded w_scaled w_high w_ready const_cast filled
            spread_copied v1_zeroed idx_loaded emb_gathered emb_used step_f step_b var1 rstd1 x1_ready x1T
            hh1 aa1 ll1 aal1 s1 e1 pv1 h1_ready var2 rstd2 ssq2 rrms2 x2_ready x2T hh2 ll2 qk_ps rope_used
            qk_ready qkh_ready qkl_ready v_ps v_ready spread_done sm max_used max_ready maxT negm_ready
            negm_stored negm_placed negm3_stored s2 e2 pv2 ot_ready otT y_ready yT yt_ready wo_ps x3_ready
            ssq3 rrms3 x3_done x3T hh3 ll3 lg_ps lmax_ready ex_ready rw_ready rwT wth_ready wt_ready moe_a
            moe_b moe_w silu ub_ready hid_ready w2_step moe_out mt_ready mtT h2_ready var4 rstd4 x4_ready
            x4T hh4 ll4 q_ps qh_ready ql_ready k_ps ka_ready k2_ready kal_ready v2_ps v2_ready sm3 max3_used
            m3_ready c1_ready c1T sum3_pool sum3_dve c3_ready c3T m3T negm3_ready negm3_placed s3 e3 pv3
            h3_ready var5 rstd5 x5_ready x5T hh5 ll5 lg5_ps others_ready othersT otherst_ready chosent_ready
            s5 hid5_ready w5_step mt5_ready mt5T h4_ready h4_free""".split()
        signal = {n: ctx.enter_context(nc.semaphore(n)) for n in names}

        def dup(ap):
            return ap.unsqueeze(2).to_broadcast([P, ap.shape[1], D])

        def by_half(x):
            return x.rearrange("p (c t) d -> p t c d", c=C)

        block = ctx.enter_context(nc.Block())

        @block.sync
        def _(sp):
            WAIT_REGISTER[sp.engine] = sp.alloc_register("wait_value")
            sp.dma_start(ident[:], a["ident"]).then_inc(signal["ident_loaded"], 16)
            sp.dma_start(lnw[:], a["lnw"]).then_inc(signal["w1_loaded"], 16)
            for half in range(2):
                sp.dma_start(w_f[D * half:D * half + D, :], a["wcat"]).then_inc(signal["w1_loaded"], 16)
            early = [(ident16, a["ident16"]), (mask_qk, a["mask_qk"]),
                     (mask_kq, a["mask_kq"]), (cos, a["cos"]), (sin, a["sin"]), (wo, a["wo"]), (iota, a["iota"]),
                     *((dst, a["spread"][:, c0:c1]) for c0, c1, dst in spread_f), (block16, a["block16"]),
                     (w2_2, a["w2_2"]), (b1_2, a["b1_2"]), (b2_2, a["b2_2"]), (bq, a["bq"]), (bk, a["bk"])]
            for dst, src in early:
                sp.dma_start(dst[:], src).then_inc(signal["const_loaded"], 16)
            sp.dma_start(bv[:], a["bv"].partition_broadcast(P)).then_inc(signal["const_loaded"], 16)
            sp.dma_start(rb[:], a["rb"].partition_broadcast(P)).then_inc(signal["const_loaded"], 16)
            sp.dma_start(w2[:, 0:MT - 1, :], a["w2"][0:(MT - 1) * P].rearrange("(m p) d -> p m d", p=P)) \
                .then_inc(signal["w2_loaded"], 16)
            sp.dma_start(w2[0:EH - (MT - 1) * P, MT - 1, :], a["w2"][(MT - 1) * P:EH]).then_inc(signal["w2_loaded"], 16)

            def embed(i):
                yield from ()

            def attend(i):
                yield "qkh"
                def spread_rows(dst, src):
                    sp.dma_start(dst.bitcast(F32), src.bitcast(F32)).then_inc(signal["spread_done"], 16)

                sp.wait_ge(signal["qkh_ready"], at(sp, i, C, C))
                for r in (0, 2):
                    for h in range(NH):
                        row = 32 * r + HD * (h // 2)
                        spread_rows(qs[row:row + HD, h, :], qkh[HD * h:HD * h + HD, :])
                for r in (0, 1):
                    spread_rows(ks[32 * r:32 * r + 32, :], qkh[64:96, :])
                yield "qkl"
                sp.wait_ge(signal["qkl_ready"], at(sp, i, C, C))
                spread_rows(ks[64:96, :], qkl[64:96, :])
                for h in range(NH):
                    row = 32 + HD * (h // 2)
                    spread_rows(qs[row:row + HD, h, :], qkl[HD * h:HD * h + HD, :])
                yield "negm"
                sp.wait_ge(signal["negm_ready"], at(sp, i, 1, 1))
                sp.dma_start(negm_dram, negm[:].bitcast(F32)).then_inc(signal["negm_stored"], 16)
                sp.wait_ge(signal["negm_stored"], at(sp, i, 16, 16))
                sp.dma_start(qs[96:97, :, :].bitcast(F32), negm_dram.rearrange("(o h t) n -> o h (t n)", o=1, h=NH)) \
                    .then_inc(signal["negm_placed"], 16)

            def route(i):
                yield from ()

            def experts(i):
                yield "negm3"
                sp.wait_ge(signal["negm3_ready"], at(sp, i, 1, 1))
                sp.dma_start(negm3_dram, negm3[:].bitcast(F32)).then_inc(signal["negm3_stored"], 16)
                sp.wait_ge(signal["negm3_stored"], at(sp, i, 16, 16))
                sp.dma_start(ql[D:D + 1, :].bitcast(F32), negm3_dram.rearrange("(o t) n -> o (t n)", o=1)) \
                    .then_inc(signal["negm3_placed"], 16)

            def finish(i):
                yield "store"
                sp.wait_ge(signal["h4_ready"], at(sp, i, 1, 1))
                b = i[0] + i[1] if isinstance(i, tuple) else i
                sp.dma_start(out[bass.ds(b, 1)].rearrange("b (t p) d -> p (b t) d", p=P), h4[:]) \
                    .then_inc(signal["h4_free"], 16)

            pipeline(sp, embed, attend, route, experts, finish)
            sp.wait_ge(signal["h4_free"], at(sp, B, 16, 16))

        @block.gpsimd
        def _(pool):
            WAIT_REGISTER[pool.engine] = pool.alloc_register("wait_value")
            pool.memset(minus_half[:], -0.5).then_inc(signal["started"], 1)

            def load_tokens(b):
                pool.dma_start(idx[:], a["x"][bass.ds(b, 1)].rearrange("b p t -> p (b t)")) \
                    .then_inc(signal["idx_loaded"], 16)
                wait_apart(pool, signal["idx_loaded"], at(pool, b, 16, 16))

            def gather(t):
                pool.indirect_dma_start(emb[:, t, :], None, a["table"], bass.IndirectOffsetOnAxis(idx[:, t:t + 1], 0)) \
                    .then_inc(signal["emb_gathered"], 16)

            def power(i, ready, v, dst, done):
                wait_apart(pool, ready, at(pool, i, 1, 1))
                pool.tensor_tensor(dst[:], v[:], minus_half[:], ALU.pow).then_inc(done, 1)

            def embed(i):
                yield "rstd1"
                power(i, signal["var1"], veps, rstd, signal["rstd1"])

            def attend(i):
                yield "rstd2"
                power(i, signal["var2"], veps, rstd, signal["rstd2"])
                yield "rrms2"
                power(i, signal["ssq2"], veps, rstd, signal["rrms2"])
                if not (isinstance(i, int) and i == B - 1):
                    yield "negm"
                    load_tokens(i + 1)
                    for t in range(T):
                        yield "prob.%d" % (4 * t)
                        gather(t)
                yield "rrms3"
                power(i, signal["ssq3"], veps, rstd, signal["rrms3"])

            def route(i):
                yield from ()

            def experts(i):
                for u in range(MT * C):
                    yield "moe.%d" % u
                    n = min(P, EH - u // C * P)
                    pool.wait_ge(signal["ub_ready"], at(pool, i, MT * C, u + 1))
                    if u >= NHID:
                        pool.wait_ge(signal["w2_step"], at(pool, i, MT, (u - NHID) // C + 1))
                    pool.wait_ge(signal["spread_copied"], at(pool, i, MT * C, u + 1))
                    pool.tensor_tensor(hid[0:n, u % NHID, :], ub[0:n, u % 2, :], weights[0:n, u % 2, :], ALU.mult) \
                        .then_inc(signal["hid_ready"], 1)
                yield "rstd4"
                power(i, signal["var4"], bveps, brstd, signal["rstd4"])
                for j in range(1, T):
                    yield "attn3.%d" % (j + 1)
                    if j == 1:
                        pool.wait_ge(signal["m3_ready"], at(pool, i, 1, 1))
                    else:
                        pool.wait_ge(signal["sum3_pool"], at(pool, i, T - 1, j - 1))
                    pool.wait_ge(signal["e3"], at(pool, i, NSELF, C * j + 1))
                    before = bprob[:, 0, :] if j == 1 else sums[:, 0, :]
                    pool.tensor_tensor(sums[:, 0, :], before, bprob[:, C * j % NHID, :], ALU.add) \
                        .then_inc(signal["sum3_pool"], 1)
                yield "rstd5"
                power(i, signal["var5"], bveps, brstd, signal["rstd5"])

            def finish(i):
                yield from ()

            load_tokens(0)
            for t in range(T):
                gather(t)
            pool.memset(ones[:], 1.0).then_inc(signal["filled"], 1)
            pool.memset(v1[:], 0.0).then_inc(signal["v1_zeroed"], 1)
            pool.wait_ge(signal["v1_zeroed"], 1)
            pool.memset(v1[:, :, :, HD:HD + 1], 1.0).then_inc(signal["filled"], 1)
            pool.memset(mx[:], -3e38).then_inc(signal["filled"], 1)
            pool.memset(wt[:].bitcast(F32), 0.0).then_inc(signal["filled"], 1)
            pool.memset(qs[:].bitcast(F32), 0.0).then_inc(signal["filled"], 1)
            pipeline(pool, embed, attend, route, experts, finish)
            pool.wait_ge(signal["emb_gathered"], at(pool, B, 16 * T, 0))

        @block.scalar
        def _(act):
            WAIT_REGISTER[act.engine] = act.alloc_register("wait_value")
            def copy(dst, src):
                return act.activation(dst, src, ACT.Copy)

            def high(i, ready, psum, dst, done):
                for c in range(C):
                    act.wait_ge(ready, at(act, i, C, c + 1))
                    copy(dst[:, HALF * c:HALF * c + HALF], psum[:, c, :]).then_inc(done, 1)

            def embed(i):
                yield "x1H"
                for c in range(C):
                    half = slice(HALF * c, HALF * c + HALF)
                    act.wait_ge(signal["x1T"], at(act, i, C, c + 1))
                    copy(hh[:, half], fo[:, c, :]).then_inc(signal["hh1"], 1)
                    copy(aa[:, half], fo[:, c, :]).then_inc(signal["aa1"], 1)
                for u in range(NSELF):
                    j, c = u // C, u % C
                    yield "attn1.%d" % j
                    act.wait_ge(signal["s1"], at(act, i, NSELF, u + 1))
                    if u >= NRING:
                        act.wait_ge(signal["pv1"], at(act, i, T, (u - NRING) // C + 1))
                    act.activation(prob[:, u % NRING, :], attn1_ring[u % 3], ACT.Exp, scale=1.0 / 8,
                                   accum_out=esum1[:, j, c:c + 1]).then_inc(signal["e1"], 1)

            def attend(i):
                yield "c1"
                act.wait_ge(signal["pv1"], at(act, i, T, T))
                copy(ot[:, 0:HALF], fo[:, 1, :]).then_inc(signal["c1_ready"], 1)
                if first(i):
                    act.wait_ge(signal["const_loaded"], 16 * 17)
                    for c0, c1, src in spread_f:
                        copy(spread[:, c0:c1], src).then_inc(signal["const_cast"], 1)
                    act.wait_ge(signal["filled"], FILLS)
                yield "x2H"
                high(i, signal["x2T"], fo, hh, signal["hh2"])
                yield "qkh"
                for c in range(C):
                    act.wait_ge(signal["qk_ready"], at(act, i, C, c + 1))
                    copy(qkh[:, HALF * c:HALF * c + HALF], qk[:, HALF * c:HALF * c + HALF]).then_inc(signal["qkh_ready"], 1)
                yield "v"
                act.wait_ge(signal["v_ps"], at(act, i, 1, 1))
                copy(v1[:, :, :, 0:HD], fo[:, 0, 0:T * 32].rearrange("p (t g d) -> p t g d", t=T, g=NKV)) \
                    .then_inc(signal["v_ready"], 1)
                yield "negm"
                act.wait_ge(signal["maxT"], at(act, i, 1, 1))
                act.activation(negm[:], fo[0:NH * T, 1, 0:P], ACT.Copy, scale=-1.0).then_inc(signal["negm_ready"], 1)
                for u, (j, c, w, heads) in enumerate(PROB_TILES):
                    yield "exp.%d" % u
                    act.wait_ge(signal["s2"], at(act, i, NPROB, u + 1))
                    if u >= NRING:
                        act.wait_ge(signal["pv2"], at(act, i, NPROB, u - NRING + 1))
                    n = w * len(heads)
                    act.activation(prob[:, u % NRING, 0:n], prob_bank(u)[:, 0:n], ACT.Exp, scale=0.25) \
                        .then_inc(signal["e2"], 1)
                    if u == SECOND + 1:
                        act.wait_ge(signal["pv2"], at(act, i, NPROB, SECOND))
                        copy(ot[:, 0:HALF], fo[:, 0, :]).then_inc(signal["ot_ready"], 1)
                yield "heads"
                act.wait_ge(signal["pv2"], at(act, i, NPROB, NPROB))
                copy(ot[:, HALF:L], fo[:, 1, :]).then_inc(signal["ot_ready"], 1)
                yield "yT"
                for c in range(C):
                    act.wait_ge(signal["yT"], at(act, i, C, c + 1))
                    copy(yt[:, HALF * c:HALF * c + HALF], fo[0:D, c, :]).then_inc(signal["yt_ready"], 1)

            def route(i):
                yield "x3H"
                high(i, signal["x3T"], bo, bhh, signal["hh3"])
                yield "lmax"
                act.wait_ge(signal["lmax_ready"], at(act, i, 1, 1))
                act.activation(ex[:], lg[:], ACT.Exp).then_inc(signal["ex_ready"], 1)
                yield "rwT"
                for c in range(C):
                    act.wait_ge(signal["rwT"], at(act, i, C, c + 1))
                    copy(wt[0:NE, HALF * c:HALF * c + HALF], bo[0:NE, c, :]).then_inc(signal["wth_ready"], 1)

            def experts(i):
                def silu(u):
                    n = min(P, EH - u // C * P)
                    act.wait_ge(signal["moe_a"], at(act, i, MT * C, u + 1))
                    if u >= 2:
                        act.wait_ge(signal["ub_ready"], at(act, i, MT * C, u - 1))
                    act.activation(sa[0:n, u % 2, :], bw[0:n, 0, :], ACT.Silu).then_inc(signal["silu"], 1)

                for u in range(MT * C):
                    yield "moe.%d" % u
                    n = min(P, EH - u // C * P)
                    if u == 0:
                        silu(0)
                    if u + 1 < MT * C:
                        silu(u + 1)
                    act.wait_ge(signal["moe_w"], at(act, i, MT * C, u + 1))
                    if u >= 2:
                        act.wait_ge(signal["hid_ready"], at(act, i, MT * C, u - 1))
                    copy(weights[0:n, u % 2, :], bo[0:n, 0, :]).then_inc(signal["spread_copied"], 1)
                yield "moe_out"
                act.wait_ge(signal["w2_step"], at(act, i, MT, MT))
                copy(mt[:], bo[:, 1, :]).then_inc(signal["mt_ready"], 1)
                yield "x4H"
                high(i, signal["x4T"], bo, bhh, signal["hh4"])
                yield "q2"
                for c in range(C):
                    half = slice(HALF * c, HALF * c + HALF)
                    act.wait_ge(signal["q_ps"], at(act, i, C, c + 1))
                    act.activation(qh[:, half], bw[:, c, :], ACT.Identity, bias=bq[:, 0:1]).then_inc(signal["qh_ready"], 1)
                yield "k2"
                for c in range(C):
                    half = slice(HALF * c, HALF * c + HALF)
                    act.wait_ge(signal["k_ps"], at(act, i, C, c + 1))
                    act.activation(ka[:, half], bw[:, c, :], ACT.Identity, bias=bk[:, 0:1]).then_inc(signal["ka_ready"], 1)
                    act.activation(k2[0:D, half], bw[0:D, c, :], ACT.Identity, bias=bk[0:D, 0:1]) \
                        .then_inc(signal["k2_ready"], 1)
                yield "negm3"
                act.wait_ge(signal["m3T"], at(act, i, 1, 1))
                act.activation(negm3[:], bo[0:T, 1, 0:P], ACT.Copy, scale=-1.0).then_inc(signal["negm3_ready"], 1)
                for u in range(NSELF):
                    j = u // C
                    yield "attn3.%d" % j
                    act.wait_ge(signal["s3"], at(act, i, NSELF, u + 1))
                    if u >= NHID:
                        before = j - NHID // C
                        act.wait_ge(signal["pv3"], at(act, i, T, before + 1))
                        act.wait_ge(signal[("sum3_pool", "sum3_dve")[u % C]], at(act, i, T - 1, max(before, 1)))
                    act.activation(bprob[:, u % NHID, :], attn3_ring[u % 3], ACT.Exp, scale=1.0 / 8).then_inc(signal["e3"], 1)
                yield "c3"
                act.wait_ge(signal["pv3"], at(act, i, T, T))
                copy(mt[:], bo[:, 0, :]).then_inc(signal["c3_ready"], 1)
                yield "x5H"
                high(i, signal["x5T"], bo, bhh, signal["hh5"])
                yield "othersT"
                for c in range(C):
                    act.wait_ge(signal["othersT"], at(act, i, C, c + 1))
                    copy(otherst[:, HALF * c:HALF * c + HALF], bo[0:E1, c, :]).then_inc(signal["otherst_ready"], 1)

            def finish(i):
                for u in range(M1 * C):
                    yield "ffn5.%d" % (u // C)
                    act.wait_ge(signal["s5"], at(act, i, M1 * C, u + 1))
                    if u >= NHID:
                        act.wait_ge(signal["w5_step"], at(act, i, M1, (u - NHID) // C + 1))
                    act.activation(hid[:, u % NHID, :], ffn5_ring[u % 3], ACT.Relu, bias=b1_2[:, u // C:u // C + 1]) \
                        .then_inc(signal["hid5_ready"], 1)
                yield "out"
                act.wait_ge(signal["w5_step"], at(act, i, M1, M1))
                act.activation(mt2[:], bo[:, 1, :], ACT.Relu).then_inc(signal["mt5_ready"], 1)

            pipeline(act, embed, attend, route, experts, finish)

        @block.vector
        def _(dve):
            WAIT_REGISTER[dve.engine] = dve.alloc_register("wait_value")
            dve.memset(ks[96:128, :].bitcast(F32), 1.0).then_inc(signal["filled"], 1)
            dve.memset(k2[D:D + 1, :].bitcast(F32), 1.0).then_inc(signal["filled"], 1)
            dve.memset(h4[:], 0.0).then_inc(signal["h4_free"], 16)

            def prepare_weights():
                dve.wait_ge(signal["w1_loaded"], 16 * 3)
                for k, (c0, c1) in enumerate((GROUP1, GROUP2)):
                    dve.tensor_scalar(w_f[:, c0:c1], w_f[:, c0:c1], lnw[:, k:k + 1], None, ALU.mult) \
                        .then_inc(signal["w_scaled"], 1)
                dve.wait_ge(signal["w_scaled"], 2)
                dve.tensor_copy(w_s[:], w_f[:]).then_inc(signal["w_high"], 1)
                dve.wait_ge(signal["w_high"], 1)
                dve.tensor_tensor(w_s[D:P, :], w_f[D:P, :], w_s[D:P, :].bitcast(F32), ALU.subtract) \
                    .then_inc(signal["w_ready"], 1)

            def low(i, ready, psum, high_of, dst, done, rows=slice(0, P)):
                for c in range(C):
                    half = slice(HALF * c, HALF * c + HALF)
                    dve.wait_ge(ready, at(dve, i, C, c + 1))
                    dve.tensor_tensor(dst[rows, half], psum[rows, c, :], high_of[rows, half].bitcast(F32),
                                      ALU.subtract).then_inc(done, 1)

            count = {}

            def link(ins, i, which="f", apart=False):
                count[which] += 1
                sem, per = (signal["step_f"], DVE_FRONT) if which == "f" else (signal["step_b"], DVE_BACK)
                ins.then_inc(sem, 1)
                if apart:
                    wait_apart(dve, sem, at(dve, i, per, count[which]))
                else:
                    dve.wait_ge(sem, at(dve, i, per, count[which]))

            def moments(i, src, st, m, v, which):
                for t in range(T):
                    ins = dve.bn_stats(st[:, t, :], src[:, t, :])
                link(ins, i, which, apart=True)
                for t in range(T):
                    ins = dve.bn_aggr(m[:, t, :], st[:, t, :])
                link(ins, i, which)
                return dve.tensor_scalar(v[:], m[:, :, 1], LN_EPS, None, ALU.add)

            def norm_back(i, src, rstd_done, done):
                dve.wait_ge(rstd_done, at(dve, i, 1, 1))
                for t in range(T):
                    ins = dve.tensor_scalar(bxd[:, t, :, :], src[:, t, :].unsqueeze(1).to_broadcast([P, 2, D]),
                                            bmv[:, t, 0:1], brstd[:, t:t + 1], ALU.subtract, ALU.mult)
                    if t % TH == TH - 1:
                        ins.then_inc(done, 1)

            def embed(i):
                count["f"] = 0
                yield "emb"
                dve.wait_ge(signal["emb_gathered"], at(dve, i, 16 * T, 16 * T))
                link(dve.tensor_scalar(keep[:], idx[:], 0, None, ALU.not_equal), i)
                dve.tensor_tensor(h0[:], emb[:], dup(keep[:]), ALU.mult).then_inc(signal["emb_used"], 1)
                dve.wait_ge(signal["emb_used"], at(dve, i, 1, 1))
                moments(i, h0, stats, mv, veps, "f").then_inc(signal["var1"], 1)
                yield "x1"
                dve.wait_ge(signal["rstd1"], at(dve, i, 1, 1))
                for t in range(T):
                    ins = dve.tensor_scalar(xd[:, t, :, :], h0[:, t, :].unsqueeze(1).to_broadcast([P, 2, D]), mv[:, t, 0:1],
                                            rstd[:, t:t + 1], ALU.subtract, ALU.mult)
                    if t % TH == TH - 1:
                        ins.then_inc(signal["x1_ready"], 1)
                yield "x1L"
                for c in range(C):
                    half = slice(HALF * c, HALF * c + HALF)
                    dve.wait_ge(signal["hh1"], at(dve, i, C, c + 1))
                    dve.wait_ge(signal["aa1"], at(dve, i, C, c + 1))
                    dve.tensor_tensor(ll[:, half], fo[:, c, :], hh[:, half].bitcast(F32), ALU.subtract) \
                        .then_inc(signal["ll1"], 1)
                    dve.tensor_tensor(aa[D:P, half], fo[D:P, c, :], aa[D:P, half].bitcast(F32), ALU.subtract) \
                        .then_inc(signal["aal1"], 1)
                if first(i):
                    prepare_weights()
                assert count["f"] == DVE_EMBED, count

            def attend(i):
                count["f"] = DVE_EMBED
                yield "h1"
                dve.wait_ge(signal["e1"], at(dve, i, NSELF, NSELF))
                link(dve.tensor_tensor(den1[:], esum1[:, :, 0], esum1[:, :, 1], ALU.add), i)
                link(dve.reciprocal(rsum[:], den1[:]), i)
                dve.wait_ge(signal["c1T"], at(dve, i, 1, 1))
                link(dve.tensor_tensor(by_half(att[:]), fo[:, 0, :].rearrange("p (t c d) -> p t c d", t=TH, c=C),
                                       by_half(dup(rsum[:])), ALU.mult), i)
                dve.tensor_tensor(h1[:], att[:], h0[:], ALU.add).then_inc(signal["h1_ready"], 1)
                if first(i):
                    dve.wait_ge(signal["const_loaded"], 16 * 17)
                    dve.wait_ge(signal["const_cast"], 2)
                    dve.wait_ge(signal["filled"], FILLS)
                dve.wait_ge(signal["h1_ready"], at(dve, i, 1, 1))
                moments(i, h1, stats, mv, veps, "f").then_inc(signal["var2"], 1)
                yield "x2"
                dve.wait_ge(signal["rstd2"], at(dve, i, 1, 1))
                for t in range(T):
                    ins = dve.tensor_scalar(x2[:, t, :], h1[:, t, :], mv[:, t, 0:1], rstd[:, t:t + 1],
                                            ALU.subtract, ALU.mult)
                link(ins, i)

                def squares(src, ssq):
                    link(dve.tensor_tensor(sq[:], src[:], src[:], ALU.mult), i)
                    link(dve.tensor_reduce(ssum[:], sq[:], AX.X, ALU.add), i)
                    dve.tensor_scalar(veps[:], ssum[:], 1.0 / D, RMS_EPS, ALU.mult, ALU.add).then_inc(ssq, 1)

                def rms(src, rrms, dst, done):
                    dve.wait_ge(rrms, at(dve, i, 1, 1))
                    for c in range(C):
                        tiles = slice(TH * c, TH * c + TH)
                        dve.tensor_tensor(dst[:, tiles], src[:, tiles].unsqueeze(2).to_broadcast([P, TH, 2, D]),
                                          rstd[:, tiles].unsqueeze(2).unsqueeze(3).to_broadcast([P, TH, 2, D]),
                                          ALU.mult).then_inc(done, 1)

                squares(x2, signal["ssq2"])
                yield "x2d"
                rms(x2, signal["rrms2"], xd, signal["x2_ready"])
                yield "x2L"
                low(i, signal["hh2"], fo, hh, ll, signal["ll2"])
                for c in range(C):
                    half = slice(HALF * c, HALF * c + HALF)
                    yield "qk.%d" % (c + 1)
                    dve.wait_ge(signal["qk_ps"], at(dve, i, C, c + 1))
                    dve.tensor_tensor(rope_a[:, c, :], fw[0:96, 0, :], cos[:, half], ALU.mult).then_inc(signal["rope_used"], 1)
                    dve.tensor_tensor(rope_b[:, c, :], fw[0:96, 1, :], sin[:, half], ALU.mult).then_inc(signal["rope_used"], 1)
                    dve.wait_ge(signal["rope_used"], at(dve, i, 2 * C, 2 * c + 2))
                    dve.tensor_tensor(qk[:, half], rope_a[:, c, :], rope_b[:, c, :], ALU.add).then_inc(signal["qk_ready"], 1)
                yield "qkl"
                for c in range(C):
                    half = slice(HALF * c, HALF * c + HALF)
                    dve.wait_ge(signal["qkh_ready"], at(dve, i, C, c + 1))
                    dve.tensor_tensor(qkl[:, half], qk[:, half], qkh[:, half].bitcast(F32), ALU.subtract) \
                        .then_inc(signal["qkl_ready"], 1)
                for u, (j, c, w, heads) in enumerate(MAX_TILES):
                    yield "reduce.%d" % u
                    dve.wait_ge(signal["sm"], at(dve, i, NMAX, u + 1))
                    n = len(heads)
                    dve.tensor_reduce(mx[:, heads[0]:heads[0] + n, j, c],
                                      max_ring[u % 3][:, 0:n * w].rearrange("p (h w) -> p h w", h=n),
                                      AX.X, ALU.max).then_inc(signal["max_used"], 1)
                yield "negm"
                dve.wait_ge(signal["max_used"], at(dve, i, NMAX, NMAX))
                dve.tensor_reduce(mxt[:], mx[:], AX.X, ALU.max).then_inc(signal["max_ready"], 1)
                yield "y"
                dve.wait_ge(signal["otT"], at(dve, i, C, C))
                for c in range(C):
                    o4 = fo[:, c, :].rearrange("p (t h d) -> p t h d", t=TH, h=NH)
                    link(dve.reciprocal(rs4[:, TH * c:TH * c + TH, :], o4[:, :, :, HD]), i)
                    dve.tensor_tensor(y[:, TH * c:TH * c + TH, :].rearrange("p t (h d) -> p t h d", h=NH),
                                      o4[:, :, :, 0:HD],
                                      rs4[:, TH * c:TH * c + TH, :].unsqueeze(3).to_broadcast([P, TH, NH, HD]),
                                      ALU.mult).then_inc(signal["y_ready"], 1)
                yield "x3"
                dve.wait_ge(signal["wo_ps"], at(dve, i, 1, 1))
                link(dve.tensor_tensor(x3[:], fw[:, 0, :].rearrange("p (t d) -> p t d", t=T), x2[:], ALU.add), i)
                if not first(i):
                    dve.wait_ge(signal["h2_ready"], at(dve, i, 1, 0))
                dve.tensor_tensor(res[:], x3[:], h1[:], ALU.add).then_inc(signal["x3_ready"], 1)
                squares(x3, signal["ssq3"])
                yield "x3d"
                if not first(i):
                    dve.wait_ge(signal["x3T"], at(dve, i, C, 0))
                rms(x3, signal["rrms3"], x3d, signal["x3_done"])
                assert count["f"] == DVE_FRONT, count

            def route(i):
                count["b"] = 0
                yield "x3L"
                low(i, signal["hh3"], bo, bhh, bll, signal["ll3"])
                yield "lmax"
                dve.wait_ge(signal["lg_ps"], at(dve, i, 1, 1))
                lg_ps = bw[:, 0, 0:T * NE].rearrange("p (t e) -> p t e", t=T)
                link(dve.tensor_reduce(lmax[:], lg_ps, AX.X, ALU.max), i, "b")
                dve.tensor_tensor(lg[:], lg_ps, lmax[:].unsqueeze(2).to_broadcast([P, T, NE]), ALU.subtract) \
                    .then_inc(signal["lmax_ready"], 1)
                wait_apart(dve, signal["lmax_ready"], at(dve, i, 1, 1))
                yield "top2"
                for t in range(T):
                    ins = dve.max(top8[:, t, :], lg[:, t, :])
                link(ins, i, "b", apart=True)
                for t in range(T):
                    ins = dve.max_index(topi[:, t, :], top8[:, t, :], lg[:, t, :])
                link(ins, i, "b")
                link(dve.tensor_copy(topf[:], topi[:, :, 0:2]), i, "b")
                experts = iota[:, 0:NE].unsqueeze(1).to_broadcast([P, T, NE])
                dve.tensor_tensor(oh_a[:], experts, topf[:, :, 0:1].to_broadcast([P, T, NE]), ALU.is_equal)
                link(dve.tensor_tensor(oh_b[:], experts, topf[:, :, 1:2].to_broadcast([P, T, NE]), ALU.is_equal), i, "b")
                link(dve.tensor_tensor(oh_a[:], oh_a[:], oh_b[:], ALU.add), i, "b")
                yield "weights"
                dve.wait_ge(signal["ex_ready"], at(dve, i, 1, 1))
                link(dve.tensor_reduce(esum[:], ex[:], AX.X, ALU.add), i, "b")
                link(dve.reciprocal(esum[:], esum[:]), i, "b")
                link(dve.tensor_tensor(ex[:], ex[:], esum[:].unsqueeze(2).to_broadcast([P, T, NE]), ALU.mult), i, "b")
                link(dve.tensor_tensor(ex[:], ex[:], oh_a[:], ALU.mult), i, "b")
                link(dve.tensor_reduce(esum[:], ex[:], AX.X, ALU.add), i, "b")
                link(dve.tensor_scalar(esum[:], esum[:], 1e-9, None, ALU.add), i, "b")
                link(dve.reciprocal(esum[:], esum[:]), i, "b")
                dve.tensor_tensor(ex[:], ex[:], esum[:].unsqueeze(2).to_broadcast([P, T, NE]), ALU.mult) \
                    .then_inc(signal["rw_ready"], 1)
                yield "rwL"
                for c in range(C):
                    half = slice(HALF * c, HALF * c + HALF)
                    dve.wait_ge(signal["wth_ready"], at(dve, i, C, c + 1))
                    dve.tensor_tensor(wt[32:32 + NE, half], bo[0:NE, c, :], wt[0:NE, half].bitcast(F32), ALU.subtract) \
                        .then_inc(signal["wt_ready"], 1)
                assert count["b"] == DVE_ROUTE, count

            def experts(i):
                count["b"] = DVE_ROUTE
                for u in range(MT * C):
                    yield "moe.%d" % u
                    n = min(P, EH - u // C * P)
                    dve.wait_ge(signal["silu"], at(dve, i, MT * C, u + 1))
                    if u >= 2:
                        dve.wait_ge(signal["hid_ready"], at(dve, i, MT * C, u - 1))
                    dve.wait_ge(signal["moe_b"], at(dve, i, MT * C, u + 1))
                    dve.tensor_tensor(ub[0:n, u % 2, :], sa[0:n, u % 2, :], bw[0:n, 1, :], ALU.mult) \
                        .then_inc(signal["ub_ready"], 1)
                yield "h2"
                dve.wait_ge(signal["mtT"], at(dve, i, 1, 1))

                dve.tensor_tensor(by_half(h2[:]), bw[:, 0, :].rearrange("p (t c d) -> p t c d", t=TH, c=C),
                                  by_half(res[:]), ALU.add).then_inc(signal["h2_ready"], 1)
                dve.wait_ge(signal["h2_ready"], at(dve, i, 1, 1))

                moments(i, h2, bstats, bmv, bveps, "b").then_inc(signal["var4"], 1)
                yield "x4"
                norm_back(i, h2, signal["rstd4"], signal["x4_ready"])
                yield "x4L"
                low(i, signal["hh4"], bo, bhh, bll, signal["ll4"])
                yield "q2L"
                for c in range(C):
                    half = slice(HALF * c, HALF * c + HALF)
                    dve.wait_ge(signal["qh_ready"], at(dve, i, C, c + 1))
                    dve.scalar_tensor_tensor(out=ql[0:D, half], in0=bw[0:D, c, :], scalar=bq[0:D, 0:1],
                                             in1=qh[0:D, half].bitcast(F32), op0=ALU.add, op1=ALU.subtract) \
                        .then_inc(signal["ql_ready"], 1)
                yield "k2L"
                for c in range(C):
                    half = slice(HALF * c, HALF * c + HALF)
                    dve.wait_ge(signal["ka_ready"], at(dve, i, C, c + 1))
                    dve.wait_ge(signal["k2_ready"], at(dve, i, C, c + 1))
                    dve.scalar_tensor_tensor(out=ka[D:P, half], in0=bw[D:P, c, :], scalar=bk[D:P, 0:1],
                                             in1=ka[D:P, half].bitcast(F32), op0=ALU.add, op1=ALU.subtract) \
                        .then_inc(signal["kal_ready"], 1)
                dve.wait_ge(signal["v2_ps"], at(dve, i, 1, 1))
                dve.tensor_tensor(v2[:], bo[:, 0, :].rearrange("p (t d) -> p t d", t=T),
                                  bv[:].unsqueeze(1).to_broadcast([P, T, D]), ALU.add).then_inc(signal["v2_ready"], 1)
                for u in range(NSELF):
                    yield "reduce3.%d" % u
                    dve.wait_ge(signal["sm3"], at(dve, i, NSELF, u + 1))
                    dve.tensor_reduce(mx3[:, u % C, u // C:u // C + 1], max3_ring[u % 3], AX.X, ALU.max) \
                        .then_inc(signal["max3_used"], 1)
                yield "negm3"
                dve.wait_ge(signal["max3_used"], at(dve, i, NSELF, NSELF))
                dve.tensor_tensor(m3[:], mx3[:, 0, :], mx3[:, 1, :], ALU.max).then_inc(signal["m3_ready"], 1)
                for j in range(1, T):
                    yield "attn3.%d" % (j + 1)
                    if j > 1:
                        dve.wait_ge(signal["sum3_dve"], at(dve, i, T - 1, j - 1))
                    dve.wait_ge(signal["e3"], at(dve, i, NSELF, C * j + C))
                    before = bprob[:, 1, :] if j == 1 else sums[:, 1, :]
                    dve.tensor_tensor(sums[:, 1, :], before, bprob[:, (C * j + 1) % NHID, :], ALU.add) \
                        .then_inc(signal["sum3_dve"], 1)
                yield "h3"
                dve.wait_ge(signal["c3T"], at(dve, i, 1, 1))
                link(dve.reciprocal(brsum[:], bw[:, 1, 0:T].rearrange("p (t c) -> p t c", c=C)), i, "b")
                link(dve.tensor_tensor(by_half(batt[:]), bw[:, 0, :].rearrange("p (t c d) -> p t c d", t=TH, c=C),
                                       brsum[:].unsqueeze(3).to_broadcast([P, TH, C, D]), ALU.mult), i, "b")
                dve.tensor_tensor(h3[:], batt[:], h2[:], ALU.add).then_inc(signal["h3_ready"], 1)
                dve.wait_ge(signal["h3_ready"], at(dve, i, 1, 1))
                moments(i, h3, bstats, bmv, bveps, "b").then_inc(signal["var5"], 1)
                yield "x5"
                norm_back(i, h3, signal["rstd5"], signal["x5_ready"])
                yield "x5L"
                low(i, signal["hh5"], bo, bhh, bll, signal["ll5"])
                yield "top1"
                dve.wait_ge(signal["lg5_ps"], at(dve, i, 1, 1))
                link(dve.tensor_tensor(lg5[:], bw[:, 0, 0:T * E1].rearrange("p (t e) -> p t e", t=T),
                                       rb[:].unsqueeze(1).to_broadcast([P, T, E1]), ALU.add), i, "b", apart=True)
                for t in range(T):
                    ins = dve.max(top8b[:, t, :], lg5[:, t, :])
                link(ins, i, "b", apart=True)
                for t in range(T):
                    ins = dve.max_index(topib[:, t, :], top8b[:, t, :], lg5[:, t, :])
                link(ins, i, "b")
                link(dve.tensor_copy(topfb[:], topib[:, :, 0]), i, "b")
                dve.tensor_tensor(others[:], iota[:].unsqueeze(1).to_broadcast([P, T, E1]),
                                  topfb[:].unsqueeze(2).to_broadcast([P, T, E1]), ALU.not_equal) \
                    .then_inc(signal["others_ready"], 1)
                yield "chosen"
                for c in range(C):
                    dve.wait_ge(signal["otherst_ready"], at(dve, i, C, c + 1))
                    dve.tensor_scalar(chosent[:, HALF * c:HALF * c + HALF], bo[0:E1, c, :], -1.0, 1.0,
                                      ALU.mult, ALU.add).then_inc(signal["chosent_ready"], 1)
                assert count["b"] == DVE_BACK, count

            def finish(i):
                yield "h4"
                dve.wait_ge(signal["h4_free"], at(dve, i, 16, 16))
                dve.wait_ge(signal["mt5T"], at(dve, i, 1, 1))
                dve.tensor_tensor(by_half(h4[:]), bw[:, 0, :].rearrange("p (t c d) -> p t c d", t=TH, c=C),
                                  by_half(h3[:]), ALU.add).then_inc(signal["h4_ready"], 1)

            pipeline(dve, embed, attend, route, experts, finish)

        @block.tensor
        def _(pe):
            WAIT_REGISTER[pe.engine] = pe.alloc_register("wait_value")
            pe.wait_ge(signal["ident_loaded"], 16)

            def transposes(i, ready, src, psum, done):
                for t in range(T):
                    if t % TH == 0:
                        pe.wait_ge(ready, at(pe, i, C, t // TH + 1))
                    ins = pe.transpose(psum[:, t // TH, P * (t % TH):P * (t % TH) + P],
                                       src[:, t, :, :].rearrange("p r d -> p (r d)"), ident[:])
                    if t % TH == TH - 1:
                        ins.then_inc(done, 1)

            def project(dst, w, h, l, c):
                half = slice(HALF * c, HALF * c + HALF)
                pe.matmul(dst, w, h[:, half], start=True, stop=False)
                return pe.matmul(dst, w, l[:, half], start=False, stop=True)

            def project_rows(dst, w, h, l, t):
                pe.matmul(dst, h[:, P * t:P * t + P], w, start=True, stop=False)
                return pe.matmul(dst, l[:, P * t:P * t + P], w, start=False, stop=True)

            def weigh(psum, pr, values, ring, j):
                for c in range(C):
                    ins = pe.matmul(psum[D * c:D * c + D, :], values, pr[:, (C * j + c) % ring, :],
                                    start=(j == 0), stop=(j == T - 1), skip_group_check=True,
                                    tile_position=(0, D * c))
                return ins

            def back_rows(src, psum):
                for t in range(TH):
                    ins = pe.transpose(psum[:, P * t:P * t + P], src[:, P * t:P * t + P], ident[:])
                return ins

            def embed(i):
                yield "x1T"
                transposes(i, signal["x1_ready"], xd, fo, signal["x1T"])

                def scores1(u):
                    j, c = u // C, u % C
                    if u < C:
                        pe.wait_ge(signal["ll1"], at(pe, i, C, c + 1))
                        pe.wait_ge(signal["aal1"], at(pe, i, C, c + 1))
                    if u >= 3:
                        pe.wait_ge(signal["e1"], at(pe, i, NSELF, u - 2))
                    project(attn1_ring[u % 3], aa[:, P * j:P * j + P], hh, ll, c).then_inc(signal["s1"], 1)

                for j in range(T + 1):
                    yield "attn1.%d" % j
                    if j < T:
                        for c in range(C):
                            scores1(C * j + c)
                    if j >= 1:
                        pe.wait_ge(signal["e1"], at(pe, i, NSELF, C * j))
                        weigh(fo[:, 1, :], prob, xd[:, j - 1, 0, :], NRING, j - 1).then_inc(signal["pv1"], 1)

            def attend(i):
                yield "c1"
                pe.wait_ge(signal["c1_ready"], at(pe, i, 1, 1))
                back_rows(ot, fo[:, 0, :]).then_inc(signal["c1T"], 1)
                if first(i):
                    pe.wait_ge(signal["w_ready"], 1)
                    pe.wait_ge(signal["const_loaded"], 16 * 17)
                    pe.wait_ge(signal["const_cast"], 2)
                    pe.wait_ge(signal["w2_loaded"], 32)
                    pe.wait_ge(signal["filled"], FILLS)
                yield "x2T"
                transposes(i, signal["x2_ready"], xd, fo, signal["x2T"])
                for c in range(C):
                    yield "qk.%d" % c
                    pe.wait_ge(signal["ll2"], at(pe, i, C, c + 1))
                    if c:
                        pe.wait_ge(signal["rope_used"], at(pe, i, 2 * C, 2 * c))
                    project(fw[0:96, 0, :], weight("qk"), hh, ll, c)
                    project(fw[0:96, 1, :], weight("qk_swapped"), hh, ll, c).then_inc(signal["qk_ps"], 1)
                yield "v"
                for t in range(T):
                    ins = project_rows(fo[:, 0, 32 * t:32 * t + 32], weight("v"), hh, ll, t)
                ins.then_inc(signal["v_ps"], 1)
                yield "max.0"
                pe.wait_ge(signal["spread_done"], at(pe, i, 16 * 15, 16 * 15))
                for u, (j, c, w, heads) in enumerate(MAX_TILES):
                    yield "max.%d" % u
                    if u < 3:
                        pe.wait_ge(signal["rope_used"], at(pe, i, 2 * C, 2 * C))
                    else:
                        pe.wait_ge(signal["max_used"], at(pe, i, NMAX, u - 2))
                    diagonal = HALF * c + w == P * (j + 1)
                    for n, h in enumerate(heads):
                        dst = max_ring[u % 3][:, n * w:n * w + w]
                        if diagonal:
                            pe.matmul(dst[:, w - P:w], ident16[:], mask_qk[:], start=True, stop=False,
                                      skip_group_check=True)
                        ins = pe.matmul(dst, qs[0:96, h, P * j:P * j + P], ks[0:96, HALF * c:HALF * c + w],
                                        start=not diagonal, stop=True, skip_group_check=True)
                    ins.then_inc(signal["sm"], 1)
                yield "negm"
                pe.wait_ge(signal["max_ready"], at(pe, i, 1, 1))
                pe.wait_ge(signal["hh2"], at(pe, i, C, C))
                pe.transpose(fo[0:NH * T, 1, 0:P], mxt[:].rearrange("p h t -> p (h t)"), ident[:]).then_inc(signal["maxT"], 1)
                yield "prob.0"
                pe.wait_ge(signal["negm_placed"], at(pe, i, 16, 16))
                pe.wait_ge(signal["v_ready"], at(pe, i, 1, 1))

                def scores2(u):
                    j, c, w, heads = PROB_TILES[u]
                    if u == SECOND + 2:
                        pe.wait_ge(signal["ot_ready"], at(pe, i, C, 1))
                    elif u >= 2:
                        gap = 2 if SECOND <= u < SECOND + 2 else 3
                        if u >= gap:
                            pe.wait_ge(signal["e2"], at(pe, i, NPROB, u - gap + 1))
                    q0 = HALF * (c + 1) - w
                    diagonal = q0 == P * j
                    for n, h in enumerate(heads):
                        dst = prob_bank(u)[:, n * w:n * w + w]
                        if diagonal:
                            pe.matmul(dst[:, 0:P], ident16[:], mask_kq[:], start=True, stop=False,
                                      skip_group_check=True)
                        ins = pe.matmul(dst, ks[0:97, P * j:P * j + P], qs[0:97, h, q0:q0 + w],
                                        start=not diagonal, stop=True, skip_group_check=True)
                    ins.then_inc(signal["s2"], 1)

                def weigh2(u):
                    j, c, w, heads = PROB_TILES[u]
                    pe.wait_ge(signal["e2"], at(pe, i, NPROB, u + 1))
                    for n, h in enumerate(heads):
                        ins = pe.matmul(fo[32 * h:32 * h + 32, c, HALF - w:HALF], v1[:, j, h // 2, :],
                                        prob[:, u % NRING, n * w:n * w + w], start=(j == 0),
                                        stop=(j == TH * (c + 1) - 1), skip_group_check=True,
                                        tile_position=(0, 32 * h))
                    ins.then_inc(signal["pv2"], 1)

                ends = [u for u in range(NPROB) if u == NPROB - 1 or PROB_TILES[u][:2] != PROB_TILES[u + 1][:2]]
                waiting = []
                for u in range(NPROB):
                    yield "prob.%d" % u
                    if u == SECOND:
                        for v in waiting:
                            weigh2(v)
                        waiting = []
                    scores2(u)
                    if u in ends:
                        for v in waiting:
                            weigh2(v)
                        waiting = [v for v in range(NPROB) if PROB_TILES[v][:2] == PROB_TILES[u][:2]]
                yield "last_heads"
                for v in waiting:
                    weigh2(v)
                yield "heads"
                pe.wait_ge(signal["ot_ready"], at(pe, i, C, C))
                for t in range(T):
                    ins = pe.transpose(fo[:, t // TH, P * (t % TH):P * (t % TH) + P], ot[:, P * t:P * t + P], ident[:])
                    if t % TH == TH - 1:
                        ins.then_inc(signal["otT"], 1)
                yield "yT"
                for t in range(T):
                    if t % TH == 0:
                        wait_apart(pe, signal["y_ready"], at(pe, i, C, t // TH + 1))
                    ins = pe.transpose(fo[0:D, t // TH, P * (t % TH):P * (t % TH) + P], y[:, t, :], ident[:])
                    if t % TH == TH - 1:
                        ins.then_inc(signal["yT"], 1)
                yield "wo"
                for t in range(T):
                    if t % TH == 0:
                        pe.wait_ge(signal["yt_ready"], at(pe, i, C, t // TH + 1))
                    ins = pe.matmul(fw[:, 0, D * t:D * t + D], yt[:, P * t:P * t + P], wo[:], start=True, stop=True)
                ins.then_inc(signal["wo_ps"], 1)

            def route(i):
                yield "x3T"
                transposes(i, signal["x3_done"], x3d, bo, signal["x3T"])
                yield "router"
                for t in range(T):
                    if t % TH == 0:
                        pe.wait_ge(signal["ll3"], at(pe, i, C, t // TH + 1))
                    ins = project_rows(bw[:, 0, NE * t:NE * t + NE], weight("router"), bhh, bll, t)
                ins.then_inc(signal["lg_ps"], 1)
                yield "rwT"
                pe.wait_ge(signal["rw_ready"], at(pe, i, 1, 1))
                for t in range(T):
                    ins = pe.transpose(bo[0:NE, t // TH, P * (t % TH):P * (t % TH) + P], ex[:, t, :], ident[:])
                    if t % TH == TH - 1:
                        ins.then_inc(signal["rwT"], 1)

            def experts(i):
                yield "moe.0"
                pe.wait_ge(signal["wt_ready"], at(pe, i, C, C))

                def experts_out(m):
                    pe.wait_ge(signal["hid_ready"], at(pe, i, MT * C, C * m + C))
                    n = min(P, EH - m * P)
                    for c in range(C):
                        ins = pe.matmul(bo[D * c:D * c + D, 1, :], w2[0:n, m, :], hid[0:n, (C * m + c) % NHID, :],
                                        start=(m == 0), stop=(m == MT - 1), skip_group_check=True,
                                        tile_position=(0, D * c))
                    ins.then_inc(signal["w2_step"], 1)
                    return ins

                def gates(u):
                    m, n = u // C, min(P, EH - u // C * P)
                    if u >= 1:
                        pe.wait_ge(signal["silu"], at(pe, i, MT * C, u))
                    project(bw[0:n, 0, :], weight("w1", P * m, n), bhh, bll, u % C).then_inc(signal["moe_a"], 1)

                def linears(u):
                    m, n = u // C, min(P, EH - u // C * P)
                    if u >= 1:
                        pe.wait_ge(signal["ub_ready"], at(pe, i, MT * C, u))
                    project(bw[0:n, 1, :], weight("w3", P * m, n), bhh, bll, u % C).then_inc(signal["moe_b"], 1)

                gates(0)
                linears(0)
                for u in range(MT * C):
                    m, c = u // C, u % C
                    n = min(P, EH - m * P)
                    yield "moe.%d" % u
                    if u + 1 < MT * C:
                        gates(u + 1)
                    if u >= 1:
                        pe.wait_ge(signal["spread_copied"], at(pe, i, MT * C, u))
                    pe.matmul(bo[0:n, 0, :], spread[:, P * m:P * m + n], wt[:, HALF * c:HALF * c + HALF],
                              start=True, stop=True).then_inc(signal["moe_w"], 1)
                    if c == 0 and m >= 2:
                        experts_out(m - 2)
                    if u + 1 < MT * C:
                        linears(u + 1)
                yield "moe.%d" % (MT * C)
                for m in (MT - 2, MT - 1):
                    experts_out(m)
                yield "moe_out"
                pe.wait_ge(signal["mt_ready"], at(pe, i, 1, 1))
                back_rows(mt, bw[:, 0, :]).then_inc(signal["mtT"], 1)
                yield "x4T"
                transposes(i, signal["x4_ready"], bxd, bo, signal["x4T"])
                yield "q2"
                pe.wait_ge(signal["h2_ready"], at(pe, i, 1, 1))
                for c in range(C):
                    pe.wait_ge(signal["ll4"], at(pe, i, C, c + 1))
                    project(bw[:, c, :], weight("q2"), bhh, bll, c).then_inc(signal["q_ps"], 1)
                yield "v2"
                for t in range(T):
                    ins = project_rows(bo[:, 0, D * t:D * t + D], weight("v2"), bhh, bll, t)
                ins.then_inc(signal["v2_ps"], 1)
                yield "k2"
                for c in range(C):
                    pe.wait_ge(signal["ql_ready"], at(pe, i, C, c + 1))
                    project(bw[:, c, :], weight("k2"), bhh, bll, c).then_inc(signal["k_ps"], 1)
                for u in range(NSELF):
                    j, c = u // C, u % C
                    yield "max3.%d" % u
                    if u < 3:
                        pe.wait_ge(signal["kal_ready"], at(pe, i, C, c + 1))
                        pe.wait_ge(signal["k2_ready"], at(pe, i, C, c + 1))
                    else:
                        pe.wait_ge(signal["max3_used"], at(pe, i, NSELF, u - 2))
                    pe.matmul(max3_ring[u % 3], qh[:, P * j:P * j + P], ka[:, HALF * c:HALF * c + HALF],
                              start=True, stop=True).then_inc(signal["sm3"], 1)
                yield "negm3"
                pe.wait_ge(signal["m3_ready"], at(pe, i, 1, 1))
                pe.transpose(bo[0:T, 1, 0:P], m3[:], ident[:]).then_inc(signal["m3T"], 1)
                yield "attn3.0"
                pe.wait_ge(signal["negm3_placed"], at(pe, i, 16, 16))
                pe.wait_ge(signal["v2_ready"], at(pe, i, 1, 1))

                def scores3(u):
                    j, c = u // C, u % C
                    half = slice(HALF * c, HALF * c + HALF)
                    if u >= 3:
                        pe.wait_ge(signal["e3"], at(pe, i, NSELF, u - 2))
                    pe.matmul(attn3_ring[u % 3], ka[:, P * j:P * j + P], qh[:, half], start=True, stop=False)
                    pe.matmul(attn3_ring[u % 3], k2[:, P * j:P * j + P], ql[:, half], start=False, stop=True) \
                        .then_inc(signal["s3"], 1)

                for j in range(T + 1):
                    yield "attn3.%d" % j
                    if j < T:
                        for c in range(C):
                            scores3(C * j + c)
                    if j >= 1:
                        pe.wait_ge(signal["e3"], at(pe, i, NSELF, C * j))
                        weigh(bo[:, 0, :], bprob, v2[:, j - 1, :], NHID, j - 1).then_inc(signal["pv3"], 1)
                yield "c3"
                pe.wait_ge(signal["c3_ready"], at(pe, i, 1, 1))
                back_rows(mt, bw[:, 0, :])
                pe.wait_ge(signal["sum3_pool"], at(pe, i, T - 1, T - 1))
                pe.wait_ge(signal["sum3_dve"], at(pe, i, T - 1, T - 1))
                for c in range(C):
                    for t in range(TH):
                        n = C * t + c
                        ins = pe.matmul(bw[:, 1, n:n + 1], sums[:, c, P * t:P * t + P], ones[:], start=True, stop=True)
                ins.then_inc(signal["c3T"], 1)
                yield "x5T"
                transposes(i, signal["x5_ready"], bxd, bo, signal["x5T"])
                yield "lg5"
                for t in range(T):
                    if t % TH == 0:
                        pe.wait_ge(signal["ll5"], at(pe, i, C, t // TH + 1))
                    ins = project_rows(bw[:, 0, E1 * t:E1 * t + E1], weight("router2"), bhh, bll, t)
                ins.then_inc(signal["lg5_ps"], 1)
                yield "othersT"
                pe.wait_ge(signal["others_ready"], at(pe, i, 1, 1))
                for t in range(T):
                    ins = pe.transpose(bo[0:E1, t // TH, P * (t % TH):P * (t % TH) + P], others[:, t, :], ident[:])
                    if t % TH == TH - 1:
                        ins.then_inc(signal["othersT"], 1)

            def finish(i):
                def experts2_out(m):
                    pe.wait_ge(signal["hid5_ready"], at(pe, i, M1 * C, C * m + C))
                    for c in range(C):
                        ins = pe.matmul(bo[D * c:D * c + D, 1, :], w2_2[:, m, :], hid[:, (C * m + c) % NHID, :],
                                        start=False, stop=(m == M1 - 1), skip_group_check=True,
                                        tile_position=(0, D * c))
                    ins.then_inc(signal["w5_step"], 1)

                yield "ffn5.0"
                pe.wait_ge(signal["chosent_ready"], at(pe, i, C, C))
                pe.wait_ge(signal["otherst_ready"], at(pe, i, C, C))
                for c in range(C):
                    pe.matmul(bo[D * c:D * c + D, 1, :], b2_2[:], chosent[:, HALF * c:HALF * c + HALF],
                              start=True, stop=False, skip_group_check=True, tile_position=(0, D * c))
                for u in range(M1 * C):
                    m, c = u // C, u % C
                    yield "ffn5.%d" % m
                    if u >= 3:
                        pe.wait_ge(signal["hid5_ready"], at(pe, i, M1 * C, u - 2))
                    half = slice(HALF * c, HALF * c + HALF)
                    w = weight("w1_2", P * m, P)
                    pe.matmul(ffn5_ring[u % 3], w, bhh[:, half], start=True, stop=False)
                    pe.matmul(ffn5_ring[u % 3], w, bll[:, half], start=False, stop=False)
                    pe.matmul(ffn5_ring[u % 3], block16[:, P * m:P * m + P], otherst[:, half],
                              start=False, stop=True).then_inc(signal["s5"], 1)
                    if c == 1 and m >= 1:
                        experts2_out(m - 1)
                yield "ffn5.%d" % M1
                experts2_out(M1 - 1)
                yield "out"
                pe.wait_ge(signal["mt5_ready"], at(pe, i, 1, 1))
                back_rows(mt2, bw[:, 0, :]).then_inc(signal["mt5T"], 1)

            pipeline(pe, embed, attend, route, experts, finish)


def constants():
    p = np.arange(P)
    inv = 1.0 / 10000.0 ** (np.arange(0, HD, 2, dtype=np.float32) / HD)
    angles = np.outer(np.arange(L, dtype=np.float32), inv)
    emb = np.concatenate([angles, angles], axis=-1)
    sign = np.where(np.arange(HD) < HD // 2, -1.0, 1.0).astype(np.float32)
    spread = np.zeros((40, MT * P), np.float32)
    for e in range(NE):
        spread[[e, 32 + e], e * HID:(e + 1) * HID] = 1.0
    block16 = np.zeros((E1, E1 * H1), np.float32)
    for e in range(E1):
        block16[e, e * H1:(e + 1) * H1] = NEG
    bf16 = mybir.dt.np(BF16)
    return {
        "ident": np.eye(P, dtype=np.float32),
        "ident16": np.eye(P, dtype=np.float32).astype(bf16),
        "mask_qk": np.where(p[None, :] > p[:, None], NEG, 0.0).astype(bf16),
        "mask_kq": np.where(p[None, :] < p[:, None], NEG, 0.0).astype(bf16),
        "cos": np.ascontiguousarray(np.tile(np.cos(emb).T, (6, 1))),
        "sin": np.ascontiguousarray(np.tile((np.sin(emb) * sign).T, (6, 1))),
        "iota": np.tile(np.arange(E1, dtype=np.float32), (P, 1)),
        "spread": spread,
        "block16": block16.astype(bf16),
    }


def layout(v):
    wq, wk = v["L0_ffn_wq"], v["L0_ffn_wk"]

    def swapped(w):
        n = w.shape[0] // HD
        return w.reshape(n, 2, HD // 2, D)[:, ::-1].reshape(n * HD, D)

    wide = [wq, wk, swapped(wq), swapped(wk), v["L0_ffn_wv"], v["L0_ffn_router_w"],
            v["L0_ffn_w1"].reshape(EH, D), v["L0_ffn_w3"].reshape(EH, D),
            v["L1_attn_Wq"].T, v["L1_attn_Wq"].T, v["L1_attn_Wk"].T, v["L1_attn_Wk"].T, v["L1_attn_Wv"].T,
            v["L1_ffn_router_w"], v["L1_ffn_W1"].transpose(0, 2, 1).reshape(E1 * H1, D)]
    lnw = np.stack([v["L0_ffn_ln1_w"], v["L0_ffn_ln2_w"]], axis=1)
    return {
        "x": v["x"].reshape(B, T, P).transpose(0, 2, 1),
        "table": v["L0_tok_W"].T,
        "wcat": np.concatenate(wide, axis=0).T,
        "lnw": np.concatenate([lnw, lnw], axis=0),
        "wo": v["L0_ffn_wo"].T,
        "w2": v["L0_ffn_w2"].transpose(0, 2, 1).reshape(EH, D),
        "w2_2": v["L1_ffn_W2"].reshape(M1, P, D).transpose(1, 0, 2),
        "b1_2": v["L1_ffn_b1"].reshape(M1, P).T,
        "b2_2": v["L1_ffn_b2"],
        "bq": np.concatenate([v["L1_attn_bq"]] * 2).reshape(P, 1),
        "bk": np.concatenate([v["L1_attn_bk"]] * 2).reshape(P, 1),
        "bv": v["L1_attn_bv"],
        "rb": v["L1_ffn_router_b"],
    }


def kernel(**inputs):
    import concourse.bacc as bacc
    from concourse.bass_utils import run_bass_kernel_spmd

    nc = bacc.Bacc("TRN2", target_bir_lowering=False, num_devices=1)
    given = {k: np.asarray(x) for k, x in inputs.items()}
    arrays = {k: np.ascontiguousarray(x) for k, x in {**layout(given), **constants()}.items()}
    aps = {k: nc.dram_tensor(f"in_{k}", x.shape, mybir.dt.from_np(x.dtype), kind="ExternalInput").ap()
           for k, x in arrays.items()}
    out = nc.dram_tensor("out", (B, L, D), F32, kind="ExternalOutput").ap()
    tower(nc, aps, out)
    r = run_bass_kernel_spmd(nc, [{f"in_{k}": x for k, x in arrays.items()}], core_ids=[0])
    return r.results[0]["out"]
```
